# Optimizing a Trainium2 kernel written in Bass

```python
import numpy as np
import jax
import jax.numpy as jnp

def _softmax(x, axis=-1):
    return jax.nn.softmax(x, axis=axis)
def _gelu(x):
    return jax.nn.gelu(x, approximate=True)
def _silu(x):
    return jax.nn.silu(x)
def _sigmoid(x):
    return jax.nn.sigmoid(x)
def _layernorm(x, axis=-1, eps=1e-5):
    m = jnp.mean(x, axis=axis, keepdims=True)
    v = jnp.var(x, axis=axis, keepdims=True)
    return (x - m) / jnp.sqrt(v + eps)
def _scatter_add(tgt, idx, src, axis=0):
    return tgt.at[idx].add(src)
def _segment_sum(src, seg, n):
    return jax.ops.segment_sum(src, seg, n)

kernel_name = 'mk_conv_attn_hybrid_d4_conv_nchw128_5f8e13'

def setup_inputs(seed: int = 0):
    np.random.seed(seed)
    _w = jnp.asarray
    def _rec_inputs():
        import jax
        import jax.numpy as jnp
        _gk = jax.random.key(seed)
        x = -0.0005207 + 1.001 * jax.random.normal(jax.random.fold_in(_gk, 1), (4, 128, 64, 64), jnp.float32)
        return x
    x = _rec_inputs()
    def _L0_conv_setup():
        import jax, jax.numpy as jnp
        import numpy as np
        D_CONV = 4
        D_STATE = 16
        GROUP = 8

        def _ln(x, g, b):
            mu = x.mean(-1, keepdims=True)
            v = ((x - mu) ** 2).mean(-1, keepdims=True)
            return (x - mu) * jax.lax.rsqrt(v + 1e-05) * g + b

        def _mamba(x, W_in, conv_w, conv_b, W_x, W_dt, b_dt, A_log, D_skip, W_out):
            B, L, Dm = x.shape
            d_inner = W_in.shape[0] // 2
            dt_rank = W_dt.shape[1]
            xz = x @ W_in.T
            xi, z = (xz[..., :d_inner], xz[..., d_inner:])
            xc = jax.lax.conv_general_dilated(xi.transpose(0, 2, 1), conv_w, (1,), [(D_CONV - 1, 0)], feature_group_count=d_inner, dimension_numbers=('NCH', 'OIH', 'NCH'))
            u = jax.nn.silu((xc + conv_b[:, None]).transpose(0, 2, 1))
            x_dbl = u @ W_x.T
            dt = jax.nn.softplus(x_dbl[..., :dt_rank] @ W_dt.T + b_dt)
            Bs = x_dbl[..., dt_rank:dt_rank + D_STATE]
            Cs = x_dbl[..., dt_rank + D_STATE:]
            A = -jnp.exp(A_log)

            def step(h, inp):
                dt_t, B_t, C_t, u_t = inp
                dA = jnp.exp(dt_t[..., None] * A)
                h = dA * h + (dt_t * u_t)[..., None] * B_t[:, None, :]
                return (h, jnp.einsum('bdn,bn->bd', h, C_t))
            h0 = jnp.zeros((B, d_inner, D_STATE), x.dtype)
            _, ys = jax.lax.scan(step, h0, (dt.transpose(1, 0, 2), Bs.transpose(1, 0, 2), Cs.transpose(1, 0, 2), u.transpose(1, 0, 2)))
            y = ys.transpose(1, 0, 2) + u * D_skip
            return y * jax.nn.silu(z) @ W_out.T
        key = jax.random.key(seed)
        ks = jax.random.split(key, 10)
        B, C, W, H = (4, 128, 64, 64)
        out_dim = 128
        d_inner = 2 * C
        dt_rank = (C + 15) // 16
        f = lambda k, s, sc=0.02: jax.random.normal(k, s, jnp.float32) * sc
        A_log = jnp.log(jnp.tile(jnp.arange(1, D_STATE + 1, dtype=jnp.float32), (d_inner, 1)))
        return dict(x=jax.random.normal(ks[0], (B, C, W, H), jnp.float32), gamma=jnp.ones((C,), jnp.float32), beta=jnp.zeros((C,), jnp.float32), W_in=f(ks[1], (2 * d_inner, C)), conv_w=f(ks[2], (d_inner, 1, D_CONV), 0.1), conv_b=jnp.zeros((d_inner,), jnp.float32), W_x=f(ks[3], (dt_rank + 2 * D_STATE, d_inner)), W_dt=f(ks[4], (d_inner, dt_rank), 0.1), b_dt=f(ks[5], (d_inner,), 0.5), A_log=A_log, D_skip=jnp.ones((d_inner,), jnp.float32), W_out=f(ks[6], (C, d_inner)), W_p=f(ks[7], (out_dim, C)), b_p=jnp.zeros((out_dim,), jnp.float32), s1=jnp.ones((1,), jnp.float32), s2=jnp.ones((1,), jnp.float32))
    _L0_conv_all = _L0_conv_setup()
    _L0_conv_in = {k: v for k, v in _L0_conv_all.items() if k in ('gamma', 'beta', 'W_in', 'conv_w', 'conv_b', 'W_x', 'W_dt', 'b_dt', 'A_log', 'D_skip', 'W_out', 'W_p', 'b_p', 's1', 's2', )}
    del _L0_conv_all

    def _L1_conv_setup():
        import jax, jax.numpy as jnp
        from jax import lax
        import numpy as np
        B, C, H, W = (8, 128, 112, 112)
        G, K, OC = (4, 3, 128)
        DN = ('NCHW', 'OIHW', 'NCHW')
        key = jax.random.key(seed)
        k1, k2, k3, k4, k5 = jax.random.split(key, 5)
        x = jax.random.normal(k1, (B, C, H, W), dtype=jnp.float32)
        w_kg = jax.random.normal(k2, (K * K * G, C // G, K, K), dtype=jnp.float32) * 0.05
        b_kg = jax.random.normal(k3, (K * K * G,), dtype=jnp.float32) * 0.05
        w_pw = jax.random.normal(k4, (OC, C // G, 1, 1), dtype=jnp.float32) * 0.05
        b_pw = jax.random.normal(k5, (OC,), dtype=jnp.float32) * 0.05
        return {'x': x, 'w_kg': w_kg, 'b_kg': b_kg, 'w_pw': w_pw, 'b_pw': b_pw}
    _L1_conv_all = _L1_conv_setup()
    _L1_conv_in = {k: v for k, v in _L1_conv_all.items() if k in ('w_kg', 'b_kg', 'w_pw', 'b_pw', )}
    del _L1_conv_all

    def _L2_attn_setup():
        import jax, jax.numpy as jnp
        import numpy as np
        HIDDEN_SIZE = 128
        MASK_LEN = 2048
        BATCH = 16
        key = jax.random.key(seed)
        q = jax.random.normal(key, (BATCH, MASK_LEN, HIDDEN_SIZE), dtype=jnp.float32)
        return {'q': q}
    _L2_attn_all = _L2_attn_setup()
    _L2_attn_in = {k: v for k, v in _L2_attn_all.items() if k in ()}
    del _L2_attn_all

    def _L2_ffn_setup():
        import jax, jax.numpy as jnp
        import numpy as np
        B, S, D, E, H, O, K = (512, 2048, 128, 64, 512, 128, 8)
        key = jax.random.key(seed)
        k0, k1, k2, k3 = jax.random.split(key, 4)
        x = jax.random.normal(k0, (B, S, D), dtype=jnp.float32)
        gate_w = jax.random.normal(k1, (E, D), dtype=jnp.float32) * (1.0 / np.sqrt(D))
        gate_b = jnp.zeros((E,), dtype=jnp.float32)
        weight1 = jax.random.uniform(k2, (E, D + 1, H), dtype=jnp.float32, minval=-1.0, maxval=1.0) * (1.0 / np.sqrt(D + 1))
        weight2 = jax.random.uniform(k3, (E, H + 1, O), dtype=jnp.float32, minval=-1.0, maxval=1.0) * (1.0 / np.sqrt(H + 1))
        return {'x': x, 'gate_w': gate_w, 'gate_b': gate_b, 'weight1': weight1, 'weight2': weight2}
    _L2_ffn_all = _L2_ffn_setup()
    _L2_ffn_in = {k: v for k, v in _L2_ffn_all.items() if k in ('gate_w', 'gate_b', 'weight1', 'weight2', )}
    del _L2_ffn_all

    def _L3_attn_setup():
        import jax, jax.numpy as jnp
        import numpy as np
        CHUNK = 64
        D_MODEL = 128
        D_STATE = 64
        HEADDIM = 64
        D_INNER = 2 * D_MODEL
        NHEADS = D_INNER // HEADDIM
        CONV_DIM = D_INNER + 2 * D_STATE
        K = 4
        D_IN_PROJ = 2 * D_INNER + 2 * D_STATE + NHEADS
        EPS = 1e-05

        def _segsum(t):
            L = t.shape[-1]
            cs = jnp.cumsum(t, -1)
            seg = cs[..., :, None] - cs[..., None, :]
            mask = jnp.tril(jnp.ones((L, L), bool))
            return jnp.where(mask, seg, -jnp.inf)

        def _ssd(xh, dt, A, Bm, Cm):
            b, l, h, p = xh.shape
            n = Bm.shape[-1]
            c = l // CHUNK
            xdt = xh * dt[..., None]
            dA = dt * A
            rc = lambda t: t.reshape(b, c, CHUNK, *t.shape[2:])
            xc, dAc, Bc, Cc = (rc(xdt), rc(dA), rc(Bm), rc(Cm))
            Acs = jnp.cumsum(dAc, axis=2)
            Lmat = jnp.exp(_segsum(dAc.transpose(0, 1, 3, 2)))
            Y_diag = jnp.einsum('bcln,bcsn,bchls,bcshp->bclhp', Cc, Bc, Lmat, xc)
            decay_st = jnp.exp(Acs[:, :, -1:, :] - Acs)
            states = jnp.einsum('bcln,bclh,bclhp->bchpn', Bc, decay_st, xc)
            chunk_decay = jnp.exp(Acs[:, :, -1])

            def step(carry, inp):
                st, dec = inp
                new = st + carry * dec[:, :, None, None]
                return (new, carry)
            init = jnp.zeros((b, h, p, n), xh.dtype)
            _, prev = jax.lax.scan(step, init, (states.transpose(1, 0, 2, 3, 4), chunk_decay.transpose(1, 0, 2)))
            prev = prev.transpose(1, 0, 2, 3, 4)
            Y_off = jnp.einsum('bcln,bchpn,bclh->bclhp', Cc, prev, jnp.exp(Acs))
            return (Y_diag + Y_off).reshape(b, l, h, p)

        def _mamba3(x, in_proj, conv_w, conv_b, A_log, dt_bias, D, norm_w, out_proj):
            b, l, _ = x.shape
            zxbcdt = x @ in_proj
            z, xbc, dt = jnp.split(zxbcdt, [D_INNER, D_INNER + CONV_DIM], axis=-1)
            xp = jnp.pad(xbc, ((0, 0), (K - 1, 0), (0, 0)))
            conv = sum((xp[:, i:i + l, :] * conv_w[:, i] for i in range(K))) + conv_b
            xbc = jax.nn.silu(conv)
            xh, Bm, Cm = jnp.split(xbc, [D_INNER, D_INNER + D_STATE], axis=-1)
            xh = xh.reshape(b, l, NHEADS, HEADDIM)
            dt = jax.nn.softplus(dt + dt_bias)
            A = -jnp.exp(A_log)
            y = _ssd(xh, dt, A, Bm, Cm) + xh * D[None, None, :, None]
            yg = y.reshape(b, l, D_INNER) * jax.nn.silu(z)
            yn = yg * jax.lax.rsqrt(jnp.mean(yg * yg, -1, keepdims=True) + EPS) * norm_w
            return yn @ out_proj
        key = jax.random.key(seed)
        ks = jax.random.split(key, 19)
        inp = {'x': jax.random.normal(ks[0], (16, 4096, D_MODEL), jnp.float32)}
        for i, pre in enumerate(['fwd', 'bwd']):
            o = 1 + 9 * i
            inp[pre + '_in_proj'] = jax.random.normal(ks[o], (D_MODEL, D_IN_PROJ), jnp.float32) * D_MODEL ** (-0.5)
            inp[pre + '_conv_w'] = jax.random.normal(ks[o + 1], (CONV_DIM, K), jnp.float32) * 0.3
            inp[pre + '_conv_b'] = jnp.zeros((CONV_DIM,), jnp.float32)
            inp[pre + '_A_log'] = jnp.log(jax.random.uniform(ks[o + 2], (NHEADS,), jnp.float32, 1.0, 16.0))
            inp[pre + '_dt_bias'] = jax.random.normal(ks[o + 3], (NHEADS,), jnp.float32) * 0.5
            inp[pre + '_D'] = jnp.ones((NHEADS,), jnp.float32)
            inp[pre + '_norm_w'] = jnp.ones((D_INNER,), jnp.float32)
            inp[pre + '_out_proj'] = jax.random.normal(ks[o + 4], (D_INNER, D_MODEL), jnp.float32) * D_INNER ** (-0.5)
        return inp
    _L3_attn_all = _L3_attn_setup()
    _L3_attn_in = {k: v for k, v in _L3_attn_all.items() if k in ('fwd_in_proj', 'fwd_conv_w', 'fwd_conv_b', 'fwd_A_log', 'fwd_dt_bias', 'fwd_D', 'fwd_norm_w', 'fwd_out_proj', 'bwd_in_proj', 'bwd_conv_w', 'bwd_conv_b', 'bwd_A_log', 'bwd_dt_bias', 'bwd_D', 'bwd_norm_w', 'bwd_out_proj', )}
    del _L3_attn_all

    def _L3_ffn_setup():
        import jax, jax.numpy as jnp
        import numpy as np
        B, S, D, E, H, O, K = (512, 2048, 128, 64, 512, 128, 8)
        key = jax.random.key(seed)
        k0, k1, k2, k3 = jax.random.split(key, 4)
        x = jax.random.normal(k0, (B, S, D), dtype=jnp.float32)
        gate_w = jax.random.normal(k1, (E, D), dtype=jnp.float32) * (1.0 / np.sqrt(D))
        gate_b = jnp.zeros((E,), dtype=jnp.float32)
        weight1 = jax.random.uniform(k2, (E, D + 1, H), dtype=jnp.float32, minval=-1.0, maxval=1.0) * (1.0 / np.sqrt(D + 1))
        weight2 = jax.random.uniform(k3, (E, H + 1, O), dtype=jnp.float32, minval=-1.0, maxval=1.0) * (1.0 / np.sqrt(H + 1))
        return {'x': x, 'gate_w': gate_w, 'gate_b': gate_b, 'weight1': weight1, 'weight2': weight2}
    _L3_ffn_all = _L3_ffn_setup()
    _L3_ffn_in = {k: v for k, v in _L3_ffn_all.items() if k in ('gate_w', 'gate_b', 'weight1', 'weight2', )}
    del _L3_ffn_all

    return {
        "x": x,
        "L0_conv_gamma": _L0_conv_in["gamma"],
        "L0_conv_beta": _L0_conv_in["beta"],
        "L0_conv_W_in": _L0_conv_in["W_in"],
        "L0_conv_conv_w": _L0_conv_in["conv_w"],
        "L0_conv_conv_b": _L0_conv_in["conv_b"],
        "L0_conv_W_x": _L0_conv_in["W_x"],
        "L0_conv_W_dt": _L0_conv_in["W_dt"],
        "L0_conv_b_dt": _L0_conv_in["b_dt"],
        "L0_conv_A_log": _L0_conv_in["A_log"],
        "L0_conv_D_skip": _L0_conv_in["D_skip"],
        "L0_conv_W_out": _L0_conv_in["W_out"],
        "L0_conv_W_p": _L0_conv_in["W_p"],
        "L0_conv_b_p": _L0_conv_in["b_p"],
        "L0_conv_s1": _L0_conv_in["s1"],
        "L0_conv_s2": _L0_conv_in["s2"],
        "L1_conv_w_kg": _L1_conv_in["w_kg"],
        "L1_conv_b_kg": _L1_conv_in["b_kg"],
        "L1_conv_w_pw": _L1_conv_in["w_pw"],
        "L1_conv_b_pw": _L1_conv_in["b_pw"],
        "L2_ffn_gate_w": _L2_ffn_in["gate_w"],
        "L2_ffn_gate_b": _L2_ffn_in["gate_b"],
        "L2_ffn_weight1": _L2_ffn_in["weight1"],
        "L2_ffn_weight2": _L2_ffn_in["weight2"],
        "L3_attn_fwd_in_proj": _L3_attn_in["fwd_in_proj"],
        "L3_attn_fwd_conv_w": _L3_attn_in["fwd_conv_w"],
        "L3_attn_fwd_conv_b": _L3_attn_in["fwd_conv_b"],
        "L3_attn_fwd_A_log": _L3_attn_in["fwd_A_log"],
        "L3_attn_fwd_dt_bias": _L3_attn_in["fwd_dt_bias"],
        "L3_attn_fwd_D": _L3_attn_in["fwd_D"],
        "L3_attn_fwd_norm_w": _L3_attn_in["fwd_norm_w"],
        "L3_attn_fwd_out_proj": _L3_attn_in["fwd_out_proj"],
        "L3_attn_bwd_in_proj": _L3_attn_in["bwd_in_proj"],
        "L3_attn_bwd_conv_w": _L3_attn_in["bwd_conv_w"],
        "L3_attn_bwd_conv_b": _L3_attn_in["bwd_conv_b"],
        "L3_attn_bwd_A_log": _L3_attn_in["bwd_A_log"],
        "L3_attn_bwd_dt_bias": _L3_attn_in["bwd_dt_bias"],
        "L3_attn_bwd_D": _L3_attn_in["bwd_D"],
        "L3_attn_bwd_norm_w": _L3_attn_in["bwd_norm_w"],
        "L3_attn_bwd_out_proj": _L3_attn_in["bwd_out_proj"],
        "L3_ffn_gate_w": _L3_ffn_in["gate_w"],
        "L3_ffn_gate_b": _L3_ffn_in["gate_b"],
        "L3_ffn_weight1": _L3_ffn_in["weight1"],
        "L3_ffn_weight2": _L3_ffn_in["weight2"],
    }

def reference(x, L0_conv_gamma, L0_conv_beta, L0_conv_W_in, L0_conv_conv_w, L0_conv_conv_b, L0_conv_W_x, L0_conv_W_dt, L0_conv_b_dt, L0_conv_A_log, L0_conv_D_skip, L0_conv_W_out, L0_conv_W_p, L0_conv_b_p, L0_conv_s1, L0_conv_s2, L1_conv_w_kg, L1_conv_b_kg, L1_conv_w_pw, L1_conv_b_pw, L2_ffn_gate_w, L2_ffn_gate_b, L2_ffn_weight1, L2_ffn_weight2, L3_attn_fwd_in_proj, L3_attn_fwd_conv_w, L3_attn_fwd_conv_b, L3_attn_fwd_A_log, L3_attn_fwd_dt_bias, L3_attn_fwd_D, L3_attn_fwd_norm_w, L3_attn_fwd_out_proj, L3_attn_bwd_in_proj, L3_attn_bwd_conv_w, L3_attn_bwd_conv_b, L3_attn_bwd_A_log, L3_attn_bwd_dt_bias, L3_attn_bwd_D, L3_attn_bwd_norm_w, L3_attn_bwd_out_proj, L3_ffn_gate_w, L3_ffn_gate_b, L3_ffn_weight1, L3_ffn_weight2):
    import jax
    import jax.numpy as jnp
    def _L0_conv_ref(x, gamma, beta, W_in, conv_w, conv_b, W_x, W_dt, b_dt, A_log, D_skip, W_out, W_p, b_p, s1, s2):
        import jax, jax.numpy as jnp
        import numpy as np
        D_CONV = 4
        D_STATE = 16
        GROUP = 8

        def _ln(x, g, b):
            mu = x.mean(-1, keepdims=True)
            v = ((x - mu) ** 2).mean(-1, keepdims=True)
            return (x - mu) * jax.lax.rsqrt(v + 1e-05) * g + b

        def _mamba(x, W_in, conv_w, conv_b, W_x, W_dt, b_dt, A_log, D_skip, W_out):
            B, L, Dm = x.shape
            d_inner = W_in.shape[0] // 2
            dt_rank = W_dt.shape[1]
            xz = x @ W_in.T
            xi, z = (xz[..., :d_inner], xz[..., d_inner:])
            xc = jax.lax.conv_general_dilated(xi.transpose(0, 2, 1), conv_w, (1,), [(D_CONV - 1, 0)], feature_group_count=d_inner, dimension_numbers=('NCH', 'OIH', 'NCH'))
            u = jax.nn.silu((xc + conv_b[:, None]).transpose(0, 2, 1))
            x_dbl = u @ W_x.T
            dt = jax.nn.softplus(x_dbl[..., :dt_rank] @ W_dt.T + b_dt)
            Bs = x_dbl[..., dt_rank:dt_rank + D_STATE]
            Cs = x_dbl[..., dt_rank + D_STATE:]
            A = -jnp.exp(A_log)

            def step(h, inp):
                dt_t, B_t, C_t, u_t = inp
                dA = jnp.exp(dt_t[..., None] * A)
                h = dA * h + (dt_t * u_t)[..., None] * B_t[:, None, :]
                return (h, jnp.einsum('bdn,bn->bd', h, C_t))
            h0 = jnp.zeros((B, d_inner, D_STATE), x.dtype)
            _, ys = jax.lax.scan(step, h0, (dt.transpose(1, 0, 2), Bs.transpose(1, 0, 2), Cs.transpose(1, 0, 2), u.transpose(1, 0, 2)))
            y = ys.transpose(1, 0, 2) + u * D_skip
            return y * jax.nn.silu(z) @ W_out.T
        B, C, W, H = x.shape
        L = W * H
        x_flat = x.reshape(B, C, L).transpose(0, 2, 1)
        x1 = _ln(x_flat, gamma, beta)
        cpg = C // GROUP
        x2 = x.reshape(B, GROUP, cpg, W, H).transpose(0, 2, 1, 3, 4).reshape(B, C, L).transpose(0, 2, 1)
        x2 = _ln(x2, gamma, beta)
        m = lambda t: _mamba(t, W_in, conv_w, conv_b, W_x, W_dt, b_dt, A_log, D_skip, W_out)
        xm = m(x1) + x1 * s1 + (m(x2) + x2 * s2)
        xm = _ln(xm, gamma, beta)
        out = xm @ W_p.T + b_p
        return out.transpose(0, 2, 1).reshape(B, -1, W, H)

    def _L1_conv_ref(x, w_kg, b_kg, w_pw, b_pw):
        import jax, jax.numpy as jnp
        from jax import lax
        import numpy as np
        B, C, H, W = (8, 128, 112, 112)
        G, K, OC = (4, 3, 128)
        DN = ('NCHW', 'OIHW', 'NCHW')
        b, c, h, w = x.shape
        kernel = lax.conv_general_dilated(x, w_kg, (1, 1), ((K // 2, K // 2), (K // 2, K // 2)), feature_group_count=G, dimension_numbers=DN)
        kernel = kernel + b_kg[None, :, None, None]
        kernel = kernel.reshape(b, G, K * K, h, w)
        p = K // 2
        xp = jnp.pad(x, ((0, 0), (0, 0), (p, p), (p, p)))
        patches = jnp.stack([xp[:, :, i:i + h, j:j + w] for i in range(K) for j in range(K)], axis=2)
        patches = patches.reshape(b, G, c // G, K * K, h, w)
        out = (patches * kernel[:, :, None]).sum(axis=3).reshape(b, c, h, w)
        out = lax.conv_general_dilated(out, w_pw, (1, 1), 'VALID', feature_group_count=G, dimension_numbers=DN)
        return out + b_pw[None, :, None, None]

    def _L2_attn_ref(q):
        import jax, jax.numpy as jnp
        import numpy as np
        HIDDEN_SIZE = 128
        MASK_LEN = 2048
        BATCH = 16
        L = q.shape[1]
        scale = 1.0 / np.sqrt(HIDDEN_SIZE).astype(np.float32)
        sim = jnp.einsum('blh,bmh->blm', q, q) * scale
        diag = jnp.eye(L, dtype=bool)
        sim = jnp.where(diag[None, :, :], jnp.float32(-1000000000.0), sim)
        attn = jax.nn.softmax(sim, axis=-1)
        return jnp.einsum('blm,bmh->blh', attn, q)

    def _L2_ffn_ref(x, gate_w, gate_b, weight1, weight2):
        import jax, jax.numpy as jnp
        import numpy as np
        B, S, D, E, H, O, K = (512, 2048, 128, 64, 512, 128, 8)
        Bn, Sn, Dn = x.shape
        logits = jnp.einsum('bsd,ed->bse', x, gate_w) + gate_b
        probs = jax.nn.softmax(logits, axis=1)
        vals, idx = jax.lax.top_k(probs.transpose(0, 2, 1), K)
        topv = vals.transpose(0, 2, 1)
        topi = idx.transpose(0, 2, 1)
        flat_idx = topi.reshape(Bn, K * E)
        gathered = jnp.take_along_axis(x, flat_idx[:, :, None], axis=1)
        gathered = gathered.reshape(Bn, K, E, Dn)
        pooled = jnp.einsum('bked,bke->bed', gathered, topv)
        ones = jnp.ones((E, Bn, 1), dtype=x.dtype)
        h = jnp.concatenate([pooled.transpose(1, 0, 2), ones], axis=-1)
        h = jax.nn.gelu(jnp.einsum('ebd,edh->ebh', h, weight1), approximate=False)
        h = jnp.concatenate([h, ones], axis=-1)
        out = jnp.einsum('ebh,eho->ebo', h, weight2)
        out = out.transpose(1, 0, 2)
        weighted = jnp.einsum('beo,bke->bkeo', out, topv).reshape(Bn, K * E, O)
        outputs = jnp.zeros((Bn, Sn, O), dtype=x.dtype)
        outputs = outputs.at[jnp.arange(Bn)[:, None], flat_idx].add(weighted)
        return outputs

    def _L3_attn_ref(x, fwd_in_proj, fwd_conv_w, fwd_conv_b, fwd_A_log, fwd_dt_bias, fwd_D, fwd_norm_w, fwd_out_proj, bwd_in_proj, bwd_conv_w, bwd_conv_b, bwd_A_log, bwd_dt_bias, bwd_D, bwd_norm_w, bwd_out_proj):
        import jax, jax.numpy as jnp
        import numpy as np
        CHUNK = 64
        D_MODEL = 128
        D_STATE = 64
        HEADDIM = 64
        D_INNER = 2 * D_MODEL
        NHEADS = D_INNER // HEADDIM
        CONV_DIM = D_INNER + 2 * D_STATE
        K = 4
        D_IN_PROJ = 2 * D_INNER + 2 * D_STATE + NHEADS
        EPS = 1e-05

        def _segsum(t):
            L = t.shape[-1]
            cs = jnp.cumsum(t, -1)
            seg = cs[..., :, None] - cs[..., None, :]
            mask = jnp.tril(jnp.ones((L, L), bool))
            return jnp.where(mask, seg, -jnp.inf)

        def _ssd(xh, dt, A, Bm, Cm):
            b, l, h, p = xh.shape
            n = Bm.shape[-1]
            c = l // CHUNK
            xdt = xh * dt[..., None]
            dA = dt * A
            rc = lambda t: t.reshape(b, c, CHUNK, *t.shape[2:])
            xc, dAc, Bc, Cc = (rc(xdt), rc(dA), rc(Bm), rc(Cm))
            Acs = jnp.cumsum(dAc, axis=2)
            Lmat = jnp.exp(_segsum(dAc.transpose(0, 1, 3, 2)))
            Y_diag = jnp.einsum('bcln,bcsn,bchls,bcshp->bclhp', Cc, Bc, Lmat, xc)
            decay_st = jnp.exp(Acs[:, :, -1:, :] - Acs)
            states = jnp.einsum('bcln,bclh,bclhp->bchpn', Bc, decay_st, xc)
            chunk_decay = jnp.exp(Acs[:, :, -1])

            def step(carry, inp):
                st, dec = inp
                new = st + carry * dec[:, :, None, None]
                return (new, carry)
            init = jnp.zeros((b, h, p, n), xh.dtype)
            _, prev = jax.lax.scan(step, init, (states.transpose(1, 0, 2, 3, 4), chunk_decay.transpose(1, 0, 2)))
            prev = prev.transpose(1, 0, 2, 3, 4)
            Y_off = jnp.einsum('bcln,bchpn,bclh->bclhp', Cc, prev, jnp.exp(Acs))
            return (Y_diag + Y_off).reshape(b, l, h, p)

        def _mamba3(x, in_proj, conv_w, conv_b, A_log, dt_bias, D, norm_w, out_proj):
            b, l, _ = x.shape
            zxbcdt = x @ in_proj
            z, xbc, dt = jnp.split(zxbcdt, [D_INNER, D_INNER + CONV_DIM], axis=-1)
            xp = jnp.pad(xbc, ((0, 0), (K - 1, 0), (0, 0)))
            conv = sum((xp[:, i:i + l, :] * conv_w[:, i] for i in range(K))) + conv_b
            xbc = jax.nn.silu(conv)
            xh, Bm, Cm = jnp.split(xbc, [D_INNER, D_INNER + D_STATE], axis=-1)
            xh = xh.reshape(b, l, NHEADS, HEADDIM)
            dt = jax.nn.softplus(dt + dt_bias)
            A = -jnp.exp(A_log)
            y = _ssd(xh, dt, A, Bm, Cm) + xh * D[None, None, :, None]
            yg = y.reshape(b, l, D_INNER) * jax.nn.silu(z)
            yn = yg * jax.lax.rsqrt(jnp.mean(yg * yg, -1, keepdims=True) + EPS) * norm_w
            return yn @ out_proj
        h_f = _mamba3(x, fwd_in_proj, fwd_conv_w, fwd_conv_b, fwd_A_log, fwd_dt_bias, fwd_D, fwd_norm_w, fwd_out_proj)
        xr = x[:, ::-1, :]
        h_b = _mamba3(xr, bwd_in_proj, bwd_conv_w, bwd_conv_b, bwd_A_log, bwd_dt_bias, bwd_D, bwd_norm_w, bwd_out_proj)[:, ::-1, :]
        return h_f + h_b

    def _L3_ffn_ref(x, gate_w, gate_b, weight1, weight2):
        import jax, jax.numpy as jnp
        import numpy as np
        B, S, D, E, H, O, K = (512, 2048, 128, 64, 512, 128, 8)
        Bn, Sn, Dn = x.shape
        logits = jnp.einsum('bsd,ed->bse', x, gate_w) + gate_b
        probs = jax.nn.softmax(logits, axis=1)
        vals, idx = jax.lax.top_k(probs.transpose(0, 2, 1), K)
        topv = vals.transpose(0, 2, 1)
        topi = idx.transpose(0, 2, 1)
        flat_idx = topi.reshape(Bn, K * E)
        gathered = jnp.take_along_axis(x, flat_idx[:, :, None], axis=1)
        gathered = gathered.reshape(Bn, K, E, Dn)
        pooled = jnp.einsum('bked,bke->bed', gathered, topv)
        ones = jnp.ones((E, Bn, 1), dtype=x.dtype)
        h = jnp.concatenate([pooled.transpose(1, 0, 2), ones], axis=-1)
        h = jax.nn.gelu(jnp.einsum('ebd,edh->ebh', h, weight1), approximate=False)
        h = jnp.concatenate([h, ones], axis=-1)
        out = jnp.einsum('ebh,eho->ebo', h, weight2)
        out = out.transpose(1, 0, 2)
        weighted = jnp.einsum('beo,bke->bkeo', out, topv).reshape(Bn, K * E, O)
        outputs = jnp.zeros((Bn, Sn, O), dtype=x.dtype)
        outputs = outputs.at[jnp.arange(Bn)[:, None], flat_idx].add(weighted)
        return outputs

    def _gn(v, G=32, eps=1e-5):
        B_, C_, H_, W_ = v.shape
        g = v.reshape(B_, G, C_ // G, H_, W_)
        m = jnp.mean(g, axis=(2, 3, 4), keepdims=True)
        s = jnp.var(g, axis=(2, 3, 4), keepdims=True)
        return ((g - m) / jnp.sqrt(s + eps)).reshape(v.shape)

    def _ln_c(v, eps=1e-6):
        m = jnp.mean(v, axis=1, keepdims=True)
        s = jnp.var(v, axis=1, keepdims=True)
        return (v - m) / jnp.sqrt(s + eps)

    def _ln_t(v, eps=1e-5):
        m = jnp.mean(v, axis=-1, keepdims=True)
        s = jnp.var(v, axis=-1, keepdims=True)
        return (v - m) / jnp.sqrt(s + eps)

    def _to_tokens(v):
        B_, C_, H_, W_ = v.shape
        return v.reshape(B_, C_, H_ * W_).transpose(0, 2, 1)
    def _from_tokens(t, like):
        B_, C_, H_, W_ = like.shape
        return t.transpose(0, 2, 1).reshape(B_, C_, H_, W_)

    x = x + _L0_conv_ref(_gn(x), L0_conv_gamma, L0_conv_beta, L0_conv_W_in, L0_conv_conv_w, L0_conv_conv_b, L0_conv_W_x, L0_conv_W_dt, L0_conv_b_dt, L0_conv_A_log, L0_conv_D_skip, L0_conv_W_out, L0_conv_W_p, L0_conv_b_p, L0_conv_s1, L0_conv_s2)
    x = x + _L1_conv_ref(_gn(x), L1_conv_w_kg, L1_conv_b_kg, L1_conv_w_pw, L1_conv_b_pw)
    t = _to_tokens(x)
    t = t + _L2_attn_ref(_ln_t(t))
    t = t + _L2_ffn_ref(_ln_t(t), L2_ffn_gate_w, L2_ffn_gate_b, L2_ffn_weight1, L2_ffn_weight2)
    t = t + _L3_attn_ref(_ln_t(t), L3_attn_fwd_in_proj, L3_attn_fwd_conv_w, L3_attn_fwd_conv_b, L3_attn_fwd_A_log, L3_attn_fwd_dt_bias, L3_attn_fwd_D, L3_attn_fwd_norm_w, L3_attn_fwd_out_proj, L3_attn_bwd_in_proj, L3_attn_bwd_conv_w, L3_attn_bwd_conv_b, L3_attn_bwd_A_log, L3_attn_bwd_dt_bias, L3_attn_bwd_D, L3_attn_bwd_norm_w, L3_attn_bwd_out_proj)
    t = t + _L3_ffn_ref(_ln_t(t), L3_ffn_gate_w, L3_ffn_gate_b, L3_ffn_weight1, L3_ffn_weight2)
    x = _from_tokens(t, x)
    return x


_drawn_inputs = setup_inputs


def setup_inputs(seed=0):
    import zlib

    import numpy as np

    out = dict(_drawn_inputs(seed))
    spreads = {'L0_conv_gamma': (1.0, 0.2),
     'L0_conv_beta': (0.0, 0.1),
     'L0_conv_conv_b': (0.0, 0.8),
     'L0_conv_D_skip': (1.0, 0.6),
     'L0_conv_b_p': (0.0, 0.1),
     'L2_ffn_gate_b': (0.0, 0.8),
     'L3_attn_fwd_conv_b': (0.0, 0.1),
     'L3_attn_fwd_D': (1.0, 0.2),
     'L3_attn_fwd_norm_w': (1.0, 0.2),
     'L3_attn_bwd_conv_b': (0.0, 0.1),
     'L3_attn_bwd_D': (1.0, 0.2),
     'L3_attn_bwd_norm_w': (1.0, 0.2),
     'L3_ffn_gate_b': (0.0, 0.1)}
    factors = {'L0_conv_W_in': 8.0,
     'L0_conv_conv_w': 8.0,
     'L0_conv_W_x': 8.0,
     'L0_conv_W_dt': 8.0,
     'L0_conv_b_dt': 8.0,
     'L0_conv_A_log': 8.0,
     'L0_conv_W_out': 8.0,
     'L2_ffn_gate_w': 8.0,
     'L2_ffn_weight1': 8.0,
     'L2_ffn_weight2': 8.0,
     'L3_ffn_gate_w': 8.0,
     'L3_ffn_weight1': 8.0,
     'L3_ffn_weight2': 8.0}
    for name, (base, spread) in spreads.items():
        noise = np.random.default_rng([zlib.crc32(name.encode()), seed]).standard_normal(out[name].shape)
        drawn = base * np.exp(spread * noise) if base else spread * noise
        out[name] = jnp.asarray(drawn.astype(out[name].dtype))
    for name, factor in factors.items():
        out[name] = (out[name] * factor).astype(out[name].dtype)
    return out
```

```python
import math
from contextlib import ExitStack

import numpy as np

import concourse.bass as bass
from concourse import mybir

F32 = mybir.dt.float32
BF16 = mybir.dt.bfloat16
ACT = mybir.ActivationFunctionType
ALU = mybir.AluOpType
AX = mybir.AxisListType

BATCH, CH, IMG = 4, 128, 64
TOK = IMG * IMG
TILE = 512
TPB = TOK // TILE
NT = BATCH * TPB
LEAD = 32


class Part:

    def __init__(self, nc, name):
        self.nc, self.name, self.stack, self.held = nc, name, ExitStack(), []

    def __enter__(self):
        self.stack.__enter__()
        return self

    def __exit__(self, *exc):
        if exc[0] is None and self.held:
            with self.nc.Block() as block:
                @block.sync
                def _(sp):
                    for held in self.held:
                        sp.sem_clear(held)
        return self.stack.__exit__(*exc)

    def sb(self, name, shape, dt=F32):
        return self.stack.enter_context(self.nc.sbuf_tensor(f"{self.name}_{name}", shape, dt))

    def ps(self, name, shape, dt=F32):
        return self.stack.enter_context(self.nc.psum_tensor(f"{self.name}_{name}", shape, dt))

    def sem(self, name):
        held = self.stack.enter_context(self.nc.semaphore(f"{self.name}_{name}"))
        self.held.append(held)
        return held

    def sems(self, names):
        return [self.sem(n) for n in names.split()]


def prime(nc, sems):
    with nc.Block() as block:
        @block.sync
        def _(sp):
            for s in sems:
                sp.sem_inc(s, LEAD)


def chunk(i, size=TILE):
    return bass.ds(i * size, size)


def column(ap):
    return ap.rearrange("(p n) -> p n", n=1)


def half_columns(ap):
    return ap.rearrange("(h p) -> p h", p=128)


def build_constants(nc, const):
    with Part(nc, "kc") as part:
        ready, = part.sems("ready")
        with nc.Block() as block:
            @block.gpsimd
            def _(pool):
                nc.gpsimd.memset(const.ident[:], 0.0).then_inc(ready, 1)
                nc.gpsimd.memset(const.center[:], -1.0 / CH).then_inc(ready, 1)
                nc.gpsimd.memset(const.mean[:], 1.0 / CH).then_inc(ready, 1)
                nc.gpsimd.memset(const.eps[:], 1e-5).then_inc(ready, 1)
                pool.wait_ge(ready, 4)
                nc.gpsimd.affine_select(out=const.ident[:], in_=const.ident[:], compare_op=ALU.not_equal, fill=1.0,
                                        base=0, pattern=[[-1, CH]], channel_multiplier=1).then_inc(ready, 1)
                nc.gpsimd.affine_select(out=const.center[:], in_=const.center[:], compare_op=ALU.not_equal,
                                        fill=1.0 - 1.0 / CH, base=0, pattern=[[-1, CH]],
                                        channel_multiplier=1).then_inc(ready, 1)
                pool.wait_ge(ready, 6)


class Constants:

    def __init__(self, part):
        self.x = part.sb("x", [CH, BATCH * TOK])
        self.ident = part.sb("ident", [CH, CH])
        self.center = part.sb("center", [CH, CH])
        self.mean = part.sb("mean", [CH, CH])
        self.eps = part.sb("eps", [CH, 1])


def load_x(nc, const, x):
    with Part(nc, "lx") as part:
        loaded, = part.sems("loaded")
        with nc.Block() as block:
            @block.sync
            def _(sp):
                for b in range(BATCH):
                    sp.dma_start(const.x[:, b * TOK:(b + 1) * TOK],
                                 x[b].rearrange("c h w -> c (h w)")).then_inc(loaded, 16)
                sp.wait_ge(loaded, 16 * BATCH)


def store_x(nc, const, out):
    with Part(nc, "sx") as part:
        stored, = part.sems("stored")
        with nc.Block() as block:
            @block.sync
            def _(sp):
                for b in range(BATCH):
                    sp.dma_start(out[b].rearrange("c h w -> c (h w)"),
                                 const.x[:, b * TOK:(b + 1) * TOK]).then_inc(stored, 16)
                sp.wait_ge(stored, 16 * BATCH)


def build_group_norm(nc, const, name, scale, shift):
    GROUPS, PER = 32, CH // 32
    PIECES = TOK // 512
    with Part(nc, name) as part:
        stats = part.sb("stats", [CH, BATCH, PIECES, 6])
        mv = part.sb("mv", [CH, BATCH, 2])
        moments = part.sb("moments", [CH, 2, BATCH])
        member = part.sb("member", [CH, CH])
        group = part.sb("group", [CH, 2, BATCH])
        msq = part.sb("msq", [CH, BATCH])
        var = part.sb("var", [CH, BATCH])
        averaged = part.ps("averaged", [CH, 2, BATCH])
        stats_done, step, member_done, averaged_done, var_done, log_done, rstd_done = part.sems(
            "stats_done step member_done averaged_done var_done log_done rstd_done")
        with nc.Block() as block:
            @block.gpsimd
            def _(pool):
                v = member[:].rearrange("p (g k) -> p g k", k=PER)
                nc.gpsimd.memset(member[:], 1.0 / PER).then_inc(member_done, 1)
                pool.wait_ge(member_done, 1)
                nc.gpsimd.affine_select(out=v, in_=v, compare_op=ALU.is_ge, fill=0.0, base=0,
                                        pattern=[[-PER, GROUPS], [0, PER]], channel_multiplier=1).then_inc(member_done, 1)
                pool.wait_ge(member_done, 2)
                nc.gpsimd.affine_select(out=v, in_=v, compare_op=ALU.is_ge, fill=0.0, base=PER - 1,
                                        pattern=[[PER, GROUPS], [0, PER]], channel_multiplier=-1).then_inc(member_done, 1)

            @block.vector
            def _(dve):
                for b in range(BATCH):
                    for i in range(PIECES):
                        nc.vector.bn_stats(stats[:, b, i, :], const.x[:, chunk(b * PIECES + i)]).then_inc(stats_done, 1)
                dve.wait_ge(stats_done, BATCH * PIECES)
                for b in range(BATCH):
                    nc.vector.bn_aggr(mv[:, b, :], stats[:, b, :, :]).then_inc(step, 1)
                dve.wait_ge(step, 4)
                nc.vector.tensor_copy(moments[:, 0, :], mv[:, :, 0]).then_inc(step, 1)
                nc.vector.tensor_tensor(msq[:], mv[:, :, 0], mv[:, :, 0], ALU.mult).then_inc(step, 1)
                dve.wait_ge(step, 6)
                nc.vector.tensor_tensor(moments[:, 1, :], mv[:, :, 1], msq[:], ALU.add).then_inc(step, 1)
                dve.wait_ge(averaged_done, 1)
                nc.vector.tensor_copy(group[:], averaged[:]).then_inc(step, 1)
                dve.wait_ge(step, 8)
                nc.vector.tensor_tensor(msq[:], group[:, 0, :], group[:, 0, :], ALU.mult).then_inc(step, 1)
                dve.wait_ge(step, 9)
                nc.vector.tensor_tensor(var[:], group[:, 1, :], msq[:], ALU.subtract).then_inc(var_done, 1)
                dve.wait_ge(rstd_done, 1)
                nc.vector.scalar_tensor_tensor(out=shift[:], in0=group[:, 0, :], scalar=-1.0, in1=scale[:],
                                               op0=ALU.mult, op1=ALU.mult).then_inc(step, 1)
                dve.wait_ge(step, 10)

            @block.tensor
            def _(pe):
                pe.wait_ge(member_done, 3)
                pe.wait_ge(step, 7)
                nc.tensor.matmul(averaged[:].rearrange("p a b -> p (a b)"), member[:],
                                 moments[:].rearrange("p a b -> p (a b)"), start=True, stop=True).then_inc(averaged_done, 1)

            @block.scalar
            def _(act):
                nc.scalar.preload_act_table_set("natural_log_exp_and_others")
                act.wait_ge(var_done, 1)
                nc.scalar.activation(var[:], var[:], ACT.Ln, bias=const.eps[:, 0:1]).then_inc(log_done, 1)
                act.wait_ge(log_done, 1)
                nc.scalar.activation(scale[:], var[:], ACT.Exp, scale=-0.5).then_inc(rstd_done, 1)


def build_layer_norm(nc, const, name, dst, affine=None, src=None, project=None, extra=False):
    with Part(nc, name) as part:
        tin = part.sb("in", [CH, 2, TILE])
        square = part.sb("square", [CH, 2, TILE])
        logv = part.sb("logv", [CH, 2, TILE])
        rstd = part.sb("rstd", [CH, 2, TILE])
        normed = part.sb("normed", [CH, 2, TILE])
        centred = part.ps("centred", [CH, 2, TILE])
        variance = part.ps("variance", [CH, 2, TILE])
        projected = part.ps("projected", [CH, 2, TILE])
        (in_ready, centre_done, square_done, var_done, log_done, rstd_done, normed_done,
         projected_done, added) = sems = part.sems(
            "in_ready centre_done square_done var_done log_done rstd_done normed_done projected_done added")
        in_loaded = part.sems("in_loaded0 in_loaded1")
        stored = part.sems("stored0 stored1")
        prime(nc, (*sems, *stored))

        with nc.Block() as block:
            @block.sync
            def _(sp):
                if src is not None:
                    with sp.Fori(0, NT // 2) as i:
                        for k in range(2):
                            t = 2 * i + k
                            sp.wait_ge(centre_done, LEAD + t - 1)
                            sp.dma_start(tin[:, k, :], src[:, chunk(t)]).then_inc(in_loaded[k], 16)
                if dst is not None:
                    with sp.Fori(0, NT // 2) as i:
                        for k in range(2):
                            t = 2 * i + k
                            sp.wait_ge(normed_done, LEAD + t + 1)
                            sp.dma_start(dst[:, chunk(t)], normed[:, k, :]).then_inc(stored[k], 16)
                    if extra:
                        sp.dma_start(dst[:, chunk(NT)], normed[:, 1, :]).then_inc(stored[1], 16)
                    sp.wait_ge(stored[0], LEAD + 8 * NT)
                    sp.wait_ge(stored[1], LEAD + 8 * NT + 16 * int(extra))

            @block.tensor
            def _(pe):
                def centre(t, k, i):
                    if src is not None:
                        pe.wait_ge(in_loaded[k], 16 * (i + 1))
                        rhs = tin[:, k, :]
                    elif affine is not None:
                        pe.wait_ge(in_ready, LEAD + t + 1)
                        rhs = tin[:, k, :]
                    else:
                        rhs = const.x[:, chunk(t)]
                    pe.wait_ge(normed_done, LEAD + t - 1)
                    nc.tensor.matmul(centred[:, k, :], const.center[:], rhs, start=True, stop=True).then_inc(centre_done, 1)

                with pe.Fori(0, NT // 2) as i:
                    for k in range(2):
                        centre(2 * i + k, k, i)
                    for k in range(2):
                        t = 2 * i + k
                        pe.wait_ge(square_done, LEAD + t + 1)
                        pe.wait_ge(log_done, LEAD + t - 1)
                        nc.tensor.matmul(variance[:, k, :], const.mean[:], square[:, k, :], start=True, stop=True
                                         ).then_inc(var_done, 1)
                    if project is not None:
                        for k in range(2):
                            t = 2 * i + k
                            pe.wait_ge(normed_done, LEAD + t + 1)
                            pe.wait_ge(added, LEAD + t - 1)
                            nc.tensor.matmul(projected[:, k, :], project[0][:], normed[:, k, :], start=True, stop=True
                                             ).then_inc(projected_done, 1)

            @block.scalar
            def _(act):
                nc.scalar.preload_act_table_set("natural_log_exp_and_others")
                with act.Fori(0, NT // 2) as i:
                    for k in range(2):
                        t = 2 * i + k
                        act.wait_ge(centre_done, LEAD + t + 1)
                        act.wait_ge(var_done, LEAD + t - 1)
                        nc.scalar.activation(square[:, k, :], centred[:, k, :], ACT.Square).then_inc(square_done, 1)
                    for k in range(2):
                        t = 2 * i + k
                        act.wait_ge(var_done, LEAD + t + 1)
                        act.wait_ge(rstd_done, LEAD + t - 1)
                        nc.scalar.activation(logv[:, k, :], variance[:, k, :], ACT.Ln, bias=const.eps[:, 0:1]
                                             ).then_inc(log_done, 1)
                        act.wait_ge(log_done, LEAD + t + 1)
                        act.wait_ge(normed_done, LEAD + t - 1)
                        nc.scalar.activation(rstd[:, k, :], logv[:, k, :], ACT.Exp, scale=-0.5).then_inc(rstd_done, 1)

            @block.vector
            def _(dve):
                with dve.Fori(0, BATCH) as b, dve.Fori(0, TPB // 2) as j:
                    i = b * (TPB // 2) + j
                    if affine is not None:
                        scale, shift = affine
                        for k in range(2):
                            t = 2 * i + k
                            dve.wait_ge(centre_done, LEAD + t - 1)
                            nc.vector.tensor_scalar(tin[:, k, :], const.x[:, chunk(t)], scale[:, bass.ds(b, 1)],
                                                    shift[:, bass.ds(b, 1)], ALU.mult, ALU.add).then_inc(in_ready, 1)
                    for k in range(2):
                        t = 2 * i + k
                        dve.wait_ge(rstd_done, LEAD + t + 1)
                        dve.wait_ge(centre_done, LEAD + t + 1)
                        if dst is not None:
                            dve.wait_ge(stored[k], LEAD + 16 * i)
                        if project is not None:
                            dve.wait_ge(projected_done, LEAD + t - 1)
                        nc.vector.tensor_tensor(normed[:, k, :], centred[:, k, :], rstd[:, k, :], ALU.mult
                                                ).then_inc(normed_done, 1)
                    if project is not None:
                        for k in range(2):
                            t = 2 * i + k
                            dve.wait_ge(projected_done, LEAD + t + 1)
                            nc.vector.scalar_tensor_tensor(
                                out=const.x[:, chunk(t)], in0=projected[:, k, :], scalar=project[1][:, 0:1],
                                in1=const.x[:, chunk(t)], op0=ALU.add, op1=ALU.add).then_inc(added, 1)


def build_transposes(nc, name, const, jobs, after=0, loaded=None):
    with Part(nc, name) as part:
        tile = part.ps("tile", [CH, 2, TILE])
        transposed, copied = part.sems("transposed copied")
        prime(nc, (copied,))
        with nc.Block() as block:
            @block.tensor
            def _(pe):
                for n, (out, src, _) in enumerate(jobs):
                    rows, cols = src.shape[0], src.shape[1]
                    pe.wait_ge(copied, LEAD + n - 1)
                    nc.tensor.transpose(tile[0:cols, n % 2, 0:rows], src, const.ident[0:rows, 0:rows]
                                        ).then_inc(transposed, 1)

            @block.vector
            def _(dve):
                for n, (out, src, scalar) in enumerate(jobs):
                    rows, cols = src.shape[0], src.shape[1]
                    dve.wait_ge(transposed, n + 1)
                    if scalar is None:
                        nc.vector.tensor_copy(out, tile[0:cols, n % 2, 0:rows]).then_inc(copied, 1)
                    else:
                        nc.vector.tensor_scalar(out, tile[0:cols, n % 2, 0:rows], scalar, None, ALU.mult
                                                ).then_inc(copied, 1)


def build_mamba(nc, const, w, normed_dram, mixed_dram, wp_t, bp):
    DI, NS, RANK, TAPS, GROUP = 256, 16, 8, 4, 8
    HALVES, CPG = DI // CH, CH // GROUP
    STEPS = 2 * NS
    AHEAD = 4
    CAP = 40.0
    ALMOST_ONE = 1.0 - 2.0 ** -23
    with Part(nc, "m") as part:
        win_t = [part.sb(f"win_t{v}", [CH, 2 * DI]) for v in range(2)]
        wx_t = part.sb("wx_t", [CH, HALVES, CH])
        wdt_t = part.sb("wdt_t", [RANK, DI])
        wout_t = part.sb("wout_t", [CH, HALVES, CH])
        skip_t = part.sb("skip_t", [CH, CH])
        pick = part.sb("pick", [CH, 2 * NS], BF16)
        taps = part.sb("taps", [CH, HALVES, TAPS])
        conv_b = part.sb("conv_b", [CH, HALVES])
        dt_b = part.sb("dt_b", [CH, HALVES])
        decay = part.sb("decay", [CH, HALVES, NS])
        d_skip = part.sb("d_skip", [CH, HALVES])
        in_b = part.sb("in_b", [CH, 2 * HALVES])
        out_b = part.sb("out_b", [CH, 1])
        keep = part.sb("keep", [CH, NT + 1])
        almost_one = part.sb("almost_one", [CH, 1])
        keep_now = part.sb("keep_now", [CH, 1])

        with Part(nc, "mw") as pre:
            win = pre.sb("win", [CH, 4, CH])
            win_p = pre.sb("win_p", [CH, 4, CH])
            win_raw_t = pre.sb("win_raw_t", [CH, 4 * CH])
            wx = pre.sb("wx", [RANK + 2 * NS, DI])
            wx_half_t = pre.sb("wx_half_t", [CH, HALVES, RANK + 2 * NS])
            wout = pre.sb("wout", [CH, DI])
            wp = pre.sb("wp", [CH, CH])
            wp_raw_t = pre.sb("wp_raw_t", [CH, CH])
            a_log = pre.sb("a_log", [CH, HALVES, NS])
            gamma = pre.sb("gamma", [CH, 2])
            beta = pre.sb("beta", [CH, 1])
            b_p = pre.sb("b_p", [CH, 1])
            s_row = pre.sb("s_row", [1, 2])
            ones_row = pre.sb("ones_row", [1, CH])
            s_col = pre.sb("s_col", [CH, 2])
            gs = pre.sb("gs", [CH, 2])
            regroup = pre.sb("regroup", [CH, CH])
            s_sum = pre.sb("s_sum", [CH, 1])
            s_ps = pre.ps("s_ps", [CH, 2])
            b_ps = pre.ps("b_ps", [CH, 8])
            loaded, made, step, exp_done, mm_done, pe_go = pre.sems("loaded made step exp_done mm_done pe_go")
            with nc.Block() as block:
                @block.sync
                def _(sp):
                    with nc.allow_non_contiguous_dma("small weights"):
                        n = 0
                        for dst, src in (
                                (win[:], w["W_in"].rearrange("(t p) c -> p t c", p=CH)),
                                (wx[:], w["W_x"]), (wout[:], w["W_out"]), (wp[:], w["W_p"]),
                                (wdt_t[:], w["W_dt"].rearrange("d r -> r d")),
                                (a_log[:], w["A_log"].rearrange("(h p) n -> p h n", p=CH)),
                                (taps[:], w["conv_w"].rearrange("(h p) o k -> p h (o k)", p=CH)),
                                (conv_b[:], half_columns(w["conv_b"])), (dt_b[:], half_columns(w["b_dt"])),
                                (d_skip[:], half_columns(w["D_skip"])),
                                (gamma[:, 0:1], column(w["gamma"])), (beta[:], column(w["beta"])),
                                (b_p[:], column(w["b_p"])), (s_row[0:1, 0:1], column(w["s1"])),
                                (s_row[0:1, 1:2], column(w["s2"]))):
                            sp.dma_start(dst, src).then_inc(loaded, 16)
                            n += 1
                        for g in range(GROUP):
                            sp.dma_start(gamma[g * CPG:(g + 1) * CPG, 1:2],
                                         w["gamma"].rearrange("(a b n) -> b a n", b=GROUP, n=1)[g]).then_inc(loaded, 16)
                            n += 1
                        sp.wait_ge(loaded, 16 * n)

                @block.gpsimd
                def _(pool):
                    nc.gpsimd.memset(ones_row[:], 1.0).then_inc(made, 1)
                    nc.gpsimd.memset(pick[:], 0.0).then_inc(made, 1)
                    nc.gpsimd.memset(keep[:], 1.0).then_inc(made, 1)
                    nc.gpsimd.memset(wx_t[:], 0.0).then_inc(made, 1)
                    nc.gpsimd.memset(almost_one[:], ALMOST_ONE).then_inc(made, 1)
                    pool.wait_ge(made, 5)
                    for n, base in enumerate((0, 64, 96)):
                        nc.gpsimd.affine_select(out=pick[:], in_=pick[:], compare_op=ALU.not_equal, fill=1.0,
                                                base=-base, pattern=[[-1, 2 * NS]],
                                                channel_multiplier=1).then_inc(made, 1)
                        pool.wait_ge(made, 6 + n)
                    nc.gpsimd.memset(keep[:, 0:NT + 1:TPB], 0.0).then_inc(made, 1)
                    pool.wait_ge(made, 9)

            jobs = [(win_raw_t[:, chunk(i, CH)], win[:, i, :], None) for i in range(4)]
            jobs += [(win_t[0][:, chunk(i, CH)], win[:, i, :], gamma[:, 0:1]) for i in range(4)]
            jobs += [(win_t[1][:, chunk(i, CH)], win_p[:, i, :], gamma[:, 1:2]) for i in range(4)]
            jobs += [(wx_half_t[:, h, :], wx[:, chunk(h, CH)], None) for h in range(HALVES)]
            jobs += [(wout_t[:, h, :], wout[:, chunk(h, CH)], None) for h in range(HALVES)]
            jobs += [(wp_raw_t[:], wp[:], None), (wp_t[:], wp[:], gamma[:, 0:1])]
            with nc.Block() as block:
                @block.vector
                def _(dve):
                    for i in range(4):
                        nc.vector.tensor_copy(win_p[:, i, :].rearrange("o (b a) -> o b a", b=GROUP),
                                              win[:, i, :].rearrange("o (a b) -> o b a", b=GROUP)).then_inc(step, 1)
                    nc.vector.tensor_copy(regroup[:].rearrange("c (a b) -> c a b", b=GROUP),
                                          const.ident[:].rearrange("c (b a) -> c a b", b=GROUP)).then_inc(step, 1)
                    dve.wait_ge(step, 5)
            build_transposes(nc, "mt", const, jobs)
            with nc.Block() as block:
                @block.tensor
                def _(pe):
                    nc.tensor.matmul(s_ps[:], ones_row[0:1, :], s_row[0:1, :], start=True, stop=True).then_inc(mm_done, 1)
                    for i in range(4):
                        nc.tensor.matmul(b_ps[:, i:i + 1], win_raw_t[:, chunk(i, CH)], beta[:],
                                         start=True, stop=True).then_inc(mm_done, 1)
                    nc.tensor.matmul(b_ps[:, 4:5], wp_raw_t[:], beta[:], start=True, stop=True).then_inc(mm_done, 1)

                @block.scalar
                def _(act):
                    nc.scalar.activation(decay[:], a_log[:], ACT.Exp).then_inc(exp_done, 1)

                @block.vector
                def _(dve):
                    n = 5

                    def after_last():
                        dve.wait_ge(step, n)

                    for h in range(HALVES):
                        nc.vector.tensor_copy(wx_t[:, h, RANK * 4:RANK * 5], wx_half_t[:, h, 0:RANK]).then_inc(step, 1)
                        for at in (0, 64, 96):
                            nc.vector.tensor_copy(wx_t[:, h, at:at + 2 * NS], wx_half_t[:, h, RANK:]).then_inc(step, 1)
                    dve.wait_ge(mm_done, 6)
                    nc.vector.tensor_copy(s_col[:], s_ps[:]).then_inc(step, 1)
                    nc.vector.tensor_copy(in_b[:], b_ps[:, 0:4]).then_inc(step, 1)
                    nc.vector.tensor_tensor(bp[:], b_ps[:, 4:5], b_p[:], ALU.add).then_inc(step, 1)
                    n += 8 + 3
                    after_last()
                    nc.vector.tensor_tensor(gs[:], gamma[:], s_col[:], ALU.mult).then_inc(step, 1)
                    nc.vector.tensor_tensor(s_sum[:], s_col[:, 0:1], s_col[:, 1:2], ALU.add).then_inc(step, 1)
                    n += 2
                    after_last()
                    nc.vector.tensor_tensor(out_b[:], s_sum[:], beta[:], ALU.mult).then_inc(step, 1)
                    nc.vector.tensor_scalar(regroup[:], regroup[:], gs[:, 1:2], None, ALU.mult).then_inc(step, 1)
                    n += 2
                    after_last()
                    nc.vector.scalar_tensor_tensor(out=skip_t[:], in0=const.ident[:], scalar=gs[:, 0:1],
                                                   in1=regroup[:], op0=ALU.mult, op1=ALU.add).then_inc(step, 1)
                    dve.wait_ge(exp_done, 1)
                    nc.vector.tensor_scalar(decay[:], decay[:], -1.0, None, ALU.mult).then_inc(step, 1)
                    n += 2
                    after_last()

        normed = [part.sb(f"normed{v}", [CH, TILE]) for v in range(2)]
        xi = [part.sb(f"xi{v}", [CH, HALVES, TAPS - 1 + TILE]) for v in range(2)]
        conv = part.sb("conv", [CH, HALVES, TILE])
        u = [part.sb(f"u{v}", [CH, HALVES, TILE]) for v in range(2)]
        gate = [part.sb(f"gate{v}", [CH, HALVES, TILE]) for v in range(2)]
        bc = [part.sb(f"bc{v}", [CH, TILE], BF16) for v in range(2)]
        rest = part.sb("rest", [CH, TILE])
        dtr = rest[0:RANK, :]
        dt = [part.sb(f"dt{v}", [CH, HALVES, TILE]) for v in range(2)]
        dtu = [part.sb(f"dtu{v}", [CH, HALVES, TILE]) for v in range(2)]
        soft = part.sb("soft", [CH, TILE])
        soft_small = part.sb("soft_small", [CH, TILE])
        soft_log = part.sb("soft_log", [CH, TILE])
        driven = part.sb("driven", [CH, 4, TILE])
        fade = part.sb("fade", [CH, AHEAD, HALVES, TILE])
        state = part.sb("state", [CH, AHEAD, HALVES, TILE])
        seen = part.sb("seen", [CH, AHEAD, HALVES, TILE])
        c_wide = part.sb("c_wide", [CH, AHEAD, TILE])
        carried = [part.sb(f"carried{v}", [CH, HALVES, NS]) for v in range(2)]
        gated = [part.sb(f"gated{v}", [CH, HALVES, TILE]) for v in range(2)]
        again = part.sb("again", [CH, TILE])
        y_ps = [[part.ps(f"y_ps{v}{h}", [CH, TILE]) for h in range(HALVES)] for v in range(2)]
        b_ps = [part.ps(f"b_ps{k}", [CH, TILE]) for k in range(2)]
        c_ps = part.ps("c_ps", [CH, TILE])
        pre_ps = part.ps("pre_ps", [CH, TILE])

        (pre_filled, pre_drained, tail_done, xi_done, tap0_done, conv_step, conv_done, u_done, gate_done,
         split_done, bc_done, dtr_done, cap_done, soft_step, dt_done, dtu_done,
         b_wide, c_bank, c_copied, fade_done, driven_done, scan_done, carried_done, seen_done, y_done,
         skipped_done, gated_done, mixed_done, keep_done, small_done) = sems = part.sems(
            "pre_filled pre_drained tail_done xi_done tap0_done conv_step conv_done u_done gate_done "
            "split_done bc_done dtr_done cap_done soft_step dt_done dtu_done "
            "b_wide c_bank c_copied fade_done driven_done scan_done carried_done seen_done y_done "
            "skipped_done gated_done mixed_done keep_done small_done")
        normed_loaded = part.sems("normed_loaded0 normed_loaded1")
        cleared, mixed_stored, again_loaded = part.sems("cleared mixed_stored again_loaded")
        prime(nc, (*sems, mixed_stored))

        XI, Z, XDBL, DT, OUT = 0, 2, 4, 5, 7
        WAYS = 7

        def fill(it, v, k):
            if it is None:
                return k
            if isinstance(it, int) and it == 0:
                return WAYS + (WAYS if v else 0) + k
            return 3 * WAYS + (it - 1) * (2 * WAYS + 1) + (WAYS + 1 if v else 0) + k

        def over_tiles(eng, tile):
            tile(0, True)
            with eng.Fori(1, NT) as it:
                tile(it, False)

        with nc.Block() as block:
            @block.sync
            def _(sp):
                def load(v, t, r):
                    sp.wait_ge(gate_done, LEAD + 2 * (r - 1))
                    sp.dma_start(normed[v][:], normed_dram[:, chunk(t)]).then_inc(normed_loaded[v], 16)

                def finish(t):
                    sp.wait_ge(mixed_done, LEAD + t + 1)
                    sp.dma_start(mixed_dram[:, chunk(t)], again[:]).then_inc(mixed_stored, 16)
                    sp.wait_ge(mixed_stored, LEAD + 16 * (t + 1))

                def tile(it, first):
                    load(1, it, 2 * it + 1)
                    load(0, it + 1, 2 * it + 2)
                    if not first:
                        finish(it - 1)
                    sp.dma_start(again[:], normed_dram[:, chunk(it)]).then_inc(again_loaded, 16)

                load(0, 0, 0)
                over_tiles(sp, tile)
                finish(NT - 1)

            @block.tensor
            def _(pe):
                def into_pre(it, v, k, pairs, rows=CH):
                    pe.wait_ge(pre_drained, LEAD + fill(it, v, k))
                    for n, (lhs, rhs) in enumerate(pairs):
                        last = nc.tensor.matmul(pre_ps[0:rows, :], lhs, rhs, start=(n == 0), stop=(n == len(pairs) - 1))
                    last.then_inc(pre_filled, 1)

                def prepare(n, it, v, r):
                    b = r % 2 if it is None else 1 - v
                    if n == 0:
                        pe.wait_ge(normed_loaded[b], 16 * ((r // 2 if it is None else (it if b else it + 1)) + 1))
                    if n in (0, 1):
                        into_pre(it, v, XI + n, [(win_t[b][:, chunk(n, CH)], normed[b][:])])
                    if n in (5, 6):
                        into_pre(it, v, Z + n - 5, [(win_t[b][:, chunk(2 + n - 5, CH)], normed[b][:])])
                    if n == 7:
                        pe.wait_ge(u_done, LEAD + 2 * (r + 1))
                        into_pre(it, v, XDBL, [(wx_t[:, h, :], u[b][:, h, :]) for h in range(HALVES)])
                    if n in (9, 11):
                        pe.wait_ge(dtr_done, LEAD + r + 1)
                        h = (n - 9) // 2
                        into_pre(it, v, DT + h, [(wdt_t[:, chunk(h, CH)], dtr)])

                def widen_b(n, b, r):
                    s = r * NS + n
                    if n == 0:
                        pe.wait_ge(bc_done, LEAD + r + 1)
                    pe.wait_ge(driven_done, LEAD + 2 * (s - 1))
                    nc.tensor.matmul(b_ps[n % 2][:], pick[:, n:n + 1].to_broadcast([CH, CH]), bc[b][:], start=True, stop=True).then_inc(b_wide, 1)

                def widen_c(n, b, r):
                    pe.wait_ge(c_copied, LEAD + r * NS + n)
                    nc.tensor.matmul(c_ps[:], pick[:, NS + n:NS + n + 1].to_broadcast([CH, CH]), bc[b][:],
                                     start=True, stop=True).then_inc(c_bank, 1)

                def sum_states(n, v, q):
                    for h in range(HALVES):
                        hs = q * STEPS + 2 * n + h
                        if n == 0:
                            pe.wait_ge(skipped_done, LEAD + 2 * (q - 2) + h + 1)
                        pe.wait_ge(seen_done, LEAD + hs + 1)
                        nc.tensor.matmul(y_ps[v][h][:], const.ident[:], seen[:, n % AHEAD, h, :],
                                         start=(n == 0), stop=(n == NS - 1)).then_inc(y_done, 1)

                for n in range(NS):
                    prepare(n, None, 0, 0)
                def finish(t, it):
                    pe.wait_ge(gated_done, LEAD + 4 * (t + 1))
                    pe.wait_ge(again_loaded, 16 * (t + 1))
                    into_pre(it, 0, OUT, [(wout_t[:, h, :], gated[b][:, h, :]) for b in range(2) for h in range(HALVES)]
                             + [(skip_t[:], again[:])])

                def tile(it, first):
                    for v in range(2):
                        q = 2 * it + v
                        for n in range(NS):
                            prepare(n, it, v, q + 1)
                            if n < NS - 2:
                                widen_b(n + 2, v, q)
                            else:
                                widen_b(n + 2 - NS, 1 - v, q + 1)
                            if n >= 2:
                                sum_states(n - 2, v, q)
                            elif v or not first:
                                sum_states(NS + n - 2, 1 - v, q - 1)
                            if n < NS - 3:
                                widen_c(n + 3, v, q)
                            else:
                                widen_c(n + 3 - NS, 1 - v, q + 1)
                            if n == 14 and v == 0 and not first:
                                finish(it - 1, it)

                for n in range(2):
                    widen_b(n, 0, 0)
                for n in range(3):
                    widen_c(n, 0, 0)
                over_tiles(pe, tile)
                sum_states(NS - 2, 1, 2 * NT - 1)
                sum_states(NS - 1, 1, 2 * NT - 1)
                pe.wait_ge(pre_drained, LEAD + fill(NT, 0, 0))
                pe.wait_ge(gated_done, LEAD + 4 * NT)
                pe.wait_ge(again_loaded, 16 * NT)
                last_pairs = [(wout_t[:, h, :], gated[b][:, h, :]) for b in range(2) for h in range(HALVES)]
                for n, (lhs, rhs) in enumerate(last_pairs + [(skip_t[:], again[:])]):
                    last = nc.tensor.matmul(pre_ps[:], lhs, rhs, start=(n == 0), stop=(n == len(last_pairs)))
                last.then_inc(pre_filled, 1)

            @block.scalar
            def _(act):
                def prepare(n, it, v, r):
                    b = r % 2 if it is None else 1 - v
                    if n in (0, 1):
                        if n == 0:
                            act.wait_ge(tail_done, LEAD + r + 1)
                        act.wait_ge(pre_filled, LEAD + fill(it, v, XI + n) + 1)
                        nc.scalar.activation(xi[b][:, n, TAPS - 1:], pre_ps[:], ACT.Identity, bias=in_b[:, n:n + 1]
                                             ).then_inc(pre_drained, 1)
                        act.wait_ge(pre_drained, LEAD + fill(it, v, XI + n) + 1)
                        act.wait_ge(u_done, LEAD + 2 * (r - 1) + n + 1)
                        nc.scalar.activation(conv[:, n, :], xi[b][:, n, 0:TILE], ACT.Identity,
                                             bias=conv_b[:, n:n + 1], scale=taps[:, n, 0:1]).then_inc(tap0_done, 1)
                    if n in (5, 6):
                        h = n - 5
                        act.wait_ge(pre_filled, LEAD + fill(it, v, Z + h) + 1)
                        act.wait_ge(gated_done, LEAD + 2 * (r - 1))
                        if n == 5:
                            nc.scalar.activation(gate[b][:, 0, :], pre_ps[:], ACT.Identity, bias=in_b[:, 2:3]
                                                 ).then_inc(pre_drained, 1)
                            act.wait_ge(pre_drained, LEAD + fill(it, v, Z) + 1)
                            return
                        act.wait_ge(skipped_done, LEAD + 2 * (r - 1))
                        act.wait_ge(dtu_done, LEAD + 2 * (r - 1))
                        act.wait_ge(conv_done, LEAD + 2 * r + 2)
                        nc.scalar.activation(gate[b][:, 1, :], pre_ps[:], ACT.Silu, bias=in_b[:, 3:4]
                                             ).then_inc(pre_drained, 1)
                        for h in range(HALVES):
                            nc.scalar.activation(u[b][:, h, :], conv[:, h, :], ACT.Silu).then_inc(u_done, 1)
                        nc.scalar.activation(gate[b][:, 0, :], gate[b][:, 0, :], ACT.Silu).then_inc(gate_done, 1)
                        act.wait_ge(pre_drained, LEAD + fill(it, v, Z + 1) + 1)
                        act.sem_inc(gate_done, 1)
                        if it is not None:
                            nc.scalar.preload_act_table_set("natural_log_exp_and_others")
                    if n == 7:
                        act.wait_ge(pre_filled, LEAD + fill(it, v, XDBL) + 1)
                        act.wait_ge(dt_done, LEAD + 2 * r)
                        nc.scalar.activation(dtr, pre_ps[4 * RANK:5 * RANK, :], ACT.Copy).then_inc(dtr_done, 1)
                        act.wait_ge(c_bank, LEAD + NS * (r - 1))
                        nc.scalar.activation(bc[b][:], pre_ps[:], ACT.Copy).then_inc(split_done, 1)
                    if n in (9, 11):
                        h = (n - 9) // 2
                        act.wait_ge(cap_done, LEAD + 2 * r + h + 1)
                        nc.scalar.activation(soft[:], soft[:], ACT.Exp).then_inc(soft_step, 1)
                        act.wait_ge(soft_step, LEAD + 3 * (2 * r + h) + 1)
                        nc.scalar.activation(soft_small[:], soft[:], ACT.Exp, scale=-0.5).then_inc(soft_step, 1)
                        nc.scalar.activation(soft_log[:], soft[:], ACT.Ln, bias=almost_one[:, 0:1]).then_inc(soft_step, 1)

                def decays(n, v, q):
                    for h in range(HALVES):
                        hs = q * STEPS + 2 * n + h
                        if n == 0:
                            act.wait_ge(dt_done, LEAD + 2 * q + h + 1)
                        act.wait_ge(scan_done, LEAD + hs - (2 * AHEAD - 1))
                        nc.scalar.activation(fade[:, n % AHEAD, h, :], dt[v][:, h, :], ACT.Exp, scale=decay[:, h, n:n + 1]
                                             ).then_inc(fade_done, 1)

                def copy_c(n, q):
                    s = q * NS + n
                    act.wait_ge(c_bank, LEAD + s + 1)
                    act.wait_ge(seen_done, LEAD + 2 * (s - AHEAD + 1))
                    nc.scalar.activation(c_wide[:, n % AHEAD, :], c_ps[:], ACT.Copy).then_inc(c_copied, 1)

                def carry(n, v, q):
                    act.wait_ge(scan_done, LEAD + q * STEPS + 2 * n + 2)
                    if v == 0 and n == 0:
                        act.wait_ge(keep_done, LEAD + (q // 2 if isinstance(q, int) else turn[0]) + 1)
                    nc.scalar.activation(carried[v][:, :, n:n + 1], state[:, n % AHEAD, :, TILE - 1:TILE],
                                         ACT.Copy, scale=keep_now[:, 0:1]).then_inc(carried_done, 1)

                def finish(t, it):
                    act.wait_ge(pre_filled, LEAD + fill(it, 0, OUT) + 1)
                    act.wait_ge(mixed_stored, LEAD + 16 * t)
                    nc.scalar.activation(again[:], pre_ps[:], ACT.Identity, bias=out_b[:, 0:1]).then_inc(pre_drained, 1)
                    act.wait_ge(pre_drained, LEAD + fill(it, 0, OUT) + 1)
                    act.sem_inc(mixed_done, 1)

                turn = [None]

                def tile(it, first):
                    turn[0] = it
                    for v in range(2):
                        q = 2 * it + v
                        for n in range(NS):
                            if n < NS - 3:
                                decays(n + 3, v, q)
                            else:
                                decays(n + 3 - NS, 1 - v, q + 1)
                            if n < NS - 2:
                                copy_c(n + 2, q)
                            else:
                                copy_c(n + 2 - NS, q + 1)
                            if n >= 2:
                                carry(n - 2, v, q)
                            elif v or not first:
                                carry(NS + n - 2, 1 - v, q - 1)
                            prepare(n, it, v, q + 1)
                            if n == 14 and v == 0 and not first:
                                finish(it - 1, it)

                for n in range(NS):
                    prepare(n, None, 0, 0)
                nc.scalar.preload_act_table_set("natural_log_exp_and_others")
                for n in range(3):
                    decays(n, 0, 0)
                for n in range(2):
                    copy_c(n, 0)
                over_tiles(act, tile)
                for n in (NS - 2, NS - 1):
                    carry(n, 1, 2 * NT - 1)
                act.wait_ge(pre_filled, LEAD + fill(NT, 0, 0) + 1)
                act.wait_ge(mixed_stored, LEAD + 16 * (NT - 1))
                nc.scalar.activation(again[:], pre_ps[:], ACT.Identity, bias=out_b[:, 0:1]).then_inc(mixed_done, 1)

            @block.vector
            def _(dve):
                def prepare(n, it, v, r):
                    b = r % 2 if it is None else 1 - v
                    if n == 0 and it is not None:
                        dve.wait_ge(conv_done, LEAD + 2 * r)
                        t = it if b else it + 1
                        nc.vector.tensor_scalar(xi[b][:, :, 0:TAPS - 1], xi[b][:, :, TILE:TILE + TAPS - 1],
                                                keep[:, bass.ds(t, 1)], None, ALU.mult).then_inc(tail_done, 1)
                    if n in (2, 3):
                        h = n - 2
                        dve.wait_ge(tap0_done, LEAD + 2 * r + h + 1)
                        for k in range(1, TAPS):
                            if k > 1:
                                dve.wait_ge(conv_step, LEAD + (2 * r + h) * (TAPS - 2) + k - 1)
                            done = conv_step if k < TAPS - 1 else conv_done
                            nc.vector.scalar_tensor_tensor(
                                out=conv[:, h, :], in0=xi[b][:, h, k:k + TILE], scalar=taps[:, h, k:k + 1],
                                in1=conv[:, h, :], op0=ALU.mult, op1=ALU.add).then_inc(done, 1)
                    if n == 8:
                        dve.wait_ge(split_done, LEAD + 3 * r + 1)
                        nc.vector.tensor_tensor(rest[64:128, :], pre_ps[64:128, :], bc[b][64:128, :], ALU.subtract
                                                ).then_inc(pre_drained, 1)
                        dve.wait_ge(pre_drained, LEAD + fill(it, v, XDBL) + 1)
                        nc.vector.tensor_copy(bc[b][64:128, :], rest[64:128, :]).then_inc(split_done, 1)
                        dve.wait_ge(split_done, LEAD + 3 * r + 2)
                        nc.vector.tensor_tensor(bc[b][96:128, :], rest[96:128, :], bc[b][96:128, :], ALU.subtract
                                                ).then_inc(split_done, 1)
                        dve.wait_ge(split_done, LEAD + 3 * r + 3)
                        dve.sem_inc(bc_done, 1)
                    if n in (9, 11):
                        h = (n - 9) // 2
                        dve.wait_ge(pre_filled, LEAD + fill(it, v, DT + h) + 1)
                        dve.wait_ge(dt_done, LEAD + 2 * r + h)
                        nc.vector.tensor_scalar(soft[:], pre_ps[:], dt_b[:, h:h + 1], CAP, ALU.add, ALU.min
                                                ).then_inc(cap_done, 1)
                    if n in (10, 12):
                        h = (n - 10) // 2
                        dve.wait_ge(soft_step, LEAD + 3 * (2 * r + h) + 3)
                        dve.wait_ge(fade_done, LEAD + STEPS * (r - 1))
                        dve.wait_ge(dtu_done, LEAD + 2 * (r - 1))
                        nc.vector.scalar_tensor_tensor(out=dt[b][:, h, :], in0=pre_ps[:], scalar=dt_b[:, h:h + 1],
                                                       in1=soft_log[:], op0=ALU.add, op1=ALU.max).then_inc(pre_drained, 1)
                        dve.wait_ge(pre_drained, LEAD + fill(it, v, DT + h) + 1)
                        dve.wait_ge(small_done, LEAD + 2 * r + h + 1)
                        nc.vector.tensor_tensor(dt[b][:, h, :], dt[b][:, h, :], soft_small[:], ALU.max
                                                ).then_inc(dt_done, 1)

                def scan(n, v, q):
                    s = q * NS + n
                    if n == 0:
                        dve.wait_ge(dtu_done, LEAD + 2 * (q + 1))
                    dve.wait_ge(b_wide, LEAD + s + 1)
                    for h in range(HALVES):
                        hs = q * STEPS + 2 * n + h
                        dve.wait_ge(scan_done, LEAD + hs - 3)
                        nc.vector.tensor_tensor(driven[:, (2 * n + h) % 4, :], dtu[v][:, h, :], b_ps[n % 2][:], ALU.mult
                                                ).then_inc(driven_done, 1)
                    for h in range(HALVES):
                        hs = q * STEPS + 2 * n + h
                        dve.wait_ge(fade_done, LEAD + hs + 1)
                        dve.wait_ge(driven_done, LEAD + hs + 1)
                        dve.wait_ge(seen_done, LEAD + hs - (2 * AHEAD - 1))
                        dve.wait_ge(carried_done, LEAD + s - (AHEAD - 1))
                        nc.vector.tensor_tensor_scan(state[:, n % AHEAD, h, :], fade[:, n % AHEAD, h, :],
                                                     driven[:, (2 * n + h) % 4, :], carried[v][:, h, n:n + 1],
                                                     ALU.mult, ALU.add).then_inc(scan_done, 1)

                for v in range(2):
                    nc.vector.memset(carried[v][:], 0.0).then_inc(cleared, 1)
                    nc.vector.memset(xi[v][:], 0.0).then_inc(cleared, 1)
                dve.wait_ge(cleared, 4)
                dve.sem_inc(tail_done, 1)
                for n in range(NS):
                    prepare(n, None, 0, 0)

                def finish(v, q, t):
                    for h in range(HALVES):
                        dve.wait_ge(y_done, LEAD + q * STEPS + STEPS)
                        dve.wait_ge(mixed_done, LEAD + t)
                        nc.vector.scalar_tensor_tensor(out=gated[v][:, h, :], in0=u[v][:, h, :],
                                                       scalar=d_skip[:, h:h + 1], in1=y_ps[v][h][:],
                                                       op0=ALU.mult, op1=ALU.add).then_inc(skipped_done, 1)

                def tile(it, first):
                    for v in range(2):
                        q = 2 * it + v
                        for n in range(NS):
                            scan(n, v, q)
                            if v == 0 and n == 1:
                                dve.wait_ge(carried_done, LEAD + 2 * NS * it)
                                nc.vector.tensor_scalar(keep_now[:], keep[:, bass.ds(it + 1, 1)], 1.0, None, ALU.mult
                                                        ).then_inc(keep_done, 1)
                            prepare(n, it, v, q + 1)
                            if n == 2 and (v or not first):
                                finish(1 - v, q - 1, it if v else it - 1)

                over_tiles(dve, tile)
                finish(1, 2 * NT - 1, NT - 1)

            @block.gpsimd
            def _(pool):
                def prepare(n, it, v, r):
                    b = r % 2 if it is None else 1 - v
                    if n in (9, 11):
                        h = (n - 9) // 2
                        pool.wait_ge(soft_step, LEAD + 3 * (2 * r + h) + 3)
                        nc.gpsimd.tensor_tensor(soft_small[:], soft_small[:], soft[:], ALU.mult).then_inc(small_done, 1)
                    if n in (11, 13):
                        h = (n - 11) // 2
                        pool.wait_ge(dt_done, LEAD + 2 * r + h + 1)
                        pool.wait_ge(driven_done, LEAD + STEPS * (r - 1))
                        nc.gpsimd.tensor_tensor(dtu[b][:, h, :], dt[b][:, h, :], u[b][:, h, :], ALU.mult
                                                ).then_inc(dtu_done, 1)

                for n in range(NS):
                    prepare(n, None, 0, 0)

                def finish(v, q):
                    for h in range(HALVES):
                        pool.wait_ge(skipped_done, LEAD + 2 * q + h + 1)
                        pool.wait_ge(gate_done, LEAD + 2 * q + 2)
                        nc.gpsimd.tensor_tensor(gated[v][:, h, :], gated[v][:, h, :], gate[v][:, h, :], ALU.mult
                                                ).then_inc(gated_done, 1)

                def tile(it, first):
                    for v in range(2):
                        q = 2 * it + v
                        for n in range(NS):
                            pool.wait_ge(c_copied, LEAD + q * NS + n + 1)
                            for h in range(HALVES):
                                hs = q * STEPS + 2 * n + h
                                pool.wait_ge(scan_done, LEAD + hs + 1)
                                pool.wait_ge(y_done, LEAD + hs - (2 * AHEAD - 1))
                                nc.gpsimd.tensor_tensor(seen[:, n % AHEAD, h, :], state[:, n % AHEAD, h, :],
                                                        c_wide[:, n % AHEAD, :], ALU.mult).then_inc(seen_done, 1)
                            prepare(n, it, v, q + 1)
                            if n == 3 and (v or not first):
                                finish(1 - v, q - 1)

                over_tiles(pool, tile)
                finish(1, 2 * NT - 1)


def layer0(nc, const, w, normed_dram, mixed_dram):
    with Part(nc, "l0") as part:
        scale = part.sb("scale", [CH, BATCH])
        shift = part.sb("shift", [CH, BATCH])
        wp_t = part.sb("wp_t", [CH, CH])
        bp = part.sb("bp", [CH, 1])
        build_group_norm(nc, const, "gn0", scale, shift)
        build_layer_norm(nc, const, "ln0", normed_dram, affine=(scale, shift), extra=True)
        build_mamba(nc, const, w, normed_dram, mixed_dram, wp_t, bp)
        build_layer_norm(nc, const, "ln1", None, src=mixed_dram, project=(wp_t, bp))


def layer1(nc, const, w):
    GROUPS, K = 4, 3
    CPG, NK = CH // GROUPS, K * K
    FILTERS = GROUPS * NK
    MID = 64
    WIDE = IMG + 2
    ROWS = TILE // IMG
    with Part(nc, "l1") as part:
        scale = part.sb("scale", [CH, BATCH])
        shift = part.sb("shift", [CH, BATCH])
        kg_t = part.sb("kg_t", [CH, NK, MID + FILTERS])
        kg_b = part.sb("kg_b", [MID + FILTERS, 1])
        pw_t = part.sb("pw_t", [CH, CH])
        pw_b = part.sb("pw_b", [CH, 1])
        spread = part.sb("spread", [CH, NK, CH], BF16)
        padded = [part.sb(f"padded{k}", [CH, WIDE, WIDE]) for k in range(2)]
        build_group_norm(nc, const, "gn1", scale, shift)
        with Part(nc, "l1w") as pre:
            kg = pre.sb("kg", [FILTERS, CPG, NK])
            pw = pre.sb("pw", [CH, CPG])
            spread_f = pre.sb("spread_f", [CH, NK * CH])
            wide_t = pre.ps("wide_t", [CH, TILE])
            loaded, made, transposed, copied = pre.sems("loaded made transposed copied")
            with nc.Block() as block:
                @block.sync
                def _(sp):
                    with nc.allow_non_contiguous_dma("small weights"):
                        sp.wait_ge(made, 6)
                        n = 0
                        for dst, src in ((kg[:], w["w_kg"].rearrange("o i a b -> o i (a b)")),
                                         (kg_b[0:FILTERS, :], column(w["b_kg"])),
                                         (kg_b[MID:MID + FILTERS, :], column(w["b_kg"])),
                                         (pw_b[:], column(w["b_pw"]))):
                            sp.dma_start(dst, src).then_inc(loaded, 16)
                            n += 1
                        for g in range(GROUPS):
                            sp.dma_start(pw_t[g * CPG:(g + 1) * CPG, g * CPG:(g + 1) * CPG],
                                         w["w_pw"][g * CPG:(g + 1) * CPG].rearrange("o i a b -> i (o a b)")
                                         ).then_inc(loaded, 16)
                            n += 1
                        sp.wait_ge(loaded, 16 * n)

                @block.gpsimd
                def _(pool):
                    nc.gpsimd.memset(kg_t[:], 0.0).then_inc(made, 1)
                    nc.gpsimd.memset(pw_t[:], 0.0).then_inc(made, 1)
                    nc.gpsimd.memset(kg_b[:], 0.0).then_inc(made, 1)
                    nc.gpsimd.memset(padded[0][:], 0.0).then_inc(made, 1)
                    nc.gpsimd.memset(padded[1][:], 0.0).then_inc(made, 1)
                    nc.gpsimd.memset(spread[:], 0.0).then_inc(made, 1)
                    pool.wait_ge(made, 6)
                    v = spread[:].rearrange("p k (g c) -> p k g c", g=GROUPS)
                    for n, base in enumerate((0, MID)):
                        nc.gpsimd.affine_select(out=v, in_=v, compare_op=ALU.not_equal, fill=1.0, base=-base,
                                                pattern=[[-1, NK], [-NK, GROUPS], [0, CPG]],
                                                channel_multiplier=1).then_inc(made, 1)
                        pool.wait_ge(made, 7 + n)

                @block.tensor
                def _(pe):
                    pe.wait_ge(loaded, 16 * 8)
                    for k in range(NK):
                        if k >= 1:
                            pe.wait_ge(copied, 2 * GROUPS * k)
                        nc.tensor.transpose(wide_t[0:CPG, 0:FILTERS], kg[:, :, k],
                                            const.ident[0:FILTERS, 0:FILTERS]).then_inc(transposed, 1)

                @block.vector
                def _(dve):
                    dve.wait_ge(made, 8)
                    for k in range(NK):
                        dve.wait_ge(transposed, k + 1)
                        for g in range(GROUPS):
                            for at in (0, MID):
                                cols = slice(at + g * NK, at + (g + 1) * NK)
                                nc.vector.tensor_copy(kg_t[g * CPG:(g + 1) * CPG, k, cols],
                                                      wide_t[0:CPG, g * NK:(g + 1) * NK]).then_inc(copied, 1)

        hi_mid = part.sb("hi_mid", [CH, 2, TILE], BF16)
        rest = part.sb("rest", [CH, TILE])
        mid = part.sb("mid", [FILTERS, TILE], BF16)
        low = part.sb("low", [FILTERS, 2, TILE], BF16)
        weighted = part.sb("weighted", [CH, 4, TILE])
        total = part.sb("total", [CH, 2, TILE])
        filt_ps = [part.ps(f"filt_ps{k}", [CH, TILE]) for k in range(2)]
        wide_ps = [part.ps(f"wide_ps{k}", [CH, TILE]) for k in range(3)]
        out_ps = [part.ps(f"out_ps{k}", [CH, TILE]) for k in range(2)]
        (image_done, filters_done, hi_done, rest_done, mid_done, low_done, split_step, wide_done, weighted_done,
         total_done, out_done, added) = sems = part.sems(
            "image_done filters_done hi_done rest_done mid_done low_done split_step wide_done weighted_done "
            "total_done out_done added")
        prime(nc, sems)

        def window(image, row, k):
            return image[:, bass.ds(row + k // K, ROWS), k % K:k % K + IMG]

        def over_tiles(eng, first, body):
            with eng.Fori(0, BATCH // 2) as pair:
                for m in range(2):
                    b = 2 * pair + m
                    first(b, m)
                    with eng.Fori(0, TPB // 2) as jj:
                        for k in range(2):
                            j = 2 * jj + k
                            body(b * TPB + j, j, m, k, b)

        with nc.Block() as block:
            @block.scalar
            def _(act):
                def tile(t, j, m, k, b):
                    act.wait_ge(filters_done, LEAD + t + 1)
                    act.wait_ge(wide_done, LEAD + NK * (t - 1))
                    nc.scalar.activation(hi_mid[0:MID + FILTERS, k, :], filt_ps[k][0:MID + FILTERS, :], ACT.Identity,
                                         bias=kg_b[:, 0:1]).then_inc(hi_done, 1)

                over_tiles(act, lambda b, m: None, tile)

            @block.vector
            def _(dve):
                def image(b, m):
                    dve.wait_ge(filters_done, LEAD + TPB * (b - 1))
                    nc.vector.tensor_scalar(padded[m][:, 1:1 + IMG, 1:1 + IMG],
                                            const.x[:, bass.ds(b * TOK, TOK)].rearrange("c (h w) -> c h w", h=IMG),
                                            scale[:, bass.ds(b, 1)], shift[:, bass.ds(b, 1)], ALU.mult, ALU.add
                                            ).then_inc(image_done, 1)

                def tile(t, j, m, k, b):
                    dve.wait_ge(image_done, LEAD + b + 1)
                    dve.wait_ge(hi_done, LEAD + t + 1)
                    rows = MID + FILTERS
                    nc.vector.scalar_tensor_tensor(out=rest[0:rows, :], in0=filt_ps[k][0:rows, :], scalar=kg_b[:, 0:1],
                                                   in1=hi_mid[0:rows, k, :], op0=ALU.add, op1=ALU.subtract
                                                   ).then_inc(split_step, 1)
                    dve.wait_ge(split_step, LEAD + 3 * t + 1)
                    dve.sem_inc(rest_done, 1)
                    nc.vector.tensor_copy(mid[:], rest[0:FILTERS, :]).then_inc(split_step, 1)
                    nc.vector.tensor_copy(hi_mid[MID:rows, k, :], rest[MID:rows, :]).then_inc(mid_done, 1)
                    dve.wait_ge(split_step, LEAD + 3 * t + 2)
                    dve.wait_ge(wide_done, LEAD + NK * (t - 1))
                    nc.vector.tensor_tensor(low[:, k, :], rest[0:FILTERS, :], mid[:], ALU.subtract).then_inc(split_step, 1)
                    dve.wait_ge(split_step, LEAD + 3 * t + 3)
                    dve.wait_ge(mid_done, LEAD + t + 1)
                    dve.sem_inc(low_done, 1)
                    for n in range(NK):
                        w_at = NK * t + n
                        slot = (NK * k + n) % 4
                        dve.wait_ge(wide_done, LEAD + w_at + 1)
                        if n == 0:
                            dve.wait_ge(total_done, LEAD + (NK - 1) * t)
                        if n >= 3:
                            dve.wait_ge(total_done, LEAD + (NK - 1) * t + n - 2)
                        nc.vector.tensor_tensor(
                            weighted[:, slot, :].rearrange("c (h w) -> c h w", h=ROWS), window(padded[m], j * ROWS, n),
                            wide_ps[(NK * k + n) % 3][:].rearrange("c (h w) -> c h w", h=ROWS), ALU.mult
                            ).then_inc(weighted_done, 1)
                    dve.wait_ge(out_done, LEAD + t + 1)
                    nc.vector.scalar_tensor_tensor(out=const.x[:, chunk(t)], in0=out_ps[k][:], scalar=pw_b[:, 0:1],
                                                   in1=const.x[:, chunk(t)], op0=ALU.add, op1=ALU.add
                                                   ).then_inc(added, 1)

                over_tiles(dve, image, tile)

            @block.gpsimd
            def _(pool):
                def tile(t, j, m, k, b):
                    pool.wait_ge(out_done, LEAD + t - 1)
                    for n in range(1, NK):
                        pool.wait_ge(weighted_done, LEAD + NK * t + n + 1)
                        first = weighted[:, NK * k % 4, :] if n == 1 else total[:, k, :]
                        if n > 1:
                            pool.wait_ge(total_done, LEAD + (NK - 1) * t + n - 1)
                        nc.gpsimd.tensor_tensor(total[:, k, :], first, weighted[:, (NK * k + n) % 4, :], ALU.add
                                                ).then_inc(total_done, 1)

                over_tiles(pool, lambda b, m: None, tile)

            @block.tensor
            def _(pe):
                def tile(t, j, m, k, b):
                    pe.wait_ge(image_done, LEAD + b + 1)
                    pe.wait_ge(rest_done, LEAD + t - 1)
                    for n in range(NK):
                        last = nc.tensor.matmul(filt_ps[k][0:MID + FILTERS, :], kg_t[:, n, :],
                                                window(padded[m], j * ROWS, n), start=(n == 0), stop=(n == NK - 1))
                    last.then_inc(filters_done, 1)
                    pe.wait_ge(low_done, LEAD + t + 1)
                    for n in range(NK):
                        pe.wait_ge(weighted_done, LEAD + NK * t + n - 2)
                        bank = wide_ps[(NK * k + n) % 3]
                        nc.tensor.matmul(bank[:], spread[0:MID + FILTERS, n, :], hi_mid[0:MID + FILTERS, k, :],
                                         start=True, stop=False)
                        nc.tensor.matmul(bank[:], spread[0:FILTERS, n, :], low[:, k, :], start=False, stop=True
                                         ).then_inc(wide_done, 1)
                    pe.wait_ge(total_done, LEAD + (NK - 1) * (t + 1))
                    pe.wait_ge(added, LEAD + t - 1)
                    nc.tensor.matmul(out_ps[k][:], pw_t[:], total[:, k, :], start=True, stop=True).then_inc(out_done, 1)

                over_tiles(pe, lambda b, m: None, tile)


def build_attention(nc, const, normed_dram):
    KEYS = TOK // CH
    DIAG = TOK - CH
    with Part(nc, "at") as part:
        q_t = part.sb("q_t", [CH, TOK])
        q = part.sb("q", [CH, KEYS, CH])
        strip = part.sb("strip", [CH, TOK - TILE + DIAG + TILE], BF16)
        weight = part.sb("weight", [CH, 4, TILE])
        total = part.sb("total", [CH, TILE])
        share = part.sb("share", [CH, TILE])
        ones = part.sb("ones", [CH, CH])
        score_ps = [part.ps(f"score_ps{k}", [CH, TILE]) for k in range(3)]
        out_ps = part.ps("out_ps", [CH, TILE])
        total_ps = part.ps("total_ps", [CH, TILE])
        turn_ps = [part.ps(f"turn_ps{k}", [CH, TILE]) for k in range(2)]
        (q_done, turned, q_copied, scores_done, exp_done, masked_done, total_done, summed, values_done,
         share_done, scaled, added) = sems = part.sems(
            "q_done turned q_copied scores_done exp_done masked_done total_done summed values_done "
            "share_done scaled added")
        q_loaded, made = part.sems("q_loaded made")
        prime(nc, sems)
        with nc.Block() as block:
            @block.gpsimd
            def _(pool):
                nc.gpsimd.memset(ones[:], 1.0).then_inc(made, 1)
                nc.gpsimd.memset(strip[:], 1.0).then_inc(made, 1)
                pool.wait_ge(made, 2)
                nc.gpsimd.affine_select(out=strip[:], in_=strip[:], compare_op=ALU.not_equal, fill=0.0, base=-DIAG,
                                        pattern=[[1, strip.shape[1]]], channel_multiplier=-1).then_inc(made, 1)

            @block.sync
            def _(sp):
                with sp.Fori(0, BATCH) as b:
                    sp.wait_ge(summed, LEAD + TPB * b)
                    sp.dma_start(q_t[:], normed_dram[:, bass.ds(b * TOK, TOK)]).then_inc(q_loaded, 16)

            @block.tensor
            def _(pe):
                pe.wait_ge(made, 3)
                with pe.Fori(0, BATCH) as b:
                    pe.wait_ge(q_loaded, 16 * (b + 1))
                    for n in range(TPB):
                        pe.wait_ge(q_copied, LEAD + TPB * b + n - 1)
                        for k in range(4):
                            last = nc.tensor.transpose(turn_ps[n % 2][:, chunk(k, CH)], q_t[:, chunk(4 * n + k, CH)],
                                                       const.ident[:])
                        last.then_inc(turned, 1)
                    with pe.Fori(0, TPB) as i:
                        c = b * TPB + i
                        pe.wait_ge(q_copied, LEAD + TPB * (b + 1))

                        def scores(m):
                            g = c * KEYS + m
                            pe.wait_ge(exp_done, LEAD + g - 2)
                            nc.tensor.matmul(score_ps[m % 3][:] , q_t[:, chunk(m, CH)], q_t[:, chunk(i)],
                                             start=True, stop=True).then_inc(scores_done, 1)

                        pe.wait_ge(exp_done, LEAD + c * KEYS)
                        scores(0)
                        scores(1)
                        for m in range(KEYS):
                            if m + 2 < KEYS:
                                scores(m + 2)
                            pe.wait_ge(masked_done, LEAD + c * KEYS + m + 1)
                            if m == 0:
                                pe.wait_ge(scaled, LEAD + c)
                            nc.tensor.matmul(out_ps[:], q[:, m, :], weight[:, m % 4, :],
                                             start=(m == 0), stop=(m == KEYS - 1)).then_inc(values_done, 1)
                        pe.wait_ge(total_done, LEAD + (KEYS - 1) * (c + 1))
                        pe.wait_ge(share_done, LEAD + c)
                        nc.tensor.matmul(total_ps[:], ones[:], total[:], start=True, stop=True).then_inc(summed, 1)

            @block.scalar
            def _(act):
                with act.Fori(0, BATCH * TPB) as c:
                    for m in range(KEYS):
                        g = c * KEYS + m
                        act.wait_ge(scores_done, LEAD + g + 1)
                        act.wait_ge(values_done, LEAD + g - 3)
                        act.wait_ge(total_done, LEAD + (KEYS - 1) * c + (max(m - 4, 1) if m >= 4 else 0))
                        nc.scalar.activation(weight[:, m % 4, :], score_ps[m % 3][:], ACT.Exp,
                                             scale=1.0 / math.sqrt(CH)).then_inc(exp_done, 1)

            @block.vector
            def _(dve):
                dve.wait_ge(made, 3)
                with dve.Fori(0, BATCH) as b:
                    for n in range(TPB):
                        dve.wait_ge(turned, LEAD + TPB * b + n + 1)
                        nc.vector.tensor_copy(q[:, 4 * n:4 * n + 4, :].rearrange("p a b -> p (a b)"), turn_ps[n % 2][:]
                                              ).then_inc(q_copied, 1)
                    with dve.Fori(0, TPB) as i:
                        c = b * TPB + i

                        def add(m):
                            dve.wait_ge(masked_done, LEAD + c * KEYS + m + 1)
                            if m == 1:
                                dve.wait_ge(summed, LEAD + c)
                            else:
                                dve.wait_ge(total_done, LEAD + (KEYS - 1) * c + m - 1)
                            first = weight[:, 0, :] if m == 1 else total[:]
                            nc.vector.tensor_tensor(total[:], first, weight[:, m % 4, :], ALU.add).then_inc(total_done, 1)

                        for m in range(KEYS):
                            dve.wait_ge(exp_done, LEAD + c * KEYS + m + 1)
                            nc.vector.tensor_tensor(weight[:, m % 4, :], weight[:, m % 4, :],
                                                    strip[:, bass.ds(i * TILE + DIAG - m * CH, TILE)], ALU.mult
                                                    ).then_inc(masked_done, 1)
                            if m >= 2:
                                add(m - 1)
                        add(KEYS - 1)
                        dve.wait_ge(summed, LEAD + c + 1)
                        nc.vector.reciprocal(share[:], total_ps[:]).then_inc(share_done, 1)
                        dve.wait_ge(share_done, LEAD + c + 1)
                        dve.wait_ge(values_done, LEAD + KEYS * (c + 1))
                        nc.vector.tensor_tensor(share[:], out_ps[:], share[:], ALU.mult).then_inc(scaled, 1)
                        dve.wait_ge(scaled, LEAD + c + 1)
                        nc.vector.tensor_tensor(const.x[:, chunk(c)], const.x[:, chunk(c)], share[:], ALU.add
                                                ).then_inc(added, 1)
                        dve.wait_ge(added, LEAD + c + 1)


def attention(nc, const, normed_dram):
    build_layer_norm(nc, const, "ln2", normed_dram)
    build_attention(nc, const, normed_dram)


def experts(nc, const, name, w, normed_dram):
    E, K, H, O = 64, 8, 512, CH
    JT = H // CH
    PAIRS = BATCH // 2
    GROUP, QUAD = 16, 4
    QUADS = GROUP // QUAD
    build_layer_norm(nc, const, name + "n", normed_dram)
    with Part(nc, name) as part:
        gate_t = part.sb("gate_t", [CH, E])
        gate_b = part.sb("gate_b", [CH, 1])
        b1_t = part.sb("b1_t", [CH, JT, E])
        b2_t = part.sb("b2_t", [CH, E])
        token_weight = part.sb("token_weight", [CH, PAIRS, TOK])
        pooled_t = part.sb("pooled_t", [CH, E, BATCH])
        out_t = part.sb("out_t", [CH, PAIRS, 2, E])
        with Part(nc, name + "g") as pre:
            gate = pre.sb("gate", [E, CH])
            b1 = pre.sb("b1", [E, H])
            b2 = pre.sb("b2", [E, O])
            loaded, = pre.sems("loaded")
            with nc.Block() as block:
                @block.sync
                def _(sp):
                    with nc.allow_non_contiguous_dma("small weights"):
                        for dst, src in ((gate[:], w["gate_w"]), (gate_b[0:E, :], column(w["gate_b"])),
                                         (gate_b[E:2 * E, :], column(w["gate_b"])),
                                         (b1[:], w["weight1"][:, CH, :]), (b2[:], w["weight2"][:, H, :])):
                            sp.dma_start(dst, src).then_inc(loaded, 16)
                        sp.wait_ge(loaded, 16 * 5)
            build_transposes(nc, name + "t", const, [(gate_t[:], gate[:], None), (b2_t[:], b2[:], None)]
                             + [(b1_t[:, t, :], b1[:, t::JT], None) for t in range(JT)])
        with Part(nc, name + "p") as pre:
            xh = [pre.sb(f"xh{k}", [CH, TOK]) for k in range(2)]
            logit = pre.sb("logit", [CH, TOK])
            top = pre.sb("top", [CH, K])
            top_exp = pre.sb("top_exp", [CH, K])
            minus_max = pre.sb("minus_max", [CH, 1])
            total = pre.sb("total", [CH, 1])
            share = pre.sb("share", [CH, 1])
            x_tok = pre.sb("x_tok", [CH, 2, 2, CH])
            w_tok = pre.sb("w_tok", [CH, 2, CH])
            logit_ps = [pre.ps(f"logit_ps{k}", [CH, TILE]) for k in range(2)]
            turn_ps = [pre.ps(f"turn_ps{k}", [CH, 3, CH]) for k in range(2)]
            pooled_ps = [pre.ps(f"pooled_ps{k}", [CH, E]) for k in range(2)]
            (logits_done, logit_copied, top_done, max_done, exp_done, top_exp_done, share_done, left_done,
             picked_done, weight_done, turned, turn_copied, x_copied, pooled, pooled_copied) = sems = pre.sems(
                "logits_done logit_copied top_done max_done exp_done top_exp_done share_done left_done "
                "picked_done weight_done turned turn_copied x_copied pooled pooled_copied")
            xh_loaded = pre.sems("xh_loaded0 xh_loaded1")
            prime(nc, sems)
            SUBS = TOK // CH
            with nc.Block() as block:
                @block.sync
                def _(sp):
                    for pair in range(PAIRS):
                        for k in range(2):
                            sp.wait_ge(pooled, LEAD + SUBS * pair)
                            sp.dma_start(xh[k][:], normed_dram[:, chunk(2 * pair + k, TOK)]).then_inc(xh_loaded[k], 16)

                @block.tensor
                def _(pe):
                    for pair in range(PAIRS):
                        for k in range(2):
                            at = slice(E * k, E * (k + 1))
                            pe.wait_ge(xh_loaded[k], 16 * (pair + 1))
                            for i in range(TPB):
                                n = (pair * 2 + k) * TPB + i
                                pe.wait_ge(logit_copied, LEAD + n - 1)
                                nc.tensor.matmul(logit_ps[i % 2][at, :], gate_t[:], xh[k][:, chunk(i)],
                                                 start=True, stop=True).then_inc(logits_done, 1)
                        pe.wait_ge(weight_done, LEAD + pair + 1)
                        pe.wait_ge(pooled_copied, LEAD + 2 * pair)

                        def turn(i):
                            pe.wait_ge(turn_copied, LEAD + pair * SUBS + i - 1)
                            pe.wait_ge(x_copied, LEAD + pair * SUBS + i - 1)
                            for k in range(2):
                                nc.tensor.transpose(turn_ps[i % 2][:, k, :], xh[k][:, chunk(i, CH)], const.ident[:])
                            nc.tensor.transpose(turn_ps[i % 2][:, 2, :], token_weight[:, pair, chunk(i, CH)],
                                                const.ident[:]).then_inc(turned, 1)

                        turn(0)
                        for i in range(SUBS):
                            if i + 1 < SUBS:
                                turn(i + 1)
                            pe.wait_ge(turn_copied, LEAD + pair * SUBS + i + 1)
                            pe.wait_ge(x_copied, LEAD + pair * SUBS + i + 1)
                            for k in range(2):
                                last = nc.tensor.matmul(pooled_ps[k][:], x_tok[:, i % 2, k, :],
                                                        w_tok[:, i % 2, E * k:E * (k + 1)],
                                                        start=(i == 0), stop=(i == SUBS - 1))
                            last.then_inc(pooled, 1)

                @block.scalar
                def _(act):
                    for pair in range(PAIRS):
                        for k in range(2):
                            at = slice(E * k, E * (k + 1))
                            for i in range(TPB):
                                n = (pair * 2 + k) * TPB + i
                                act.wait_ge(logits_done, LEAD + n + 1)
                                act.wait_ge(left_done, LEAD + pair)
                                nc.scalar.activation(logit[at, chunk(i)], logit_ps[i % 2][at, :], ACT.Identity,
                                                     bias=gate_b[at, 0:1]).then_inc(logit_copied, 1)
                        act.wait_ge(max_done, LEAD + pair + 1)
                        act.wait_ge(logit_copied, LEAD + (pair + 1) * 2 * TPB)
                        nc.scalar.activation(token_weight[:, pair, :], logit[:], ACT.Exp, bias=minus_max[:, 0:1],
                                             accum_out=total[:, 0:1]).then_inc(exp_done, 1)
                        nc.scalar.activation(top_exp[:], top[:], ACT.Exp, bias=minus_max[:, 0:1]).then_inc(top_exp_done, 1)

                @block.vector
                def _(dve):
                    for pair in range(PAIRS):
                        dve.wait_ge(logit_copied, LEAD + (pair + 1) * 2 * TPB)
                        dve.wait_ge(left_done, LEAD + pair)
                        nc.vector.max(top[:], logit[:]).then_inc(top_done, 1)
                        dve.wait_ge(top_done, LEAD + pair + 1)
                        nc.vector.tensor_scalar(minus_max[:], top[:, 0:1], -1.0, None, ALU.mult).then_inc(max_done, 1)
                        dve.wait_ge(exp_done, LEAD + pair + 1)
                        dve.wait_ge(top_exp_done, LEAD + pair + 1)
                        nc.vector.reciprocal(share[:], total[:]).then_inc(share_done, 1)
                        nc.vector.match_replace(logit[:], top_exp[:], token_weight[:, pair, :], 0.0).then_inc(left_done, 1)
                        dve.wait_ge(left_done, LEAD + pair + 1)
                        nc.vector.tensor_tensor(token_weight[:, pair, :], token_weight[:, pair, :], logit[:], ALU.subtract
                                                ).then_inc(picked_done, 1)
                        dve.wait_ge(picked_done, LEAD + pair + 1)
                        dve.wait_ge(share_done, LEAD + pair + 1)
                        nc.vector.tensor_scalar(token_weight[:, pair, :], token_weight[:, pair, :], share[:, 0:1], None,
                                                ALU.mult).then_inc(weight_done, 1)
                        for i in range(SUBS):
                            dve.wait_ge(turned, LEAD + pair * SUBS + i + 1)
                            dve.wait_ge(pooled, LEAD + pair * SUBS + i - 1)
                            nc.vector.tensor_copy(x_tok[:, i % 2, :, :], turn_ps[i % 2][:, 0:2, :]).then_inc(x_copied, 1)
                            nc.vector.tensor_copy(w_tok[:, i % 2, :], turn_ps[i % 2][:, 2, :]).then_inc(turn_copied, 1)
                        for k in range(2):
                            dve.wait_ge(pooled, LEAD + SUBS * (pair + 1))
                            nc.vector.tensor_copy(pooled_t[:, :, 2 * pair + k], pooled_ps[k][:]).then_inc(pooled_copied, 1)

        with Part(nc, name + "x") as pre:
            ring = [pre.sb(f"ring{n}", [CH, QUAD, H]) for n in range(2 * QUADS)]
            ring_loaded = [pre.sem(f"ring_loaded{n}") for n in range(2 * QUADS)]
            ring_used = [pre.sem(f"ring_used{n}") for n in range(2 * QUADS)]

            def load_quad(eng, n, g):
                first = g * GROUP + (n % QUADS) * QUAD
                if n < QUADS:
                    src = w["weight1"][bass.ds(first, QUAD), 0:CH, :].rearrange("e d j -> d e j")
                    dst = ring[n][:]
                else:
                    src = w["weight2"][bass.ds(first, QUAD), 0:H, :].rearrange("e (p t) o -> p e (t o)", t=JT)
                    dst = ring[n][:]
                eng.dma_start(dst, src).then_inc(ring_loaded[n], 16)

            hidden = pre.sb("hidden", [CH, 2, GROUP, JT, BATCH])
            hidden_ps = [pre.ps(f"hidden_ps{k}", [CH, GROUP, JT, BATCH]) for k in range(2)]
            out_ps = [pre.ps(f"out_ps{k}", [CH, GROUP, BATCH]) for k in range(2)]
            (biased_done, gelu_done, out_done) = sems = pre.sems("biased_done gelu_done out_done")
            prime(nc, sems)
            first_done, second_done = ring_used[QUADS - 1], ring_used[2 * QUADS - 1]
            TURNS = E // GROUP
            with nc.Block() as block:
                @block.sync
                def _(sp):
                    with sp.Fori(0, TURNS) as g:
                        for n in range(2 * QUADS):
                            sp.wait_ge(ring_used[n], g)
                            load_quad(sp, n, g)

                @block.tensor
                def _(pe):
                    with pe.Fori(0, TURNS) as g:
                        for n in range(QUADS):
                            pe.wait_ge(ring_loaded[n], 16 * (g + 1))
                            if n == 0:
                                pe.wait_ge(biased_done, LEAD + g)
                            for e in range(QUAD):
                                for t in range(JT):
                                    last = nc.tensor.matmul(
                                        hidden_ps[0][:, n * QUAD + e, t, :], ring[n][:, e, t::JT],
                                        pooled_t[:, bass.ds(g * GROUP + n * QUAD + e, 1), :].rearrange("d a b -> d (a b)"),
                                        start=True, stop=True)
                                    if e == QUAD - 1 and t == JT - 1:
                                        last.then_inc(ring_used[n], 1)
                        pe.wait_ge(gelu_done, LEAD + g + 1)
                        pe.wait_ge(out_done, LEAD + BATCH * g)
                        for n in range(QUADS):
                            pe.wait_ge(ring_loaded[QUADS + n], 16 * (g + 1))
                            for e in range(QUAD):
                                for t in range(JT):
                                    last = nc.tensor.matmul(
                                        out_ps[0][:, n * QUAD + e, :], ring[QUADS + n][:, e, chunk(t, O)],
                                        hidden[:, 1, n * QUAD + e, t, :], start=(t == 0), stop=(t == JT - 1))
                                    if e == QUAD - 1 and t == JT - 1:
                                        last.then_inc(ring_used[QUADS + n], 1)

                @block.scalar
                def _(act):
                    with act.Fori(0, TURNS) as g:
                        act.wait_ge(biased_done, LEAD + g + 1)
                        act.wait_ge(second_done, g)
                        nc.scalar.activation(hidden[:, 1, :, :, :], hidden[:, 0, :, :, :], ACT.Gelu).then_inc(gelu_done, 1)

                @block.vector
                def _(dve):
                    with dve.Fori(0, TURNS) as g:
                        dve.wait_ge(first_done, g + 1)
                        dve.wait_ge(gelu_done, LEAD + g)
                        nc.vector.tensor_tensor(
                            hidden[:, 0, :, :, :], hidden_ps[0][:],
                            b1_t[:, :, bass.ds(g * GROUP, GROUP)].rearrange("p t e -> p e t")
                            .unsqueeze(3).to_broadcast([CH, GROUP, JT, BATCH]), ALU.add).then_inc(biased_done, 1)
                        dve.wait_ge(second_done, g + 1)
                        for b in range(BATCH):
                            nc.vector.tensor_tensor(
                                out_t[:, b // 2, b % 2, bass.ds(g * GROUP, GROUP)], out_ps[0][:, :, b],
                                b2_t[:, bass.ds(g * GROUP, GROUP)], ALU.add).then_inc(out_done, 1)
                    dve.wait_ge(out_done, LEAD + BATCH * TURNS)

        with Part(nc, name + "o") as pre:
            out_e = pre.sb("out_e", [CH, PAIRS, O])
            back_ps = [pre.ps(f"back_ps{k}", [CH, TILE]) for k in range(2)]
            back_done, added = sems = pre.sems("back_done added")
            prime(nc, sems)
            build_transposes(nc, name + "u", const,
                             [(out_e[:, p, :], out_t[:, p, :, :].rearrange("o b e -> o (b e)"), None)
                              for p in range(PAIRS)])
            with nc.Block() as block:
                @block.tensor
                def _(pe):
                    for b in range(BATCH):
                        at = slice(E * (b % 2), E * (b % 2 + 1))
                        for i in range(TPB):
                            t = b * TPB + i
                            pe.wait_ge(added, LEAD + t - 1)
                            nc.tensor.matmul(back_ps[i % 2][:], out_e[at, b // 2, :], token_weight[at, b // 2, chunk(i)],
                                             start=True, stop=True).then_inc(back_done, 1)

                @block.vector
                def _(dve):
                    with dve.Fori(0, NT // 2) as j:
                        for k in range(2):
                            t = 2 * j + k
                            dve.wait_ge(back_done, LEAD + t + 1)
                            nc.vector.tensor_tensor(const.x[:, chunk(t)], back_ps[k][:], const.x[:, chunk(t)], ALU.add
                                                    ).then_inc(added, 1)
                    dve.wait_ge(added, LEAD + NT)


def build_ssd(nc, const, name, w, normed_dram, back):
    DI, NS, HEADS, HD, TAPS = 256, 64, 4, 64, 4
    HALVES = DI // CH
    SUBS = TILE // CH
    CONV = 3
    IN = 2 * DI + 2 * NS + HEADS
    CAP = 40.0
    ALMOST_ONE = 1.0 - 2.0 ** -23
    DT, DA, DTD, DCH = range(4)
    edge = TILE if back else 0
    here = 0 if back else TAPS - 1

    def tap(k):
        return TAPS - 1 - k if back else k

    def place(t):
        return t * -1 + (NT - 1) if back else t

    def placed(eng, t):
        if isinstance(t, int):
            return place(t)
        at = eng.snap(place(t))
        eng.compute_val(at)
        return at

    def sub(u):
        return SUBS - 1 - u if back else u

    with Part(nc, name) as part:
        in_w = part.sb("in_w", [CH, IN])
        conv_w = part.sb("conv_w", [CH, CONV, TAPS])
        conv_b = part.sb("conv_b", [CH, CONV])
        d_skip = part.sb("d_skip", [CH, HALVES])
        out_w = part.sb("out_w", [CH, HALVES, CH])
        after = part.sb("after", [CH, CH])
        upto = part.sb("upto", [CH, CH])
        scalars = part.sb("scalars", [CH, NT * SUBS, 4, HEADS])
        keep = part.sb("keep", [CH, NT])

        with Part(nc, name + "w") as pre:
            norm_w = pre.sb("norm_w", [CH, HALVES])
            rows = pre.sb("rows", [1, 2 * HEADS])
            ones_row = pre.sb("ones_row", [1, CH])
            head_row = pre.sb("head_row", [1, HEADS])
            heads = pre.sb("heads", [CH, 2 * HEADS])
            minus_a = pre.sb("minus_a", [CH, HEADS])
            heads_ps = pre.ps("heads_ps", [CH, 2 * HEADS])
            ones = pre.sb("ones", [CH, CH])
            dt_ps = pre.ps("dt_ps", [CH, NT * SUBS, HEADS])
            sum_ps = [pre.ps(f"sum_ps{k}", [CH, TILE]) for k in range(2)]
            xh = pre.sb("xh", [CH, 2, TILE])
            a = pre.sb("a", [CH, NT * SUBS, HEADS])
            e = pre.sb("e", [CH, NT * SUBS, HEADS])
            small = pre.sb("small", [CH, NT * SUBS, HEADS])
            log = pre.sb("log", [CH, NT * SUBS, HEADS])
            dt = pre.sb("dt", [CH, NT * SUBS, HEADS])
            da = pre.sb("da", [CH, NT * SUBS, HEADS])
            almost_one = pre.sb("almost_one", [CH, 1])
            (loaded, made, heads_done, step, exp_done, projected, dt_step, e_done, small_done, log_done, da_done,
             sums_done, sums_exp, scalars_done) = pre.sems(
                "loaded made heads_done step exp_done projected dt_step e_done small_done log_done da_done "
                "sums_done sums_exp scalars_done")
            xh_loaded = pre.sems("xh_loaded0 xh_loaded1")
            xh_used = pre.sem("xh_used")
            prime(nc, (xh_used,))
            with nc.Block() as block:
                @block.sync
                def _(sp):
                    with nc.allow_non_contiguous_dma("small weights"):
                        n = 0
                        loads = [(in_w[:], w["in_proj"]),
                                 (conv_w[:], w["conv_w"].rearrange("(t p) k -> p t k", p=CH)),
                                 (conv_b[:], w["conv_b"].rearrange("(t p) -> p t", p=CH)),
                                 (norm_w[:], half_columns(w["norm_w"])),
                                 (out_w[:], w["out_proj"].rearrange("(h p) c -> p h c", p=CH)),
                                 (rows[0:1, 0:HEADS], w["dt_bias"].rearrange("(a n) -> a n", a=1)),
                                 (rows[0:1, HEADS:], w["A_log"].rearrange("(a n) -> a n", a=1))]
                        for h in range(HEADS):
                            loads.append((d_skip[HD * (h % 2):HD * (h % 2 + 1), h // 2:h // 2 + 1],
                                          w["D"][h:h + 1].rearrange("(a n) -> a n", a=1).to_broadcast([HD, 1])))
                        for dst, src in loads:
                            sp.dma_start(dst, src).then_inc(loaded, 16)
                            n += 1
                        sp.wait_ge(loaded, 16 * n)
                    with sp.Fori(0, NT // 2) as i:
                        for k in range(2):
                            sp.wait_ge(xh_used, LEAD + 2 * i + k - 1)
                            sp.dma_start(xh[:, k, :], normed_dram[:, chunk(2 * i + k)]).then_inc(xh_loaded[k], 16)

                @block.gpsimd
                def _(pool):
                    nc.gpsimd.memset(ones_row[:], 1.0).then_inc(made, 1)
                    nc.gpsimd.memset(ones[:], 1.0).then_inc(made, 1)
                    nc.gpsimd.memset(after[:], 1.0).then_inc(made, 1)
                    nc.gpsimd.memset(upto[:], 1.0).then_inc(made, 1)
                    nc.gpsimd.memset(keep[:], 1.0).then_inc(made, 1)
                    nc.gpsimd.memset(almost_one[:], ALMOST_ONE).then_inc(made, 1)
                    pool.wait_ge(made, 6)
                    sign = -1 if back else 1
                    nc.gpsimd.affine_select(out=after[:], in_=after[:], compare_op=ALU.is_gt, fill=0.0, base=0,
                                            pattern=[[-sign, CH]], channel_multiplier=sign).then_inc(made, 1)
                    nc.gpsimd.affine_select(out=upto[:], in_=upto[:], compare_op=ALU.is_ge, fill=0.0, base=0,
                                            pattern=[[sign, CH]], channel_multiplier=-sign).then_inc(made, 1)
                    nc.gpsimd.memset(keep[:, 0:NT:TPB], 0.0).then_inc(made, 1)
                    pool.wait_ge(made, 9)

                @block.tensor
                def _(pe):
                    pe.wait_ge(made, 9)
                    pe.wait_ge(loaded, 16 * 11)
                    nc.tensor.matmul(heads_ps[:], ones_row[0:1, :], rows[0:1, :], start=True, stop=True
                                     ).then_inc(heads_done, 1)
                    with pe.Fori(0, NT // 2) as i:
                        for k in range(2):
                            pe.wait_ge(xh_loaded[k], 16 * (i + 1))
                            for c in range(SUBS):
                                last = nc.tensor.matmul(
                                    dt_ps[:, bass.ds((2 * i + k) * SUBS + c, 1), :].rearrange("p a h -> p (a h)"),
                                    xh[:, k, chunk(c, CH)], in_w[:, IN - HEADS:], start=True, stop=True)
                            last.then_inc(xh_used, 1)
                    pe.wait_ge(da_done, 1)
                    flat = da[:].rearrange("p s h -> p (s h)")
                    nc.tensor.matmul(sum_ps[0][:], after[:], flat, start=True, stop=True).then_inc(sums_done, 1)
                    nc.tensor.matmul(sum_ps[1][:], ones[:], flat, start=True, stop=True).then_inc(sums_done, 1)

                @block.scalar
                def _(act):
                    nc.scalar.preload_act_table_set("natural_log_exp_and_others")
                    act.wait_ge(step, 1)
                    nc.scalar.activation(minus_a[:], heads[:, HEADS:], ACT.Exp).then_inc(exp_done, 1)
                    act.wait_ge(dt_step, 2)
                    nc.scalar.activation(e[:], a[:], ACT.Exp).then_inc(e_done, 1)
                    act.wait_ge(e_done, 1)
                    nc.scalar.activation(small[:], e[:], ACT.Exp, scale=-0.5).then_inc(small_done, 1)
                    nc.scalar.activation(log[:], e[:], ACT.Ln, bias=almost_one[:, 0:1]).then_inc(log_done, 1)
                    act.wait_ge(sums_done, 1)
                    act.wait_ge(dt_step, 7)
                    nc.scalar.activation(a[:].rearrange("p s h -> p (s h)"), sum_ps[0][:], ACT.Exp).then_inc(sums_exp, 1)
                    act.wait_ge(sums_done, 2)
                    nc.scalar.activation(scalars[:, :, DCH, :], sum_ps[1][:].rearrange("p (s h) -> p s h", h=HEADS),
                                         ACT.Exp).then_inc(sums_exp, 1)

                @block.vector
                def _(dve):
                    dve.wait_ge(heads_done, 1)
                    nc.vector.tensor_copy(heads[:], heads_ps[:]).then_inc(step, 1)
                    dve.wait_ge(loaded, 16 * 11)
                    for h in range(HALVES):
                        nc.vector.tensor_scalar(out_w[:, h, :], out_w[:, h, :], norm_w[:, h:h + 1], None, ALU.mult
                                                ).then_inc(step, 1)
                    dve.wait_ge(exp_done, 1)
                    nc.vector.tensor_scalar(minus_a[:], minus_a[:], -1.0, None, ALU.mult).then_inc(step, 1)
                    dve.wait_ge(step, 4)
                    dve.wait_ge(xh_used, LEAD + NT)
                    every = [CH, NT * SUBS, HEADS]
                    nc.vector.tensor_tensor(dt[:], dt_ps[:], heads[:, 0:HEADS].unsqueeze(1).to_broadcast(every), ALU.add
                                            ).then_inc(dt_step, 1)
                    dve.wait_ge(dt_step, 1)
                    nc.vector.tensor_scalar(a[:], dt[:], CAP, None, ALU.min).then_inc(dt_step, 1)
                    dve.wait_ge(log_done, 1)
                    nc.vector.tensor_tensor(dt[:], dt[:], log[:], ALU.max).then_inc(dt_step, 1)
                    dve.wait_ge(small_done, 1)
                    nc.vector.tensor_tensor(small[:], small[:], e[:], ALU.mult).then_inc(dt_step, 1)
                    dve.wait_ge(dt_step, 4)
                    nc.vector.tensor_tensor(dt[:], dt[:], small[:], ALU.max).then_inc(dt_step, 1)
                    dve.wait_ge(dt_step, 5)
                    nc.vector.tensor_tensor(da[:], dt[:], minus_a[:].unsqueeze(1).to_broadcast(every), ALU.mult
                                            ).then_inc(da_done, 1)
                    nc.vector.tensor_copy(scalars[:, :, DT, :], dt[:]).then_inc(dt_step, 1)
                    dve.wait_ge(da_done, 1)
                    nc.vector.tensor_copy(scalars[:, :, DA, :], da[:]).then_inc(dt_step, 1)
                    dve.wait_ge(sums_exp, 2)
                    nc.vector.tensor_tensor(scalars[:, :, DTD, :], dt[:], a[:], ALU.mult).then_inc(scalars_done, 1)
                    dve.wait_ge(scalars_done, 1)
                    dve.wait_ge(dt_step, 7)

        xh = [part.sb(f"xh{k}", [CH, TILE]) for k in range(2)]
        xbc = part.sb("xbc", [CH, CONV, TILE + TAPS - 1])
        conv = part.sb("conv", [CH, CONV, TILE])
        xs = [part.sb(f"xs{k}", [CH, HALVES, TILE]) for k in range(2)]
        b_t = [part.sb(f"b_t{k}", [NS, TILE]) for k in range(2)]
        c_t = [part.sb(f"c_t{k}", [NS, TILE]) for k in range(2)]
        gate = [part.sb(f"gate{k}", [CH, HALVES, TILE]) for k in range(2)]
        now = [part.sb(f"now{k}", [CH, SUBS, 4, HEADS]) for k in range(2)]
        seg_w = [part.sb(f"seg_w{u}", [CH, HEADS, CH]) for u in range(SUBS)]
        mix = [part.sb(f"mix{u}", [CH, HEADS, CH]) for u in range(SUBS)]
        cb = [part.sb(f"cb{k}", [CH, CH]) for k in range(2)]
        xdt = [part.sb(f"xdt{k}", [CH, HEADS, HD]) for k in range(2)]
        xdd = [part.sb(f"xdd{k}", [CH, HEADS, HD]) for k in range(2)]
        b_tok = [part.sb(f"b_tok{k}", [CH, NS]) for k in range(2)]
        c_fade = [part.sb(f"c_fade{u}", [NS, HEADS, CH]) for u in range(SUBS)]
        state = part.sb("state", [NS, HEADS, HD])
        y = part.sb("y", [CH, HALVES, TILE])
        square = part.sb("square", [CH, HALVES, TILE])
        logv = part.sb("logv", [CH, TILE])
        rstd = part.sb("rstd", [CH, TILE])
        pre_ps = part.ps("pre_ps", [CH, TILE])
        seg_ps = part.ps("seg_ps", [CH, HEADS, CH])
        fade_ps = part.ps("fade_ps", [NS, HEADS, CH])
        turn_ps = part.ps("turn_ps", [CH, 3, CH])
        cb_ps = part.ps("cb_ps", [CH, CH])
        state_ps = part.ps("state_ps", [NS, HEADS, HD])
        y_ps = [part.ps(f"y_ps{h}", [CH, TILE]) for h in range(HALVES)]
        (pre_filled, pre_drained, tail_done, xbc_done, tap0_done, conv_step, conv_done, silu_done, now_done,
         seg_w_done, seg_done, mix_exp, mix_done, cb_raw, cb_done, turned, xdt_done, xdd_done, b_tok_done,
         fade_done, c_exp, c_fade_done, y_done, state_new, state_done, skipped, gated, squared, log_done, rstd_done,
         normed, state_kept) = sems = part.sems(
            "pre_filled pre_drained tail_done xbc_done tap0_done conv_step conv_done silu_done now_done "
            "seg_w_done seg_done mix_exp mix_done cb_raw cb_done turned xdt_done xdd_done b_tok_done "
            "fade_done c_exp c_fade_done y_done state_new state_done skipped gated squared log_done rstd_done "
            "normed state_kept")
        xh_loaded = part.sems("xh_loaded0 xh_loaded1")
        cleared = part.sem("cleared")
        prime(nc, sems)

        ORDER = ("X0", "X1", "BC", "MS", "Z0", "Z1", "OUT")
        FIRST = ("X0", "X1", "BC", "Z0", "Z1")
        N = len(ORDER)

        def fill(t, what):
            if isinstance(t, int) and t == -1:
                return FIRST.index(what)
            if isinstance(t, int) and t == 0:
                return len(FIRST) + FIRST.index(what)
            base = 2 * len(FIRST) + (t - 1) * N
            if isinstance(t, int) and t == NT - 1:
                return base + {"MS": 0, "OUT": 1, "MS_LAST": 2, "OUT_LAST": 3}[what]
            return base + ORDER.index(what)

        def over_tiles(eng, tile):
            tile(0, 0, True, False)
            with eng.Fori(0, (NT - 2) // 2) as i:
                tile(2 * i + 1, 1, False, False)
                tile(2 * i + 2, 0, False, False)
            tile(NT - 1, 1, False, True)

        with nc.Block() as block:
            @block.sync
            def _(sp):
                def load(t, k):
                    at = placed(sp, t)
                    sp.wait_ge(silu_done, LEAD + 6 * (t - 1))
                    sp.dma_start(xh[k][:], normed_dram[:, chunk(at)]).then_inc(xh_loaded[k], 16)

                load(0, 0)
                load(1, 1)
                with sp.Fori(0, (NT - 2) // 2) as i:
                    load(2 * i + 2, 0)
                    load(2 * i + 3, 1)

            @block.tensor
            def _(pe):
                def into_pre(t, what, pairs):
                    pe.wait_ge(pre_drained, LEAD + fill(t, what))
                    for n, (lhs, rhs) in enumerate(pairs):
                        last = nc.tensor.matmul(pre_ps[:], lhs, rhs, start=(n == 0), stop=(n == len(pairs) - 1))
                    last.then_inc(pre_filled, 1)

                def prepare(t, what, r, k):
                    col = {"Z0": 0, "Z1": CH, "X0": 2 * CH, "X1": 3 * CH, "BC": 4 * CH}[what]
                    if what == "X0":
                        pe.wait_ge(xh_loaded[k], 16 * ((r - k) // 2 + 1 if isinstance(r, int) else half_of(r, k) + 1))
                    into_pre(t, what, [(in_w[:, col:col + CH], xh[k][:])])

                def half_of(r, k):
                    return turns[0] + (1 if k == 0 else (0 if turn_k[0] == 1 else 1))

                turns, turn_k = [None], [None]

                def decays(t, k, u):
                    c = 4 * t + u
                    if u == 0:
                        pe.wait_ge(now_done, LEAD + t + 1)
                    pe.wait_ge(c_exp, LEAD + c)
                    for h in range(HEADS):
                        last = nc.tensor.matmul(fade_ps[:, h, :], now[k][:, sub(u), DA, h:h + 1].to_broadcast([CH, NS]),
                                                upto[:], start=True, stop=True)
                    last.then_inc(fade_done, 1)
                    pe.wait_ge(mix_exp, LEAD + c)
                    pe.wait_ge(seg_w_done, LEAD + c + 1)
                    for h in range(HEADS):
                        last = nc.tensor.matmul(seg_ps[:, h, :], seg_w[u][:, h, :], upto[:], start=True, stop=True)
                    last.then_inc(seg_done, 1)

                def chunk_in(t, k, u, last_tile):
                    c = 4 * t + u
                    cols = chunk(sub(u), CH)
                    if u == 0:
                        pe.wait_ge(silu_done, LEAD + 6 * t + 4)
                    pe.wait_ge(cb_done, LEAD + c)
                    nc.tensor.matmul(cb_ps[:], b_t[k][:, cols], c_t[k][:, cols], start=True, stop=True).then_inc(cb_raw, 1)
                    pe.wait_ge(xdt_done, LEAD + c)
                    pe.wait_ge(xdd_done, LEAD + c)
                    pe.wait_ge(b_tok_done, LEAD + c)
                    for h in range(HALVES):
                        nc.tensor.transpose(turn_ps[:, h, :], xs[k][:, h, cols], const.ident[:])
                    nc.tensor.transpose(turn_ps[:, 2, 0:NS], b_t[k][:, cols], const.ident[0:NS, 0:NS]).then_inc(turned, 1)
                    if u < SUBS - 1:
                        decays(t, k, u + 1)
                    elif not last_tile:
                        decays(t + 1, 1 - k, 0)

                def chunk_out(t, k, u):
                    c = 4 * t + u
                    cols = chunk(sub(u), CH)
                    pe.wait_ge(xdd_done, LEAD + c + 1)
                    pe.wait_ge(b_tok_done, LEAD + c + 1)
                    pe.wait_ge(state_done, LEAD + HEADS * c)
                    nc.tensor.matmul(state_ps[:].rearrange("n h p -> n (h p)"), b_tok[u % 2][:],
                                     xdd[u % 2][:].rearrange("s h p -> s (h p)"), start=True, stop=True
                                     ).then_inc(state_new, 1)
                    if u == 0:
                        pe.wait_ge(skipped, LEAD + HALVES * t)
                        pe.wait_ge(state_kept, LEAD + t + 1)
                    pe.wait_ge(xdt_done, LEAD + c + 1)
                    pe.wait_ge(mix_done, LEAD + c + 1)
                    pe.wait_ge(c_fade_done, LEAD + c + 1)
                    for h in range(HEADS):
                        at = slice(HD * (h % 2), HD * (h % 2 + 1))
                        nc.tensor.matmul(y_ps[h // 2][at, cols], xdt[u % 2][:, h, :], mix[u][:, h, :],
                                         start=True, stop=False)
                        last = nc.tensor.matmul(y_ps[h // 2][at, cols], state[:, h, :], c_fade[u][:, h, :],
                                                start=False, stop=True)
                    last.then_inc(y_done, 1)

                def mean_square(t, what, r):
                    pe.wait_ge(squared, LEAD + HALVES * (r + 1))
                    into_pre(t, what, [(const.mean[:], square[:, h, :]) for h in range(HALVES)])

                def project(t, what, r):
                    pe.wait_ge(normed, LEAD + HALVES * (r + 1))
                    into_pre(t, what, [(out_w[:, h, :], y[:, h, :]) for h in range(HALVES)])

                def tile(t, k, first, last):
                    r, rk = t + 1, 1 - k
                    chunk_in(t, k, 0, last)
                    if not first:
                        chunk_out(t - 1, 1 - k, SUBS - 1)
                    if not last:
                        prepare(t, "X0", r, rk)
                        prepare(t, "X1", r, rk)
                    chunk_in(t, k, 1, last)
                    chunk_out(t, k, 0)
                    if not last:
                        prepare(t, "BC", r, rk)
                    chunk_in(t, k, 2, last)
                    if not first:
                        mean_square(t, "MS", t - 1)
                    chunk_out(t, k, 1)
                    if not last:
                        prepare(t, "Z0", r, rk)
                    chunk_in(t, k, 3, last)
                    if not last:
                        prepare(t, "Z1", r, rk)
                    chunk_out(t, k, 2)
                    if not first:
                        project(t, "OUT", t - 1)

                for what in FIRST:
                    prepare(-1, what, 0, 0)
                decays(0, 0, 0)
                tile(0, 0, True, False)
                with pe.Fori(0, (NT - 2) // 2) as i:
                    turns[0], turn_k[0] = i, 1
                    tile(2 * i + 1, 1, False, False)
                    turn_k[0] = 0
                    tile(2 * i + 2, 0, False, False)
                tile(NT - 1, 1, False, True)
                chunk_out(NT - 1, 1, SUBS - 1)
                mean_square(NT - 1, "MS_LAST", NT - 1)
                project(NT - 1, "OUT_LAST", NT - 1)

            @block.scalar
            def _(act):
                def taken(t, what, n):
                    r = t + 1
                    if n == 0:
                        act.wait_ge(tail_done, LEAD + r + 1)
                    act.wait_ge(pre_filled, LEAD + fill(t, what) + 1)
                    nc.scalar.activation(xbc[:, n, here:here + TILE], pre_ps[:], ACT.Copy).then_inc(pre_drained, 1)
                    act.wait_ge(pre_drained, LEAD + fill(t, what) + 1)
                    act.wait_ge(silu_done, LEAD + 6 * r)
                    nc.scalar.activation(conv[:, n, :], xbc[:, n, tap(0):tap(0) + TILE], ACT.Identity,
                                         bias=conv_b[:, n:n + 1], scale=conv_w[:, n, 0:1]).then_inc(tap0_done, 1)

                def z0(t, k):
                    r = t + 1
                    act.wait_ge(pre_filled, LEAD + fill(t, "Z0") + 1)
                    act.wait_ge(gated, LEAD + HALVES * (r - 1))
                    nc.scalar.activation(gate[k][:, 0, :], pre_ps[:], ACT.Copy).then_inc(pre_drained, 1)
                    act.wait_ge(pre_drained, LEAD + fill(t, "Z0") + 1)

                def silus(t, k):
                    r = t + 1
                    act.wait_ge(skipped, LEAD + HALVES * (r - 1))
                    act.wait_ge(turned, LEAD + SUBS * (r - 1))
                    act.wait_ge(c_fade_done, LEAD + SUBS * (r - 1))
                    act.wait_ge(conv_done, LEAD + CONV * (r + 1))
                    for n in range(HALVES):
                        nc.scalar.activation(xs[k][:, n, :], conv[:, n, :], ACT.Silu).then_inc(silu_done, 1)
                    nc.scalar.activation(b_t[k][:], conv[0:NS, 2, :], ACT.Silu).then_inc(silu_done, 1)
                    nc.scalar.activation(c_t[k][:], conv[NS:2 * NS, 2, :], ACT.Silu).then_inc(silu_done, 1)
                    nc.scalar.activation(gate[k][:, 0, :], gate[k][:, 0, :], ACT.Silu).then_inc(silu_done, 1)
                    act.wait_ge(pre_filled, LEAD + fill(t, "Z1") + 1)
                    nc.scalar.activation(gate[k][:, 1, :], pre_ps[:], ACT.Silu).then_inc(pre_drained, 1)
                    act.wait_ge(pre_drained, LEAD + fill(t, "Z1") + 1)
                    act.sem_inc(silu_done, 1)

                def decays(t, u):
                    c = 4 * t + u
                    act.wait_ge(fade_done, LEAD + c + 1)
                    act.wait_ge(y_done, LEAD + c - SUBS + 1)
                    nc.scalar.activation(c_fade[u][:], fade_ps[:], ACT.Exp).then_inc(c_exp, 1)
                    act.wait_ge(seg_done, LEAD + c + 1)
                    nc.scalar.activation(mix[u][:], seg_ps[:], ACT.Exp).then_inc(mix_exp, 1)

                def squares(r):
                    for n in range(HALVES):
                        act.wait_ge(gated, LEAD + HALVES * r + n + 1)
                        nc.scalar.activation(square[:, n, :], y[:, n, :], ACT.Square).then_inc(squared, 1)

                def rstds(t, what, r):
                    act.wait_ge(pre_filled, LEAD + fill(t, what) + 1)
                    nc.scalar.activation(logv[:], pre_ps[:], ACT.Ln, bias=const.eps[:, 0:1], scale=1.0 / HALVES
                                         ).then_inc(pre_drained, 1)
                    act.wait_ge(pre_drained, LEAD + fill(t, what) + 1)
                    act.wait_ge(normed, LEAD + HALVES * r)
                    nc.scalar.activation(rstd[:], logv[:], ACT.Exp, scale=-0.5).then_inc(rstd_done, 1)

                def tile(t, k, first, last):
                    decays(t, 1)
                    if not last:
                        taken(t, "X0", 0)
                        taken(t, "X1", 1)
                    decays(t, 2)
                    if not last:
                        taken(t, "BC", 2)
                    if not first:
                        squares(t - 1)
                    decays(t, 3)
                    if not first:
                        rstds(t, "MS", t - 1)
                    if not last:
                        z0(t, 1 - k)
                        decays(t + 1, 0)
                        silus(t, 1 - k)
                        nc.scalar.preload_act_table_set("natural_log_exp_and_others")

                taken(-1, "X0", 0)
                taken(-1, "X1", 1)
                taken(-1, "BC", 2)
                z0(-1, 0)
                silus(-1, 0)
                nc.scalar.preload_act_table_set("natural_log_exp_and_others")
                decays(0, 0)
                over_tiles(act, tile)
                squares(NT - 1)
                rstds(NT - 1, "MS_LAST", NT - 1)

            @block.vector
            def _(dve):
                def tail(t):
                    r = t + 1
                    dve.wait_ge(conv_done, LEAD + CONV * r)
                    dst, src = (slice(TILE, TILE + TAPS - 1), slice(0, TAPS - 1)) if back else (
                        slice(0, TAPS - 1), slice(TILE, TILE + TAPS - 1))
                    nc.vector.tensor_scalar(xbc[:, :, dst], xbc[:, :, src], keep[:, bass.ds(r, 1)], None, ALU.mult
                                            ).then_inc(tail_done, 1)

                def convolve(t, n):
                    r = t + 1
                    dve.wait_ge(tap0_done, LEAD + CONV * r + n + 1)
                    for j in range(1, TAPS):
                        if j > 1:
                            dve.wait_ge(conv_step, LEAD + (CONV * r + n) * (TAPS - 2) + j - 1)
                        done = conv_step if j < TAPS - 1 else conv_done
                        nc.vector.scalar_tensor_tensor(
                            out=conv[:, n, :], in0=xbc[:, n, tap(j):tap(j) + TILE], scalar=conv_w[:, n, j:j + 1],
                            in1=conv[:, n, :], op0=ALU.mult, op1=ALU.add).then_inc(done, 1)

                def take_scalars(t, k):
                    r = t + 1
                    at = placed(dve, r)
                    dve.wait_ge(seg_done, LEAD + SUBS * (r - 1))
                    dve.wait_ge(state_done, LEAD + SUBS * HEADS * (r - 1))
                    nc.vector.tensor_scalar(now[k][:].rearrange("p s f h -> p (s f h)"),
                                            scalars[:, bass.ds(at * SUBS, SUBS), :, :].rearrange(
                                                "p s f h -> p (s f h)"), 1.0, None, ALU.mult).then_inc(now_done, 1)

                def chunk_in(t, k, u):
                    c = 4 * t + u
                    wide = [CH, HEADS, HD]
                    dve.wait_ge(cb_raw, LEAD + c + 1)
                    dve.wait_ge(mix_done, LEAD + c - 1)
                    nc.vector.tensor_tensor(cb[u % 2][:], cb_ps[:], upto[:], ALU.mult).then_inc(cb_done, 1)
                    dve.wait_ge(turned, LEAD + c + 1)
                    dve.wait_ge(y_done, LEAD + c - 1)
                    tok = turn_ps[:, 0:2, :].rearrange("s a (b p) -> s (a b) p", p=HD)
                    nc.vector.tensor_tensor(xdt[u % 2][:], tok,
                                            now[k][:, sub(u), DT, :].unsqueeze(2).to_broadcast(wide), ALU.mult
                                            ).then_inc(xdt_done, 1)
                    dve.wait_ge(state_new, LEAD + c - 1)
                    nc.vector.tensor_copy(b_tok[u % 2][:], turn_ps[:, 2, 0:NS]).then_inc(b_tok_done, 1)
                    nc.vector.tensor_tensor(xdd[u % 2][:], tok,
                                            now[k][:, sub(u), DTD, :].unsqueeze(2).to_broadcast(wide), ALU.mult
                                            ).then_inc(xdd_done, 1)
                    dve.wait_ge(mix_exp, LEAD + c + 1)
                    dve.wait_ge(cb_done, LEAD + c + 1)
                    nc.vector.tensor_tensor(mix[u][:], mix[u][:],
                                            cb[u % 2][:].unsqueeze(1).to_broadcast([CH, HEADS, CH]), ALU.mult
                                            ).then_inc(mix_done, 1)

                def chunk_out(t, k, u):
                    c = 4 * t + u
                    dve.wait_ge(state_new, LEAD + c + 1)
                    dve.wait_ge(y_done, LEAD + c + 1)
                    for h in range(HEADS):
                        nc.vector.scalar_tensor_tensor(out=state[:, h, :], in0=state[:, h, :],
                                                       scalar=now[k][0:NS, sub(u), DCH, h:h + 1], in1=state_ps[:, h, :],
                                                       op0=ALU.mult, op1=ALU.add).then_inc(state_done, 1)
                    dve.wait_ge(state_done, LEAD + HEADS * (c + 1))

                def skip(t, r, k):
                    for n in range(HALVES):
                        if t is None:
                            dve.wait_ge(pre_filled, LEAD + fill(NT - 1, "OUT") + 1)
                        else:
                            dve.wait_ge(pre_filled, LEAD + fill(t, "MS" if isinstance(t, int) else "X0"))
                        nc.vector.scalar_tensor_tensor(out=y[:, n, :], in0=xs[k][:, n, :], scalar=d_skip[:, n:n + 1],
                                                       in1=y_ps[n][:], op0=ALU.mult, op1=ALU.add).then_inc(skipped, 1)

                def add(t, what, r):
                    at = placed(dve, r)
                    dve.wait_ge(pre_filled, LEAD + fill(t, what) + 1)
                    nc.vector.tensor_tensor(const.x[:, chunk(at)], pre_ps[:], const.x[:, chunk(at)], ALU.add
                                            ).then_inc(pre_drained, 1)

                def tile(t, k, first, last):
                    if not last:
                        tail(t)
                    chunk_in(t, k, 0)
                    if not first:
                        chunk_out(t - 1, 1 - k, SUBS - 1)
                        skip(t, t - 1, 1 - k)
                    dve.wait_ge(state_done, LEAD + SUBS * HEADS * t)
                    nc.vector.tensor_scalar(state[:], state[:], keep[0:NS, bass.ds(t, 1)], None, ALU.mult
                                            ).then_inc(state_kept, 1)
                    if not last:
                        take_scalars(t, 1 - k)
                    chunk_in(t, k, 1)
                    dve.wait_ge(state_kept, LEAD + t + 1)
                    chunk_out(t, k, 0)
                    if not last:
                        convolve(t, 0)
                        convolve(t, 1)
                    chunk_in(t, k, 2)
                    chunk_out(t, k, 1)
                    if not last:
                        convolve(t, 2)
                    chunk_in(t, k, 3)
                    chunk_out(t, k, 2)
                    if not first:
                        add(t, "OUT", t - 1)

                nc.vector.memset(state[:], 0.0).then_inc(cleared, 1)
                nc.vector.memset(xbc[:], 0.0).then_inc(cleared, 1)
                dve.wait_ge(cleared, 2)
                tail(-1)
                take_scalars(-1, 0)
                for n in range(CONV):
                    convolve(-1, n)
                over_tiles(dve, tile)
                chunk_out(NT - 1, 1, SUBS - 1)
                skip(None, NT - 1, 1)
                add(NT - 1, "OUT_LAST", NT - 1)

            @block.gpsimd
            def _(pool):
                def segments(t, k, u):
                    c = 4 * t + u
                    if u == 0:
                        pool.wait_ge(now_done, LEAD + t + 1)
                    pool.wait_ge(seg_done, LEAD + c - SUBS + 1)
                    wide = [CH, HEADS, CH]
                    nc.gpsimd.tensor_tensor(seg_w[u][:], after[:].unsqueeze(1).to_broadcast(wide),
                                            now[k][:, sub(u), DA, :].unsqueeze(2).to_broadcast(wide), ALU.mult
                                            ).then_inc(seg_w_done, 1)

                def fade(t, k, u):
                    c = 4 * t + u
                    if u == 0:
                        pool.wait_ge(silu_done, LEAD + 6 * t + 4)
                    pool.wait_ge(c_exp, LEAD + c + 1)
                    nc.gpsimd.tensor_tensor(c_fade[u][:], c_fade[u][:],
                                            c_t[k][:, chunk(sub(u), CH)].unsqueeze(1).to_broadcast([NS, HEADS, CH]),
                                            ALU.mult).then_inc(c_fade_done, 1)

                def gates(t, k):
                    pool.wait_ge(silu_done, LEAD + 6 * (t + 1))
                    for n in range(HALVES):
                        pool.wait_ge(skipped, LEAD + HALVES * t + n + 1)
                        nc.gpsimd.tensor_tensor(y[:, n, :], y[:, n, :], gate[k][:, n, :], ALU.mult).then_inc(gated, 1)

                def norm(r):
                    pool.wait_ge(rstd_done, LEAD + r + 1)
                    pool.wait_ge(squared, LEAD + HALVES * (r + 1))
                    for n in range(HALVES):
                        nc.gpsimd.tensor_tensor(y[:, n, :], y[:, n, :], rstd[:], ALU.mult).then_inc(normed, 1)

                def tile(t, k, first, last):
                    segments(t, k, 2)
                    fade(t, k, 0)
                    segments(t, k, 3)
                    if not first:
                        gates(t - 1, 1 - k)
                    fade(t, k, 1)
                    if not last:
                        segments(t + 1, 1 - k, 0)
                    fade(t, k, 2)
                    if not last:
                        segments(t + 1, 1 - k, 1)
                    fade(t, k, 3)
                    if not first:
                        norm(t - 1)

                segments(0, 0, 0)
                segments(0, 0, 1)
                over_tiles(pool, tile)
                gates(NT - 1, 1)
                norm(NT - 1)


def bimamba(nc, const, fwd, bwd, normed_dram):
    build_layer_norm(nc, const, "ln3", normed_dram)
    build_ssd(nc, const, "sf", fwd, normed_dram, False)
    build_ssd(nc, const, "sb", bwd, normed_dram, True)


def build(nc, a, out):
    def of(prefix):
        return {n[len(prefix):]: v for n, v in a.items() if n.startswith(prefix)}

    normed_dram = nc.dram_tensor("normed_dram", (CH, (NT + 1) * TILE), F32, kind="Internal").ap()
    mixed_dram = nc.dram_tensor("mixed_dram", (CH, NT * TILE), F32, kind="Internal").ap()
    with Part(nc, "k") as part:
        const = Constants(part)
        build_constants(nc, const)
        load_x(nc, const, a["x"])
        layer0(nc, const, of("L0_conv_"), normed_dram, mixed_dram)
        layer1(nc, const, of("L1_conv_"))
        attention(nc, const, normed_dram)
        experts(nc, const, "f2", of("L2_ffn_"), normed_dram)
        bimamba(nc, const, of("L3_attn_fwd_"), of("L3_attn_bwd_"), normed_dram)
        experts(nc, const, "f3", of("L3_ffn_"), normed_dram)
        store_x(nc, const, out)


_INS = ["x", "L0_conv_gamma", "L0_conv_beta", "L0_conv_W_in", "L0_conv_conv_w", "L0_conv_conv_b", "L0_conv_W_x",
        "L0_conv_W_dt", "L0_conv_b_dt", "L0_conv_A_log", "L0_conv_D_skip", "L0_conv_W_out", "L0_conv_W_p",
        "L0_conv_b_p", "L0_conv_s1", "L0_conv_s2", "L1_conv_w_kg", "L1_conv_b_kg", "L1_conv_w_pw", "L1_conv_b_pw",
        "L2_ffn_gate_w", "L2_ffn_gate_b", "L2_ffn_weight1", "L2_ffn_weight2",
        "L3_attn_fwd_in_proj", "L3_attn_fwd_conv_w", "L3_attn_fwd_conv_b", "L3_attn_fwd_A_log",
        "L3_attn_fwd_dt_bias", "L3_attn_fwd_D", "L3_attn_fwd_norm_w", "L3_attn_fwd_out_proj",
        "L3_attn_bwd_in_proj", "L3_attn_bwd_conv_w", "L3_attn_bwd_conv_b", "L3_attn_bwd_A_log",
        "L3_attn_bwd_dt_bias", "L3_attn_bwd_D", "L3_attn_bwd_norm_w", "L3_attn_bwd_out_proj",
        "L3_ffn_gate_w", "L3_ffn_gate_b", "L3_ffn_weight1", "L3_ffn_weight2"]
_OUT = (BATCH, CH, IMG, IMG)


def kernel(**inputs):
    import numpy as _np
    import concourse.bacc as _bacc
    from concourse.bass_utils import run_bass_kernel_spmd as _run

    nc = _bacc.Bacc("TRN2", target_bir_lowering=False, num_devices=1)
    arrays, args = {}, {}
    for name in _INS:
        a = _np.ascontiguousarray(inputs[name])
        arrays[f"in_{name}"] = a
        args[name] = nc.dram_tensor(f"in_{name}", a.shape, mybir.dt.from_np(a.dtype), kind="ExternalInput").ap()
    out = nc.dram_tensor("out_x", _OUT, F32, kind="ExternalOutput").ap()
    build(nc, args, out)
    r = _run(nc, [arrays], core_ids=[0])
    return r.results[0]["out_x"]
```

```python
import math
from contextlib import ExitStack

import numpy as np

import concourse.bass as bass
from concourse import mybir

F32 = mybir.dt.float32
BF16 = mybir.dt.bfloat16
F16 = mybir.dt.float16
ACT = mybir.ActivationFunctionType
ALU = mybir.AluOpType
AX = mybir.AxisListType

BATCH, CH, IMG = 4, 128, 64
TOK = IMG * IMG
TILE = 512
TPB = TOK // TILE
NT = BATCH * TPB
LEAD = 32


class Part:

    def __init__(self, nc, name):
        self.nc, self.name, self.stack, self.held = nc, name, ExitStack(), []

    def __enter__(self):
        self.stack.__enter__()
        return self

    def __exit__(self, *exc):
        if exc[0] is None and self.held:
            with self.nc.Block() as block:
                @block.sync
                def _(sp):
                    for held in self.held:
                        sp.sem_clear(held)
        return self.stack.__exit__(*exc)

    def sb(self, name, shape, dt=F32):
        return self.stack.enter_context(self.nc.sbuf_tensor(f"{self.name}_{name}", shape, dt))

    def ps(self, name, shape, dt=F32):
        return self.stack.enter_context(self.nc.psum_tensor(f"{self.name}_{name}", shape, dt))

    def sem(self, name):
        held = self.stack.enter_context(self.nc.semaphore(f"{self.name}_{name}"))
        self.held.append(held)
        return held

    def sems(self, names):
        return [self.sem(n) for n in names.split()]


def prime(nc, sems):
    with nc.Block() as block:
        @block.sync
        def _(sp):
            for s in sems:
                sp.sem_inc(s, LEAD)


def chunk(i, size=TILE):
    return bass.ds(i * size, size)


def column(ap):
    return ap.rearrange("(p n) -> p n", n=1)


def half_columns(ap):
    return ap.rearrange("(h p) -> p h", p=128)


def build_constants(nc, const):
    with Part(nc, "kc") as part:
        ready, = part.sems("ready")
        with nc.Block() as block:
            @block.gpsimd
            def _(pool):
                nc.gpsimd.memset(const.ident[:], 0.0).then_inc(ready, 1)
                nc.gpsimd.memset(const.center[:], -1.0 / CH).then_inc(ready, 1)
                nc.gpsimd.memset(const.mean[:], 1.0 / CH).then_inc(ready, 1)
                nc.gpsimd.memset(const.eps[:], 1e-5).then_inc(ready, 1)
                pool.wait_ge(ready, 4)
                nc.gpsimd.affine_select(out=const.ident[:], in_=const.ident[:], compare_op=ALU.not_equal, fill=1.0,
                                        base=0, pattern=[[-1, CH]], channel_multiplier=1).then_inc(ready, 1)
                nc.gpsimd.affine_select(out=const.center[:], in_=const.center[:], compare_op=ALU.not_equal,
                                        fill=1.0 - 1.0 / CH, base=0, pattern=[[-1, CH]],
                                        channel_multiplier=1).then_inc(ready, 1)
                pool.wait_ge(ready, 6)


class Constants:

    def __init__(self, part):
        self.x = part.sb("x", [CH, BATCH * TOK])
        self.ident = part.sb("ident", [CH, CH])
        self.center = part.sb("center", [CH, CH])
        self.mean = part.sb("mean", [CH, CH])
        self.eps = part.sb("eps", [CH, 1])


def build_group_norm(nc, const, name, scale, shift, x=None):
    GROUPS, PER = 32, CH // 32
    PIECES = TOK // 512
    PARTS = 2
    with Part(nc, name) as part:
        stats = part.sb("stats", [CH, BATCH, PIECES, 6])
        mv = part.sb("mv", [CH, BATCH, 2])
        moments = part.sb("moments", [CH, 2, BATCH])
        member = part.sb("member", [CH, CH])
        group = part.sb("group", [CH, 2, BATCH])
        msq = part.sb("msq", [CH, BATCH])
        var = part.sb("var", [CH, BATCH])
        averaged = part.ps("averaged", [CH, 2, BATCH])
        stats_done, step, member_done, averaged_done, var_done, log_done, rstd_done = part.sems(
            "stats_done step member_done averaged_done var_done log_done rstd_done")
        loaded = [[part.sem(f"loaded{b}{k}") for k in range(PARTS)] for b in range(BATCH)]
        with nc.Block() as block:
            @block.sync
            def _(sp):
                if x is not None:
                    for b in range(BATCH):
                        for k in range(PARTS):
                            rows = slice(k * IMG // PARTS, (k + 1) * IMG // PARTS)
                            sp.dma_start(const.x[:, chunk(b * PARTS + k, TOK // PARTS)],
                                         x[b, :, rows, :].rearrange("c h w -> c (h w)")).then_inc(loaded[b][k], 16)

            @block.gpsimd
            def _(pool):
                v = member[:].rearrange("p (g k) -> p g k", k=PER)
                nc.gpsimd.memset(member[:], 1.0 / PER).then_inc(member_done, 1)
                pool.wait_ge(member_done, 1)
                nc.gpsimd.affine_select(out=v, in_=v, compare_op=ALU.is_ge, fill=0.0, base=0,
                                        pattern=[[-PER, GROUPS], [0, PER]], channel_multiplier=1).then_inc(member_done, 1)
                pool.wait_ge(member_done, 2)
                nc.gpsimd.affine_select(out=v, in_=v, compare_op=ALU.is_ge, fill=0.0, base=PER - 1,
                                        pattern=[[PER, GROUPS], [0, PER]], channel_multiplier=-1).then_inc(member_done, 1)

            @block.vector
            def _(dve):
                for b in range(BATCH):
                    for i in range(PIECES):
                        if x is not None and i % (PIECES // PARTS) == 0:
                            dve.wait_ge(loaded[b][i // (PIECES // PARTS)], 16)
                        nc.vector.bn_stats(stats[:, b, i, :], const.x[:, chunk(b * PIECES + i)]).then_inc(stats_done, 1)
                dve.wait_ge(stats_done, BATCH * PIECES)
                for b in range(BATCH):
                    nc.vector.bn_aggr(mv[:, b, :], stats[:, b, :, :]).then_inc(step, 1)
                dve.wait_ge(step, 4)
                nc.vector.tensor_copy(moments[:, 0, :], mv[:, :, 0]).then_inc(step, 1)
                nc.vector.tensor_tensor(msq[:], mv[:, :, 0], mv[:, :, 0], ALU.mult).then_inc(step, 1)
                dve.wait_ge(step, 6)
                nc.vector.tensor_tensor(moments[:, 1, :], mv[:, :, 1], msq[:], ALU.add).then_inc(step, 1)
                dve.wait_ge(averaged_done, 1)
                nc.vector.tensor_copy(group[:], averaged[:]).then_inc(step, 1)
                dve.wait_ge(step, 8)
                nc.vector.tensor_tensor(msq[:], group[:, 0, :], group[:, 0, :], ALU.mult).then_inc(step, 1)
                dve.wait_ge(step, 9)
                nc.vector.tensor_tensor(var[:], group[:, 1, :], msq[:], ALU.subtract).then_inc(var_done, 1)
                dve.wait_ge(rstd_done, 1)
                nc.vector.scalar_tensor_tensor(out=shift[:], in0=group[:, 0, :], scalar=-1.0, in1=scale[:],
                                               op0=ALU.mult, op1=ALU.mult).then_inc(step, 1)
                dve.wait_ge(step, 10)

            @block.tensor
            def _(pe):
                pe.wait_ge(member_done, 3)
                pe.wait_ge(step, 7)
                nc.tensor.matmul(averaged[:].rearrange("p a b -> p (a b)"), member[:],
                                 moments[:].rearrange("p a b -> p (a b)"), start=True, stop=True).then_inc(averaged_done, 1)

            @block.scalar
            def _(act):
                nc.scalar.preload_act_table_set("natural_log_exp_and_others")
                act.wait_ge(var_done, 1)
                nc.scalar.activation(var[:], var[:], ACT.Ln, bias=const.eps[:, 0:1]).then_inc(log_done, 1)
                act.wait_ge(log_done, 1)
                nc.scalar.activation(scale[:], var[:], ACT.Exp, scale=-0.5).then_inc(rstd_done, 1)


def build_layer_norm(nc, const, name, dst, affine=None, src=None, project=None, extra=False,
                     keep=None):
    SLOTS = 4
    with Part(nc, name) as part:
        if src is not None or affine is not None:
            tin = part.sb("in", [CH, SLOTS, TILE])
        square = part.sb("square", [CH, SLOTS, TILE])
        logv = part.sb("logv", [CH, SLOTS, TILE])
        rstd = part.sb("rstd", [CH, SLOTS, TILE])
        if keep is None:
            normed = part.sb("normed", [CH, SLOTS, TILE])
        centred = part.ps("centred", [CH, SLOTS, TILE])
        variance = part.ps("variance", [CH, 2, TILE])
        projected = part.ps("projected", [CH, 2, TILE])
        (in_ready, centre_done, square_done, var_done, log_done, rstd_done, normed_done,
         projected_done, added) = sems = part.sems(
            "in_ready centre_done square_done var_done log_done rstd_done normed_done projected_done added")
        in_loaded = [part.sem(f"in_loaded{k}") for k in range(SLOTS)]
        stored = [part.sem(f"stored{k}") for k in range(SLOTS)]
        prime(nc, (*sems, *stored))
        TURNS = NT // SLOTS

        with nc.Block() as block:
            @block.sync
            def _(sp):
                if src is not None:
                    with sp.Fori(0, TURNS) as i:
                        for k in range(SLOTS):
                            t = SLOTS * i + k
                            sp.wait_ge(centre_done, LEAD + t - (SLOTS - 1))
                            sp.dma_start(tin[:, k, :], src[:, chunk(t)]).then_inc(in_loaded[k], 16)
                if dst is not None:
                    with sp.Fori(0, TURNS) as i:
                        for k in range(SLOTS):
                            t = SLOTS * i + k
                            sp.wait_ge(normed_done, LEAD + t + 1)
                            sp.dma_start(dst[:, chunk(t)], normed[:, k, :]).then_inc(stored[k], 16)
                    if extra:
                        sp.dma_start(dst[:, chunk(NT)], normed[:, SLOTS - 1, :]).then_inc(stored[SLOTS - 1], 16)
                    for k in range(SLOTS):
                        sp.wait_ge(stored[k], LEAD + 16 * (TURNS + int(extra and k == SLOTS - 1)))

            @block.tensor
            def _(pe):
                with pe.Fori(0, TURNS) as i:
                    for k in range(SLOTS):
                        t = SLOTS * i + k
                        if src is not None:
                            pe.wait_ge(in_loaded[k], 16 * (i + 1))
                            rhs = tin[:, k, :]
                        elif affine is not None:
                            pe.wait_ge(in_ready, LEAD + t + 1)
                            rhs = tin[:, k, :]
                        else:
                            rhs = const.x[:, chunk(t)]
                        pe.wait_ge(normed_done, LEAD + t - (SLOTS - 1))
                        nc.tensor.matmul(centred[:, k, :], const.center[:], rhs, start=True, stop=True
                                         ).then_inc(centre_done, 1)
                    for k in range(SLOTS):
                        t = SLOTS * i + k
                        pe.wait_ge(square_done, LEAD + t + 1)
                        pe.wait_ge(log_done, LEAD + t - 1)
                        nc.tensor.matmul(variance[:, k % 2, :], const.mean[:], square[:, k, :], start=True, stop=True
                                         ).then_inc(var_done, 1)
                    if project is not None:
                        for k in range(SLOTS):
                            t = SLOTS * i + k
                            pe.wait_ge(normed_done, LEAD + t + 1)
                            pe.wait_ge(added, LEAD + t - 1)
                            nc.tensor.matmul(projected[:, k % 2, :], project[0][:], normed[:, k, :], start=True,
                                             stop=True).then_inc(projected_done, 1)

            @block.scalar
            def _(act):
                nc.scalar.preload_act_table_set("natural_log_exp_and_others")
                with act.Fori(0, TURNS) as i:
                    for k in range(SLOTS):
                        t = SLOTS * i + k
                        act.wait_ge(centre_done, LEAD + t + 1)
                        act.wait_ge(var_done, LEAD + t - (SLOTS - 1))
                        nc.scalar.activation(square[:, k, :], centred[:, k, :], ACT.Square).then_inc(square_done, 1)
                    for k in range(SLOTS):
                        t = SLOTS * i + k
                        act.wait_ge(var_done, LEAD + t + 1)
                        act.wait_ge(rstd_done, LEAD + t - (SLOTS - 1))
                        nc.scalar.activation(logv[:, k, :], variance[:, k % 2, :], ACT.Ln, bias=const.eps[:, 0:1]
                                             ).then_inc(log_done, 1)
                        act.wait_ge(log_done, LEAD + t + 1)
                        act.wait_ge(normed_done, LEAD + t - (SLOTS - 1))
                        nc.scalar.activation(rstd[:, k, :], logv[:, k, :], ACT.Exp, scale=-0.5).then_inc(rstd_done, 1)

            @block.vector
            def _(dve):
                with dve.Fori(0, BATCH) as b, dve.Fori(0, TPB // SLOTS) as j:
                    i = b * (TPB // SLOTS) + j
                    if affine is not None:
                        scale, shift = affine
                        for k in range(SLOTS):
                            t = SLOTS * i + k
                            dve.wait_ge(centre_done, LEAD + t - (SLOTS - 1))
                            nc.vector.tensor_scalar(tin[:, k, :], const.x[:, chunk(t)], scale[:, bass.ds(b, 1)],
                                                    shift[:, bass.ds(b, 1)], ALU.mult, ALU.add).then_inc(in_ready, 1)
                    for k in range(SLOTS):
                        t = SLOTS * i + k
                        dve.wait_ge(rstd_done, LEAD + t + 1)
                        dve.wait_ge(centre_done, LEAD + t + 1)
                        if dst is not None:
                            dve.wait_ge(stored[k], LEAD + 16 * i)
                        if project is not None:
                            dve.wait_ge(projected_done, LEAD + t - (SLOTS - 1))
                        nc.vector.tensor_tensor(normed[:, k, :] if keep is None else keep[:, chunk(t)], centred[:, k, :], rstd[:, k, :],
                                                ALU.mult).then_inc(normed_done, 1)
                    if project is not None:
                        for k in range(SLOTS):
                            t = SLOTS * i + k
                            dve.wait_ge(projected_done, LEAD + t + 1)
                            nc.vector.scalar_tensor_tensor(
                                out=const.x[:, chunk(t)], in0=projected[:, k % 2, :], scalar=project[1][:, 0:1],
                                in1=const.x[:, chunk(t)], op0=ALU.add, op1=ALU.add).then_inc(added, 1)


def build_transposes(nc, name, const, jobs, after=0, loaded=None):
    with Part(nc, name) as part:
        tile = part.ps("tile", [CH, 2, TILE])
        transposed, copied = part.sems("transposed copied")
        prime(nc, (copied,))
        with nc.Block() as block:
            @block.tensor
            def _(pe):
                for n, (out, src, _) in enumerate(jobs):
                    rows, cols = src.shape[0], src.shape[1]
                    pe.wait_ge(copied, LEAD + n - 1)
                    nc.tensor.transpose(tile[0:cols, n % 2, 0:rows], src, const.ident[0:rows, 0:rows]
                                        ).then_inc(transposed, 1)

            @block.vector
            def _(dve):
                for n, (out, src, scalar) in enumerate(jobs):
                    rows, cols = src.shape[0], src.shape[1]
                    dve.wait_ge(transposed, n + 1)
                    if scalar is None:
                        nc.vector.tensor_copy(out, tile[0:cols, n % 2, 0:rows]).then_inc(copied, 1)
                    else:
                        nc.vector.tensor_scalar(out, tile[0:cols, n % 2, 0:rows], scalar, None, ALU.mult
                                                ).then_inc(copied, 1)


def build_mamba(nc, const, w, normed_dram, mixed_dram, wp_t, bp):
    DI, NS, RANK, TAPS, GROUP = 256, 16, 8, 4, 8
    HALVES, CPG = DI // CH, CH // GROUP
    STEPS = 2 * NS
    AHEAD = 4
    CAP = 40.0
    ALMOST_ONE = 1.0 - 2.0 ** -23
    with Part(nc, "m") as part:
        win_t = [part.sb(f"win_t{v}", [CH, 2 * DI]) for v in range(2)]
        wx_t = part.sb("wx_t", [CH, HALVES, CH])
        wdt_t = part.sb("wdt_t", [RANK, DI])
        wout_t = part.sb("wout_t", [CH, HALVES, CH])
        skip_t = part.sb("skip_t", [CH, CH])
        pick = part.sb("pick", [CH, 2 * NS], BF16)
        taps = part.sb("taps", [CH, HALVES, TAPS])
        conv_b = part.sb("conv_b", [CH, HALVES])
        dt_b = part.sb("dt_b", [CH, HALVES])
        decay = part.sb("decay", [CH, HALVES, NS])
        d_skip = part.sb("d_skip", [CH, HALVES])
        in_b = part.sb("in_b", [CH, 2 * HALVES])
        out_b = part.sb("out_b", [CH, 1])
        keep = part.sb("keep", [CH, NT + 1])
        almost_one = part.sb("almost_one", [CH, 1])
        keep_now = part.sb("keep_now", [CH, 1])

        with Part(nc, "mw") as pre:
            win = pre.sb("win", [CH, 4, CH])
            win_p = pre.sb("win_p", [CH, 4, CH])
            win_raw_t = pre.sb("win_raw_t", [CH, 4 * CH])
            wx = pre.sb("wx", [RANK + 2 * NS, DI])
            wx_half_t = pre.sb("wx_half_t", [CH, HALVES, RANK + 2 * NS])
            wout = pre.sb("wout", [CH, DI])
            wp = pre.sb("wp", [CH, CH])
            wp_raw_t = pre.sb("wp_raw_t", [CH, CH])
            a_log = pre.sb("a_log", [CH, HALVES, NS])
            gamma = pre.sb("gamma", [CH, 2])
            beta = pre.sb("beta", [CH, 1])
            b_p = pre.sb("b_p", [CH, 1])
            s_row = pre.sb("s_row", [1, 2])
            ones_row = pre.sb("ones_row", [1, CH])
            s_col = pre.sb("s_col", [CH, 2])
            gs = pre.sb("gs", [CH, 2])
            regroup = pre.sb("regroup", [CH, CH])
            s_sum = pre.sb("s_sum", [CH, 1])
            s_ps = pre.ps("s_ps", [CH, 2])
            b_ps = pre.ps("b_ps", [CH, 8])
            loaded, made, step, exp_done, mm_done, pe_go = pre.sems("loaded made step exp_done mm_done pe_go")
            with nc.Block() as block:
                @block.sync
                def _(sp):
                    with nc.allow_non_contiguous_dma("small weights"):
                        n = 0
                        for dst, src in (
                                (win[:], w["W_in"].rearrange("(t p) c -> p t c", p=CH)),
                                (wx[:], w["W_x"]), (wout[:], w["W_out"]), (wp[:], w["W_p"]),
                                (wdt_t[:], w["W_dt"].rearrange("d r -> r d")),
                                (a_log[:], w["A_log"].rearrange("(h p) n -> p h n", p=CH)),
                                (taps[:], w["conv_w"].rearrange("(h p) o k -> p h (o k)", p=CH)),
                                (conv_b[:], half_columns(w["conv_b"])), (dt_b[:], half_columns(w["b_dt"])),
                                (d_skip[:], half_columns(w["D_skip"])),
                                (gamma[:, 0:1], column(w["gamma"])), (beta[:], column(w["beta"])),
                                (b_p[:], column(w["b_p"])), (s_row[0:1, 0:1], column(w["s1"])),
                                (s_row[0:1, 1:2], column(w["s2"]))):
                            sp.dma_start(dst, src).then_inc(loaded, 16)
                            n += 1
                        for g in range(GROUP):
                            sp.dma_start(gamma[g * CPG:(g + 1) * CPG, 1:2],
                                         w["gamma"].rearrange("(a b n) -> b a n", b=GROUP, n=1)[g]).then_inc(loaded, 16)
                            n += 1
                        sp.wait_ge(loaded, 16 * n)

                @block.gpsimd
                def _(pool):
                    nc.gpsimd.memset(ones_row[:], 1.0).then_inc(made, 1)
                    nc.gpsimd.memset(pick[:], 0.0).then_inc(made, 1)
                    nc.gpsimd.memset(keep[:], 1.0).then_inc(made, 1)
                    nc.gpsimd.memset(wx_t[:], 0.0).then_inc(made, 1)
                    nc.gpsimd.memset(almost_one[:], ALMOST_ONE).then_inc(made, 1)
                    pool.wait_ge(made, 5)
                    for n, base in enumerate((0, 64, 96)):
                        nc.gpsimd.affine_select(out=pick[:], in_=pick[:], compare_op=ALU.not_equal, fill=1.0,
                                                base=-base, pattern=[[-1, 2 * NS]],
                                                channel_multiplier=1).then_inc(made, 1)
                        pool.wait_ge(made, 6 + n)
                    nc.gpsimd.memset(keep[:, 0:NT + 1:TPB], 0.0).then_inc(made, 1)
                    pool.wait_ge(made, 9)

            jobs = [(win_raw_t[:, chunk(i, CH)], win[:, i, :], None) for i in range(4)]
            jobs += [(win_t[0][:, chunk(i, CH)], win[:, i, :], gamma[:, 0:1]) for i in range(4)]
            jobs += [(win_t[1][:, chunk(i, CH)], win_p[:, i, :], gamma[:, 1:2]) for i in range(4)]
            jobs += [(wx_half_t[:, h, :], wx[:, chunk(h, CH)], None) for h in range(HALVES)]
            jobs += [(wout_t[:, h, :], wout[:, chunk(h, CH)], None) for h in range(HALVES)]
            jobs += [(wp_raw_t[:], wp[:], None), (wp_t[:], wp[:], gamma[:, 0:1])]
            with nc.Block() as block:
                @block.vector
                def _(dve):
                    for i in range(4):
                        nc.vector.tensor_copy(win_p[:, i, :].rearrange("o (b a) -> o b a", b=GROUP),
                                              win[:, i, :].rearrange("o (a b) -> o b a", b=GROUP)).then_inc(step, 1)
                    nc.vector.tensor_copy(regroup[:].rearrange("c (a b) -> c a b", b=GROUP),
                                          const.ident[:].rearrange("c (b a) -> c a b", b=GROUP)).then_inc(step, 1)
                    dve.wait_ge(step, 5)
            build_transposes(nc, "mt", const, jobs)
            with nc.Block() as block:
                @block.tensor
                def _(pe):
                    nc.tensor.matmul(s_ps[:], ones_row[0:1, :], s_row[0:1, :], start=True, stop=True).then_inc(mm_done, 1)
                    for i in range(4):
                        nc.tensor.matmul(b_ps[:, i:i + 1], win_raw_t[:, chunk(i, CH)], beta[:],
                                         start=True, stop=True).then_inc(mm_done, 1)
                    nc.tensor.matmul(b_ps[:, 4:5], wp_raw_t[:], beta[:], start=True, stop=True).then_inc(mm_done, 1)

                @block.scalar
                def _(act):
                    nc.scalar.activation(decay[:], a_log[:], ACT.Exp).then_inc(exp_done, 1)

                @block.vector
                def _(dve):
                    n = 5

                    def after_last():
                        dve.wait_ge(step, n)

                    for h in range(HALVES):
                        nc.vector.tensor_copy(wx_t[:, h, RANK * 4:RANK * 5], wx_half_t[:, h, 0:RANK]).then_inc(step, 1)
                        for at in (0, 64, 96):
                            nc.vector.tensor_copy(wx_t[:, h, at:at + 2 * NS], wx_half_t[:, h, RANK:]).then_inc(step, 1)
                    dve.wait_ge(mm_done, 6)
                    nc.vector.tensor_copy(s_col[:], s_ps[:]).then_inc(step, 1)
                    nc.vector.tensor_copy(in_b[:], b_ps[:, 0:4]).then_inc(step, 1)
                    nc.vector.tensor_tensor(bp[:], b_ps[:, 4:5], b_p[:], ALU.add).then_inc(step, 1)
                    n += 8 + 3
                    after_last()
                    nc.vector.tensor_tensor(gs[:], gamma[:], s_col[:], ALU.mult).then_inc(step, 1)
                    nc.vector.tensor_tensor(s_sum[:], s_col[:, 0:1], s_col[:, 1:2], ALU.add).then_inc(step, 1)
                    n += 2
                    after_last()
                    nc.vector.tensor_tensor(out_b[:], s_sum[:], beta[:], ALU.mult).then_inc(step, 1)
                    nc.vector.tensor_scalar(regroup[:], regroup[:], gs[:, 1:2], None, ALU.mult).then_inc(step, 1)
                    n += 2
                    after_last()
                    nc.vector.scalar_tensor_tensor(out=skip_t[:], in0=const.ident[:], scalar=gs[:, 0:1],
                                                   in1=regroup[:], op0=ALU.mult, op1=ALU.add).then_inc(step, 1)
                    dve.wait_ge(exp_done, 1)
                    nc.vector.tensor_scalar(decay[:], decay[:], -1.0, None, ALU.mult).then_inc(step, 1)
                    n += 2
                    after_last()

        normed = [part.sb(f"normed{v}", [CH, TILE]) for v in range(2)]
        xi = [part.sb(f"xi{v}", [CH, HALVES, TAPS - 1 + TILE]) for v in range(2)]
        conv = part.sb("conv", [CH, HALVES, TILE])
        u = [part.sb(f"u{v}", [CH, HALVES, TILE]) for v in range(2)]
        gate = [part.sb(f"gate{v}", [CH, HALVES, TILE]) for v in range(2)]
        bc = [part.sb(f"bc{v}", [CH, TILE], BF16) for v in range(2)]
        rest = part.sb("rest", [CH, TILE])
        dtr = rest[0:RANK, :]
        dt = [part.sb(f"dt{v}", [CH, HALVES, TILE]) for v in range(2)]
        dtu = [part.sb(f"dtu{v}", [CH, HALVES, TILE]) for v in range(2)]
        soft = part.sb("soft", [CH, TILE])
        second = soft
        soft_small = part.sb("soft_small", [CH, TILE])
        soft_log = part.sb("soft_log", [CH, TILE])
        driven = part.sb("driven", [CH, 4, TILE])
        fade = part.sb("fade", [CH, AHEAD, HALVES, TILE])
        state = part.sb("state", [CH, AHEAD, HALVES, TILE])
        seen = part.sb("seen", [CH, AHEAD, HALVES, TILE])
        c_wide = part.sb("c_wide", [CH, AHEAD, TILE])
        carried = [part.sb(f"carried{v}", [CH, HALVES, NS]) for v in range(2)]
        gated = [part.sb(f"gated{v}", [CH, HALVES, TILE]) for v in range(2)]
        again = part.sb("again", [CH, TILE])
        y_ps = [[part.ps(f"y_ps{v}{h}", [CH, TILE]) for h in range(HALVES)] for v in range(2)]
        b_ps = [part.ps(f"b_ps{k}", [CH, TILE]) for k in range(2)]
        c_ps = part.ps("c_ps", [CH, TILE])
        pre_ps = part.ps("pre_ps", [CH, TILE])

        (pre_filled, pre_drained, tail_done, xi_done, tap0_done, tap1_done, conv_step, conv_done, u_done, gate_done,
         split_done, bc_done, dtr_done, cap_done, soft_step, dt_done, dtu_done,
         b_wide, c_bank, c_copied, fade_done, driven_done, scan_done, carried_done, seen_done, y_done,
         skipped_done, gated_done, mixed_done, keep_done, small_done) = sems = part.sems(
            "pre_filled pre_drained tail_done xi_done tap0_done tap1_done conv_step conv_done u_done gate_done "
            "split_done bc_done dtr_done cap_done soft_step dt_done dtu_done "
            "b_wide c_bank c_copied fade_done driven_done scan_done carried_done seen_done y_done "
            "skipped_done gated_done mixed_done keep_done small_done")
        normed_loaded = part.sems("normed_loaded0 normed_loaded1")
        cleared, mixed_stored, again_loaded = part.sems("cleared mixed_stored again_loaded")
        prime(nc, (*sems, mixed_stored))

        XI, Z, XDBL, DT, OUT = 0, 2, 4, 5, 7
        WAYS = 7

        def fill(it, v, k):
            if it is None:
                return k
            if isinstance(it, int) and it == 0:
                return WAYS + (WAYS if v else 0) + k
            return 3 * WAYS + (it - 1) * (2 * WAYS + 1) + (WAYS + 1 if v else 0) + k

        def over_tiles(eng, tile):
            tile(0, True)
            with eng.Fori(1, NT) as it:
                tile(it, False)

        with nc.Block() as block:
            @block.sync
            def _(sp):
                def load(v, t, r):
                    sp.wait_ge(gate_done, LEAD + 2 * (r - 1))
                    sp.dma_start(normed[v][:], normed_dram[:, chunk(t)]).then_inc(normed_loaded[v], 16)

                def finish(t):
                    sp.wait_ge(mixed_done, LEAD + t + 1)
                    sp.dma_start(mixed_dram[:, chunk(t)], again[:]).then_inc(mixed_stored, 16)
                    sp.wait_ge(mixed_stored, LEAD + 16 * (t + 1))

                def tile(it, first):
                    load(1, it, 2 * it + 1)
                    load(0, it + 1, 2 * it + 2)
                    if not first:
                        finish(it - 1)
                    sp.dma_start(again[:], normed_dram[:, chunk(it)]).then_inc(again_loaded, 16)

                load(0, 0, 0)
                over_tiles(sp, tile)
                finish(NT - 1)

            @block.tensor
            def _(pe):
                def into_pre(it, v, k, pairs, rows=CH):
                    pe.wait_ge(pre_drained, LEAD + fill(it, v, k))
                    for n, (lhs, rhs) in enumerate(pairs):
                        last = nc.tensor.matmul(pre_ps[0:rows, :], lhs, rhs, start=(n == 0), stop=(n == len(pairs) - 1))
                    last.then_inc(pre_filled, 1)

                def prepare(n, it, v, r):
                    b = r % 2 if it is None else 1 - v
                    if n == 0:
                        pe.wait_ge(normed_loaded[b], 16 * ((r // 2 if it is None else (it if b else it + 1)) + 1))
                    if n in (0, 1):
                        into_pre(it, v, XI + n, [(win_t[b][:, chunk(n, CH)], normed[b][:])])
                    if n in (5, 6):
                        into_pre(it, v, Z + n - 5, [(win_t[b][:, chunk(2 + n - 5, CH)], normed[b][:])])
                    if n == 7:
                        pe.wait_ge(u_done, LEAD + 2 * (r + 1))
                        into_pre(it, v, XDBL, [(wx_t[:, h, :], u[b][:, h, :]) for h in range(HALVES)])
                    if n in (9, 11):
                        pe.wait_ge(dtr_done, LEAD + r + 1)
                        h = (n - 9) // 2
                        into_pre(it, v, DT + h, [(wdt_t[:, chunk(h, CH)], dtr)])

                def widen_b(n, b, r):
                    s = r * NS + n
                    if n == 0:
                        pe.wait_ge(bc_done, LEAD + r + 1)
                    pe.wait_ge(driven_done, LEAD + 2 * (s - 1))
                    nc.tensor.matmul(b_ps[n % 2][:], pick[:, n:n + 1].to_broadcast([CH, CH]), bc[b][:], start=True, stop=True).then_inc(b_wide, 1)

                def widen_c(n, b, r):
                    pe.wait_ge(c_copied, LEAD + r * NS + n)
                    nc.tensor.matmul(c_ps[:], pick[:, NS + n:NS + n + 1].to_broadcast([CH, CH]), bc[b][:],
                                     start=True, stop=True).then_inc(c_bank, 1)

                def sum_states(n, v, q):
                    for h in range(HALVES):
                        hs = q * STEPS + 2 * n + h
                        if n == 0:
                            pe.wait_ge(skipped_done, LEAD + 2 * (q - 2) + h + 1)
                        pe.wait_ge(seen_done, LEAD + hs + 1)
                        nc.tensor.matmul(y_ps[v][h][:], const.ident[:], seen[:, n % AHEAD, h, :],
                                         start=(n == 0), stop=(n == NS - 1)).then_inc(y_done, 1)

                for n in range(NS):
                    prepare(n, None, 0, 0)
                def finish(t, it):
                    pe.wait_ge(gated_done, LEAD + 4 * (t + 1))
                    pe.wait_ge(again_loaded, 16 * (t + 1))
                    into_pre(it, 0, OUT, [(wout_t[:, h, :], gated[b][:, h, :]) for b in range(2) for h in range(HALVES)]
                             + [(skip_t[:], again[:])])

                def tile(it, first):
                    for v in range(2):
                        q = 2 * it + v
                        for n in range(NS):
                            prepare(n, it, v, q + 1)
                            if n < NS - 2:
                                widen_b(n + 2, v, q)
                            else:
                                widen_b(n + 2 - NS, 1 - v, q + 1)
                            if n >= 2:
                                sum_states(n - 2, v, q)
                            elif v or not first:
                                sum_states(NS + n - 2, 1 - v, q - 1)
                            if n < NS - 3:
                                widen_c(n + 3, v, q)
                            else:
                                widen_c(n + 3 - NS, 1 - v, q + 1)
                            if n == 14 and v == 0 and not first:
                                finish(it - 1, it)

                for n in range(2):
                    widen_b(n, 0, 0)
                for n in range(3):
                    widen_c(n, 0, 0)
                over_tiles(pe, tile)
                sum_states(NS - 2, 1, 2 * NT - 1)
                sum_states(NS - 1, 1, 2 * NT - 1)
                pe.wait_ge(pre_drained, LEAD + fill(NT, 0, 0))
                pe.wait_ge(gated_done, LEAD + 4 * NT)
                pe.wait_ge(again_loaded, 16 * NT)
                last_pairs = [(wout_t[:, h, :], gated[b][:, h, :]) for b in range(2) for h in range(HALVES)]
                for n, (lhs, rhs) in enumerate(last_pairs + [(skip_t[:], again[:])]):
                    last = nc.tensor.matmul(pre_ps[:], lhs, rhs, start=(n == 0), stop=(n == len(last_pairs)))
                last.then_inc(pre_filled, 1)

            @block.scalar
            def _(act):
                def prepare(n, it, v, r):
                    b = r % 2 if it is None else 1 - v
                    if n in (0, 1):
                        if n == 0:
                            act.wait_ge(tail_done, LEAD + r + 1)
                        act.wait_ge(pre_filled, LEAD + fill(it, v, XI + n) + 1)
                        nc.scalar.activation(xi[b][:, n, TAPS - 1:], pre_ps[:], ACT.Identity, bias=in_b[:, n:n + 1]
                                             ).then_inc(pre_drained, 1)
                        act.wait_ge(pre_drained, LEAD + fill(it, v, XI + n) + 1)
                        act.wait_ge(u_done, LEAD + 2 * (r - 1) + n + 1)
                        nc.scalar.activation(conv[:, n, :], xi[b][:, n, 0:TILE], ACT.Identity,
                                             bias=conv_b[:, n:n + 1], scale=taps[:, n, 0:1]).then_inc(tap0_done, 1)
                        act.wait_ge(dt_done, LEAD + 2 * r)
                        act.wait_ge(tap1_done, LEAD + 2 * r + n)
                        nc.scalar.activation(second[:], xi[b][:, n, 1:1 + TILE], ACT.Copy, scale=taps[:, n, 1:2]
                                             ).then_inc(tap0_done, 1)
                    if n in (5, 6):
                        h = n - 5
                        act.wait_ge(pre_filled, LEAD + fill(it, v, Z + h) + 1)
                        act.wait_ge(gated_done, LEAD + 2 * (r - 1))
                        if n == 5:
                            nc.scalar.activation(gate[b][:, 0, :], pre_ps[:], ACT.Identity, bias=in_b[:, 2:3]
                                                 ).then_inc(pre_drained, 1)
                            act.wait_ge(pre_drained, LEAD + fill(it, v, Z) + 1)
                            return
                        act.wait_ge(skipped_done, LEAD + 2 * (r - 1))
                        act.wait_ge(dtu_done, LEAD + 2 * (r - 1))
                        act.wait_ge(conv_done, LEAD + 2 * r + 2)
                        nc.scalar.activation(gate[b][:, 1, :], pre_ps[:], ACT.Silu, bias=in_b[:, 3:4]
                                             ).then_inc(pre_drained, 1)
                        for h in range(HALVES):
                            nc.scalar.activation(u[b][:, h, :], conv[:, h, :], ACT.Silu).then_inc(u_done, 1)
                        nc.scalar.activation(gate[b][:, 0, :], gate[b][:, 0, :], ACT.Silu).then_inc(gate_done, 1)
                        act.wait_ge(pre_drained, LEAD + fill(it, v, Z + 1) + 1)
                        act.sem_inc(gate_done, 1)
                        if it is not None:
                            nc.scalar.preload_act_table_set("natural_log_exp_and_others")
                    if n == 7:
                        act.wait_ge(pre_filled, LEAD + fill(it, v, XDBL) + 1)
                        act.wait_ge(dt_done, LEAD + 2 * r)
                        nc.scalar.activation(dtr, pre_ps[4 * RANK:5 * RANK, :], ACT.Copy).then_inc(dtr_done, 1)
                        act.wait_ge(c_bank, LEAD + NS * (r - 1))
                        nc.scalar.activation(bc[b][:], pre_ps[:], ACT.Copy).then_inc(split_done, 1)
                    if n in (9, 11):
                        h = (n - 9) // 2
                        act.wait_ge(cap_done, LEAD + 2 * r + h + 1)
                        nc.scalar.activation(soft[:], soft[:], ACT.Exp).then_inc(soft_step, 1)
                        act.wait_ge(soft_step, LEAD + 3 * (2 * r + h) + 1)
                        nc.scalar.activation(soft_small[:], soft[:], ACT.Exp, scale=-0.5).then_inc(soft_step, 1)
                        nc.scalar.activation(soft_log[:], soft[:], ACT.Ln, bias=almost_one[:, 0:1]).then_inc(soft_step, 1)

                def decays(n, v, q):
                    for h in range(HALVES):
                        hs = q * STEPS + 2 * n + h
                        if n == 0:
                            act.wait_ge(dt_done, LEAD + 2 * q + h + 1)
                        act.wait_ge(scan_done, LEAD + hs - (2 * AHEAD - 1))
                        nc.scalar.activation(fade[:, n % AHEAD, h, :], dt[v][:, h, :], ACT.Exp, scale=decay[:, h, n:n + 1]
                                             ).then_inc(fade_done, 1)

                def copy_c(n, q):
                    s = q * NS + n
                    act.wait_ge(c_bank, LEAD + s + 1)
                    act.wait_ge(seen_done, LEAD + 2 * (s - AHEAD + 1))
                    nc.scalar.activation(c_wide[:, n % AHEAD, :], c_ps[:], ACT.Copy).then_inc(c_copied, 1)

                def carry(n, v, q):
                    act.wait_ge(scan_done, LEAD + q * STEPS + 2 * n + 2)
                    if v == 0 and n == 0:
                        act.wait_ge(keep_done, LEAD + (q // 2 if isinstance(q, int) else turn[0]) + 1)
                    nc.scalar.activation(carried[v][:, :, n:n + 1], state[:, n % AHEAD, :, TILE - 1:TILE],
                                         ACT.Copy, scale=keep_now[:, 0:1]).then_inc(carried_done, 1)

                def finish(t, it):
                    act.wait_ge(pre_filled, LEAD + fill(it, 0, OUT) + 1)
                    act.wait_ge(mixed_stored, LEAD + 16 * t)
                    nc.scalar.activation(again[:], pre_ps[:], ACT.Identity, bias=out_b[:, 0:1]).then_inc(pre_drained, 1)
                    act.wait_ge(pre_drained, LEAD + fill(it, 0, OUT) + 1)
                    act.sem_inc(mixed_done, 1)

                turn = [None]

                def tile(it, first):
                    turn[0] = it
                    for v in range(2):
                        q = 2 * it + v
                        for n in range(NS):
                            if n < NS - 3:
                                decays(n + 3, v, q)
                            else:
                                decays(n + 3 - NS, 1 - v, q + 1)
                            if n < NS - 2:
                                copy_c(n + 2, q)
                            else:
                                copy_c(n + 2 - NS, q + 1)
                            if n >= 2:
                                carry(n - 2, v, q)
                            elif v or not first:
                                carry(NS + n - 2, 1 - v, q - 1)
                            prepare(n, it, v, q + 1)
                            if n == 14 and v == 0 and not first:
                                finish(it - 1, it)

                for n in range(NS):
                    prepare(n, None, 0, 0)
                nc.scalar.preload_act_table_set("natural_log_exp_and_others")
                for n in range(3):
                    decays(n, 0, 0)
                for n in range(2):
                    copy_c(n, 0)
                over_tiles(act, tile)
                for n in (NS - 2, NS - 1):
                    carry(n, 1, 2 * NT - 1)
                act.wait_ge(pre_filled, LEAD + fill(NT, 0, 0) + 1)
                act.wait_ge(mixed_stored, LEAD + 16 * (NT - 1))
                nc.scalar.activation(again[:], pre_ps[:], ACT.Identity, bias=out_b[:, 0:1]).then_inc(mixed_done, 1)

            @block.vector
            def _(dve):
                def prepare(n, it, v, r):
                    b = r % 2 if it is None else 1 - v
                    if n == 0 and it is not None:
                        dve.wait_ge(conv_done, LEAD + 2 * r)
                        t = it if b else it + 1
                        nc.vector.tensor_scalar(xi[b][:, :, 0:TAPS - 1], xi[b][:, :, TILE:TILE + TAPS - 1],
                                                keep[:, bass.ds(t, 1)], None, ALU.mult).then_inc(tail_done, 1)
                    if n in (2, 3):
                        h = n - 2
                        dve.wait_ge(tap1_done, LEAD + 2 * r + h + 1)
                        for k in range(2, TAPS):
                            if k > 2:
                                dve.wait_ge(conv_step, LEAD + (2 * r + h) * (TAPS - 3) + k - 2)
                            done = conv_step if k < TAPS - 1 else conv_done
                            nc.vector.scalar_tensor_tensor(
                                out=conv[:, h, :], in0=xi[b][:, h, k:k + TILE], scalar=taps[:, h, k:k + 1],
                                in1=conv[:, h, :], op0=ALU.mult, op1=ALU.add).then_inc(done, 1)
                    if n == 8:
                        dve.wait_ge(split_done, LEAD + 3 * r + 1)
                        nc.vector.tensor_tensor(rest[64:128, :], pre_ps[64:128, :], bc[b][64:128, :], ALU.subtract
                                                ).then_inc(pre_drained, 1)
                        dve.wait_ge(pre_drained, LEAD + fill(it, v, XDBL) + 1)
                        nc.vector.tensor_copy(bc[b][64:128, :], rest[64:128, :]).then_inc(split_done, 1)
                        dve.wait_ge(split_done, LEAD + 3 * r + 2)
                        nc.vector.tensor_tensor(bc[b][96:128, :], rest[96:128, :], bc[b][96:128, :], ALU.subtract
                                                ).then_inc(split_done, 1)
                        dve.wait_ge(split_done, LEAD + 3 * r + 3)
                        dve.sem_inc(bc_done, 1)
                    if n in (9, 11):
                        h = (n - 9) // 2
                        dve.wait_ge(pre_filled, LEAD + fill(it, v, DT + h) + 1)
                        dve.wait_ge(dt_done, LEAD + 2 * r + h)
                        nc.vector.tensor_scalar(soft[:], pre_ps[:], dt_b[:, h:h + 1], CAP, ALU.add, ALU.min
                                                ).then_inc(cap_done, 1)
                    if n in (10, 12):
                        h = (n - 10) // 2
                        dve.wait_ge(soft_step, LEAD + 3 * (2 * r + h) + 3)
                        dve.wait_ge(fade_done, LEAD + STEPS * (r - 1))
                        dve.wait_ge(dtu_done, LEAD + 2 * (r - 1))
                        nc.vector.scalar_tensor_tensor(out=dt[b][:, h, :], in0=pre_ps[:], scalar=dt_b[:, h:h + 1],
                                                       in1=soft_log[:], op0=ALU.add, op1=ALU.max).then_inc(pre_drained, 1)
                        dve.wait_ge(pre_drained, LEAD + fill(it, v, DT + h) + 1)
                        dve.wait_ge(small_done, LEAD + 2 * r + h + 1)
                        nc.vector.tensor_tensor(dt[b][:, h, :], dt[b][:, h, :], soft_small[:], ALU.max
                                                ).then_inc(dt_done, 1)

                def scan(n, v, q):
                    s = q * NS + n
                    if n == 0:
                        dve.wait_ge(dtu_done, LEAD + 2 * (q + 1))
                    dve.wait_ge(b_wide, LEAD + s + 1)
                    for h in range(HALVES):
                        hs = q * STEPS + 2 * n + h
                        dve.wait_ge(scan_done, LEAD + hs - 3)
                        nc.vector.tensor_tensor(driven[:, (2 * n + h) % 4, :], dtu[v][:, h, :], b_ps[n % 2][:], ALU.mult
                                                ).then_inc(driven_done, 1)
                    for h in range(HALVES):
                        hs = q * STEPS + 2 * n + h
                        dve.wait_ge(fade_done, LEAD + hs + 1)
                        dve.wait_ge(driven_done, LEAD + hs + 1)
                        dve.wait_ge(seen_done, LEAD + hs - (2 * AHEAD - 1))
                        dve.wait_ge(carried_done, LEAD + s - (AHEAD - 1))
                        nc.vector.tensor_tensor_scan(state[:, n % AHEAD, h, :], fade[:, n % AHEAD, h, :],
                                                     driven[:, (2 * n + h) % 4, :], carried[v][:, h, n:n + 1],
                                                     ALU.mult, ALU.add).then_inc(scan_done, 1)

                for v in range(2):
                    nc.vector.memset(carried[v][:], 0.0).then_inc(cleared, 1)
                    nc.vector.memset(xi[v][:], 0.0).then_inc(cleared, 1)
                dve.wait_ge(cleared, 4)
                dve.sem_inc(tail_done, 1)
                for n in range(NS):
                    prepare(n, None, 0, 0)

                def finish(v, q, t):
                    for h in range(HALVES):
                        dve.wait_ge(y_done, LEAD + q * STEPS + STEPS)
                        dve.wait_ge(mixed_done, LEAD + t)
                        nc.vector.scalar_tensor_tensor(out=gated[v][:, h, :], in0=u[v][:, h, :],
                                                       scalar=d_skip[:, h:h + 1], in1=y_ps[v][h][:],
                                                       op0=ALU.mult, op1=ALU.add).then_inc(skipped_done, 1)

                def tile(it, first):
                    for v in range(2):
                        q = 2 * it + v
                        for n in range(NS):
                            scan(n, v, q)
                            if v == 0 and n == 1:
                                dve.wait_ge(carried_done, LEAD + 2 * NS * it)
                                nc.vector.tensor_scalar(keep_now[:], keep[:, bass.ds(it + 1, 1)], 1.0, None, ALU.mult
                                                        ).then_inc(keep_done, 1)
                            prepare(n, it, v, q + 1)
                            if n == 2 and (v or not first):
                                finish(1 - v, q - 1, it if v else it - 1)

                over_tiles(dve, tile)
                finish(1, 2 * NT - 1, NT - 1)

            @block.gpsimd
            def _(pool):
                def prepare(n, it, v, r):
                    b = r % 2 if it is None else 1 - v
                    if n in (1, 2):
                        h = n - 1
                        pool.wait_ge(tap0_done, LEAD + 2 * (2 * r + h + 1))
                        nc.gpsimd.tensor_tensor(conv[:, h, :], conv[:, h, :], second[:], ALU.add).then_inc(tap1_done, 1)
                    if n in (9, 11):
                        h = (n - 9) // 2
                        pool.wait_ge(soft_step, LEAD + 3 * (2 * r + h) + 3)
                        nc.gpsimd.tensor_tensor(soft_small[:], soft_small[:], soft[:], ALU.mult).then_inc(small_done, 1)
                    if n in (11, 13):
                        h = (n - 11) // 2
                        pool.wait_ge(dt_done, LEAD + 2 * r + h + 1)
                        pool.wait_ge(driven_done, LEAD + STEPS * (r - 1))
                        nc.gpsimd.tensor_tensor(dtu[b][:, h, :], dt[b][:, h, :], u[b][:, h, :], ALU.mult
                                                ).then_inc(dtu_done, 1)

                for n in range(NS):
                    prepare(n, None, 0, 0)

                def finish(v, q):
                    for h in range(HALVES):
                        pool.wait_ge(skipped_done, LEAD + 2 * q + h + 1)
                        pool.wait_ge(gate_done, LEAD + 2 * q + 2)
                        nc.gpsimd.tensor_tensor(gated[v][:, h, :], gated[v][:, h, :], gate[v][:, h, :], ALU.mult
                                                ).then_inc(gated_done, 1)

                def tile(it, first):
                    for v in range(2):
                        q = 2 * it + v
                        for n in range(NS):
                            pool.wait_ge(c_copied, LEAD + q * NS + n + 1)
                            for h in range(HALVES):
                                hs = q * STEPS + 2 * n + h
                                pool.wait_ge(scan_done, LEAD + hs + 1)
                                pool.wait_ge(y_done, LEAD + hs - (2 * AHEAD - 1))
                                nc.gpsimd.tensor_tensor(seen[:, n % AHEAD, h, :], state[:, n % AHEAD, h, :],
                                                        c_wide[:, n % AHEAD, :], ALU.mult).then_inc(seen_done, 1)
                            prepare(n, it, v, q + 1)
                            if n == 3 and (v or not first):
                                finish(1 - v, q - 1)

                over_tiles(pool, tile)
                finish(1, 2 * NT - 1)


def layer0(nc, const, w, x, normed_dram, mixed_dram):
    with Part(nc, "l0") as part:
        scale = part.sb("scale", [CH, BATCH])
        shift = part.sb("shift", [CH, BATCH])
        wp_t = part.sb("wp_t", [CH, CH])
        bp = part.sb("bp", [CH, 1])
        build_group_norm(nc, const, "gn0", scale, shift, x)
        build_layer_norm(nc, const, "ln0", normed_dram, affine=(scale, shift), extra=True)
        build_mamba(nc, const, w, normed_dram, mixed_dram, wp_t, bp)
        build_layer_norm(nc, const, "ln1", None, src=mixed_dram, project=(wp_t, bp))


def layer1(nc, const, w):
    GROUPS, K = 4, 3
    CPG, NK = CH // GROUPS, K * K
    FILTERS = GROUPS * NK
    MID = 64
    WIDE = IMG + 2
    ROWS = TILE // IMG
    SLOTS = 6
    with Part(nc, "l1") as part:
        scale = part.sb("scale", [CH, BATCH])
        shift = part.sb("shift", [CH, BATCH])
        kg_t = part.sb("kg_t", [CH, NK, MID + FILTERS])
        kg_b = part.sb("kg_b", [MID + FILTERS, 1])
        pw_t = part.sb("pw_t", [CH, CH])
        pw_b = part.sb("pw_b", [CH, 1])
        spread = part.sb("spread", [CH, NK, CH], BF16)
        padded = [part.sb(f"padded{k}", [CH, WIDE, WIDE]) for k in range(2)]
        build_group_norm(nc, const, "gn1", scale, shift)
        with Part(nc, "l1w") as pre:
            kg = pre.sb("kg", [FILTERS, CPG, NK])
            pw = pre.sb("pw", [CH, CPG])
            spread_f = pre.sb("spread_f", [CH, NK * CH])
            wide_t = pre.ps("wide_t", [CH, TILE])
            loaded, made, transposed, copied = pre.sems("loaded made transposed copied")
            with nc.Block() as block:
                @block.sync
                def _(sp):
                    with nc.allow_non_contiguous_dma("small weights"):
                        sp.wait_ge(made, 6)
                        n = 0
                        for dst, src in ((kg[:], w["w_kg"].rearrange("o i a b -> o i (a b)")),
                                         (kg_b[0:FILTERS, :], column(w["b_kg"])),
                                         (kg_b[MID:MID + FILTERS, :], column(w["b_kg"])),
                                         (pw_b[:], column(w["b_pw"]))):
                            sp.dma_start(dst, src).then_inc(loaded, 16)
                            n += 1
                        for g in range(GROUPS):
                            sp.dma_start(pw_t[g * CPG:(g + 1) * CPG, g * CPG:(g + 1) * CPG],
                                         w["w_pw"][g * CPG:(g + 1) * CPG].rearrange("o i a b -> i (o a b)")
                                         ).then_inc(loaded, 16)
                            n += 1
                        sp.wait_ge(loaded, 16 * n)

                @block.gpsimd
                def _(pool):
                    nc.gpsimd.memset(kg_t[:], 0.0).then_inc(made, 1)
                    nc.gpsimd.memset(pw_t[:], 0.0).then_inc(made, 1)
                    nc.gpsimd.memset(kg_b[:], 0.0).then_inc(made, 1)
                    nc.gpsimd.memset(padded[0][:], 0.0).then_inc(made, 1)
                    nc.gpsimd.memset(padded[1][:], 0.0).then_inc(made, 1)
                    nc.gpsimd.memset(spread[:], 0.0).then_inc(made, 1)
                    pool.wait_ge(made, 6)
                    v = spread[:].rearrange("p k (g c) -> p k g c", g=GROUPS)
                    for n, base in enumerate((0, MID)):
                        nc.gpsimd.affine_select(out=v, in_=v, compare_op=ALU.not_equal, fill=1.0, base=-base,
                                                pattern=[[-1, NK], [-NK, GROUPS], [0, CPG]],
                                                channel_multiplier=1).then_inc(made, 1)
                        pool.wait_ge(made, 7 + n)

                @block.tensor
                def _(pe):
                    pe.wait_ge(loaded, 16 * 8)
                    for k in range(NK):
                        if k >= 1:
                            pe.wait_ge(copied, 2 * GROUPS * k)
                        nc.tensor.transpose(wide_t[0:CPG, 0:FILTERS], kg[:, :, k],
                                            const.ident[0:FILTERS, 0:FILTERS]).then_inc(transposed, 1)

                @block.vector
                def _(dve):
                    dve.wait_ge(made, 8)
                    for k in range(NK):
                        dve.wait_ge(transposed, k + 1)
                        for g in range(GROUPS):
                            for at in (0, MID):
                                cols = slice(at + g * NK, at + (g + 1) * NK)
                                nc.vector.tensor_copy(kg_t[g * CPG:(g + 1) * CPG, k, cols],
                                                      wide_t[0:CPG, g * NK:(g + 1) * NK]).then_inc(copied, 1)

        hi_mid = part.sb("hi_mid", [CH, 2, TILE], BF16)
        rest = part.sb("rest", [CH, TILE])
        mid = part.sb("mid", [FILTERS, TILE], BF16)
        low = part.sb("low", [MID + FILTERS, 2, TILE], BF16)
        weighted = part.sb("weighted", [CH, SLOTS, TILE])
        total = part.sb("total", [CH, 2, TILE])
        filt_ps = [part.ps(f"filt_ps{k}", [CH, TILE]) for k in range(2)]
        wide_ps = [part.ps(f"wide_ps{k}", [CH, TILE]) for k in range(3)]
        out_ps = [part.ps(f"out_ps{k}", [CH, TILE]) for k in range(2)]
        (image_done, filters_done, hi_done, rest_done, mid_done, low_done, split_step, wide_done, weighted_done,
         total_done, out_done, added) = sems = part.sems(
            "image_done filters_done hi_done rest_done mid_done low_done split_step wide_done weighted_done "
            "total_done out_done added")
        cleared = part.sem("cleared")
        prime(nc, sems)

        def window(image, row, k):
            return image[:, bass.ds(row + k // K, ROWS), k % K:k % K + IMG]

        def over_tiles(eng, image, filters, taps, leave):
            def at(b, j, k):
                return b * TPB + j, j, b % 2, k, b

            image(0, 0)
            filters(*at(0, 0, 0))
            for b in range(BATCH):
                filters(*at(b, 1, 1))
                taps(*at(b, 0, 0))
                if b > 0:
                    leave(*at(b - 1, TPB - 1, 1))
                if b + 1 < BATCH:
                    image(b + 1, (b + 1) % 2)
                with eng.Fori(0, TPB // 2 - 1) as jj:
                    for j, k in ((2 * jj + 1, 1), (2 * jj + 2, 0)):
                        filters(*at(b, j + 1, 1 - k))
                        taps(*at(b, j, k))
                        leave(*at(b, j - 1, 1 - k))
                if b + 1 < BATCH:
                    filters(*at(b + 1, 0, 0))
                taps(*at(b, TPB - 1, 1))
                leave(*at(b, TPB - 2, 0))
            leave(*at(BATCH - 1, TPB - 1, 1))

        def nothing(*_):
            pass

        with nc.Block() as block:
            @block.scalar
            def _(act):
                def filters(t, j, m, k, b):
                    act.wait_ge(filters_done, LEAD + t + 1)
                    act.wait_ge(wide_done, LEAD + NK * (t - 1))
                    nc.scalar.activation(hi_mid[0:MID + FILTERS, k, :], filt_ps[k][0:MID + FILTERS, :], ACT.Identity,
                                         bias=kg_b[:, 0:1]).then_inc(hi_done, 1)

                over_tiles(act, nothing, filters, nothing, nothing)

            @block.vector
            def _(dve):
                def image(b, m):
                    dve.wait_ge(filters_done, LEAD + TPB * (b - 1))
                    nc.vector.tensor_scalar(padded[m][:, 1:1 + IMG, 1:1 + IMG],
                                            const.x[:, bass.ds(b * TOK, TOK)].rearrange("c (h w) -> c h w", h=IMG),
                                            scale[:, bass.ds(b, 1)], shift[:, bass.ds(b, 1)], ALU.mult, ALU.add
                                            ).then_inc(image_done, 1)

                def filters(t, j, m, k, b):
                    dve.wait_ge(image_done, LEAD + b + 1)
                    dve.wait_ge(hi_done, LEAD + t + 1)
                    rows = MID + FILTERS
                    nc.vector.scalar_tensor_tensor(out=rest[0:rows, :], in0=filt_ps[k][0:rows, :], scalar=kg_b[:, 0:1],
                                                   in1=hi_mid[0:rows, k, :], op0=ALU.add, op1=ALU.subtract
                                                   ).then_inc(split_step, 1)
                    dve.wait_ge(split_step, LEAD + 3 * t + 1)
                    dve.sem_inc(rest_done, 1)
                    nc.vector.tensor_copy(mid[:], rest[0:FILTERS, :]).then_inc(split_step, 1)
                    nc.vector.tensor_copy(hi_mid[MID:rows, k, :], rest[MID:rows, :]).then_inc(mid_done, 1)
                    dve.wait_ge(split_step, LEAD + 3 * t + 2)
                    dve.wait_ge(wide_done, LEAD + NK * (t - 1))
                    nc.vector.tensor_tensor(low[0:FILTERS, k, :], rest[0:FILTERS, :], mid[:], ALU.subtract).then_inc(split_step, 1)
                    dve.wait_ge(split_step, LEAD + 3 * t + 3)
                    dve.wait_ge(mid_done, LEAD + t + 1)
                    dve.sem_inc(low_done, 1)

                def taps(t, j, m, k, b):
                    for n in range(NK):
                        slot = (NK * k + n) % SLOTS
                        dve.wait_ge(wide_done, LEAD + NK * t + n + 1)
                        if n >= SLOTS:
                            dve.wait_ge(total_done, LEAD + (NK - 1) * t + max(n - SLOTS, 1))
                        else:
                            dve.wait_ge(total_done, LEAD + (NK - 1) * (t - 1) + n + NK - SLOTS)
                        nc.vector.tensor_tensor(
                            weighted[:, slot, :].rearrange("c (h w) -> c h w", h=ROWS), window(padded[m], j * ROWS, n),
                            wide_ps[(NK * k + n) % 3][:].rearrange("c (h w) -> c h w", h=ROWS), ALU.mult
                            ).then_inc(weighted_done, 1)

                def leave(t, j, m, k, b):
                    dve.wait_ge(out_done, LEAD + t + 1)
                    nc.vector.scalar_tensor_tensor(out=const.x[:, chunk(t)], in0=out_ps[k][:], scalar=pw_b[:, 0:1],
                                                   in1=const.x[:, chunk(t)], op0=ALU.add, op1=ALU.add
                                                   ).then_inc(added, 1)

                nc.vector.memset(low[:], 0.0).then_inc(cleared, 1)
                dve.wait_ge(cleared, 1)
                over_tiles(dve, image, filters, taps, leave)

            @block.gpsimd
            def _(pool):
                def taps(t, j, m, k, b):
                    pool.wait_ge(out_done, LEAD + t - 1)
                    for n in range(1, NK):
                        pool.wait_ge(weighted_done, LEAD + NK * t + n + 1)
                        first = weighted[:, NK * k % SLOTS, :] if n == 1 else total[:, k, :]
                        if n > 1:
                            pool.wait_ge(total_done, LEAD + (NK - 1) * t + n - 1)
                        nc.gpsimd.tensor_tensor(total[:, k, :], first, weighted[:, (NK * k + n) % SLOTS, :], ALU.add
                                                ).then_inc(total_done, 1)

                over_tiles(pool, nothing, nothing, taps, nothing)

            @block.tensor
            def _(pe):
                def filter_tap(t, j, m, k, b, n):
                    if n == 0:
                        pe.wait_ge(image_done, LEAD + b + 1)
                        pe.wait_ge(rest_done, LEAD + t - 1)
                    last = nc.tensor.matmul(filt_ps[k][0:MID + FILTERS, :], kg_t[:, n, :],
                                            window(padded[m], j * ROWS, n), start=(n == 0), stop=(n == NK - 1))
                    if n == NK - 1:
                        last.then_inc(filters_done, 1)

                def step(t, k, ahead):
                    pe.wait_ge(low_done, LEAD + t + 1)
                    for n in range(NK):
                        pe.wait_ge(weighted_done, LEAD + NK * t + n - 2)
                        bank = wide_ps[(NK * k + n) % 3]
                        nc.tensor.matmul(bank[:], spread[0:MID + FILTERS, n, :], hi_mid[0:MID + FILTERS, k, :],
                                         start=True, stop=False)
                        nc.tensor.matmul(bank[:], spread[0:MID + FILTERS, n, :], low[:, k, :], start=False, stop=True
                                         ).then_inc(wide_done, 1)
                        if ahead is not None:
                            filter_tap(*ahead, n)

                def leave(t, k):
                    pe.wait_ge(total_done, LEAD + (NK - 1) * (t + 1))
                    pe.wait_ge(added, LEAD + t - 1)
                    nc.tensor.matmul(out_ps[k][:], pw_t[:], total[:, k, :], start=True, stop=True).then_inc(out_done, 1)

                def at(b, j, k):
                    return b * TPB + j, j, b % 2, k, b

                for k in range(2):
                    for n in range(NK):
                        filter_tap(*at(0, k, k), n)
                for b in range(BATCH):
                    first = b * TPB
                    step(first, 0, at(b, 2, 0))
                    if b > 0:
                        leave(first - 1, 1)
                    step(first + 1, 1, at(b, 3, 1))
                    leave(first, 0)
                    with pe.Fori(1, TPB // 2 - 1) as jj:
                        for k in range(2):
                            j = 2 * jj + k
                            step(first + j, k, at(b, j + 2, k))
                            leave(first + j - 1, 1 - k)
                    for k in range(2):
                        t = first + TPB - 2 + k
                        step(t, k, at(b + 1, k, k) if b + 1 < BATCH else None)
                        leave(t - 1, 1 - k)
                leave(NT - 1, 1)


def build_attention(nc, const, normed_dram):
    KEYS = TOK // CH
    DIAG = TOK - CH
    SLOTS = 4
    FINISH = 4
    with Part(nc, "at") as part:
        q_in = part.sb("q_in", [CH, TOK])
        q_high = part.sb("q_high", [CH, TOK], F16)
        q_low = part.sb("q_low", [CH, TOK], F16)
        q = part.sb("q", [CH, KEYS, CH])
        strip = part.sb("strip", [CH, TOK - TILE + DIAG + TILE], BF16)
        weight = part.sb("weight", [CH, SLOTS, TILE])
        total = part.sb("total", [CH, 2, TILE])
        share = part.sb("share", [CH, TILE])
        ones = part.sb("ones", [CH, CH])
        score_ps = [part.ps(f"score_ps{k}", [CH, TILE]) for k in range(3)]
        out_ps = [part.ps(f"out_ps{k}", [CH, TILE]) for k in range(2)]
        total_ps = part.ps("total_ps", [CH, TILE])
        turn_ps = [part.ps(f"turn_ps{k}", [CH, TILE]) for k in range(2)]
        (high_done, low_done, turned, q_copied, scores_done, exp_done, masked_done, total_done, summed, values_done,
         share_done, scaled, added) = sems = part.sems(
            "high_done low_done turned q_copied scores_done exp_done masked_done total_done summed values_done "
            "share_done scaled added")
        q_loaded, made = part.sems("q_loaded made")
        prime(nc, sems)

        def over_chunks(eng, batch, chunk_of, finish):
            with eng.Fori(0, BATCH) as b:
                batch(b)
                chunk_of(b, 0, 0, True)
                with eng.Fori(0, TPB // 2 - 1) as ii:
                    chunk_of(b, 2 * ii + 1, 1, False)
                    chunk_of(b, 2 * ii + 2, 0, False)
                chunk_of(b, TPB - 1, 1, False)
                finish(b * TPB + TPB - 1, 1)

        def nothing(*_):
            pass

        with nc.Block() as block:
            @block.gpsimd
            def _(pool):
                nc.gpsimd.memset(ones[:], 1.0).then_inc(made, 1)
                nc.gpsimd.memset(strip[:], 1.0).then_inc(made, 1)
                pool.wait_ge(made, 2)
                nc.gpsimd.affine_select(out=strip[:], in_=strip[:], compare_op=ALU.not_equal, fill=0.0, base=-DIAG,
                                        pattern=[[1, strip.shape[1]]], channel_multiplier=-1).then_inc(made, 1)

                def batch(b):
                    pool.wait_ge(high_done, LEAD + b + 1)
                    nc.gpsimd.tensor_tensor(q_low[:], q_in[:], q_high[:], ALU.subtract).then_inc(low_done, 1)

                def sums(b, i, k, first):
                    c = b * TPB + i
                    for m in range(1, KEYS):
                        pool.wait_ge(masked_done, LEAD + c * KEYS + m + 1)
                        if m == 1:
                            pool.wait_ge(summed, LEAD + c - 1)
                        else:
                            pool.wait_ge(total_done, LEAD + (KEYS - 1) * c + m - 1)
                        start = weight[:, 0, :] if m == 1 else total[:, k, :]
                        nc.gpsimd.tensor_tensor(total[:, k, :], start, weight[:, m % SLOTS, :], ALU.add
                                                ).then_inc(total_done, 1)

                over_chunks(pool, batch, sums, nothing)

            @block.sync
            def _(sp):
                with sp.Fori(0, BATCH) as b:
                    sp.wait_ge(low_done, LEAD + b)
                    sp.wait_ge(turned, LEAD + TPB * b)
                    sp.dma_start(q_in[:], normed_dram[:, bass.ds(b * TOK, TOK)]).then_inc(q_loaded, 16)

            @block.tensor
            def _(pe):
                pe.wait_ge(made, 3)

                def batch(b):
                    pe.wait_ge(q_loaded, 16 * (b + 1))
                    for n in range(TPB):
                        pe.wait_ge(q_copied, LEAD + TPB * b + n - 1)
                        for k in range(4):
                            last = nc.tensor.transpose(turn_ps[n % 2][:, chunk(k, CH)], q_in[:, chunk(4 * n + k, CH)],
                                                       const.ident[:])
                        last.then_inc(turned, 1)
                    pe.wait_ge(low_done, LEAD + b + 1)

                def finish(c, k):
                    pe.wait_ge(total_done, LEAD + (KEYS - 1) * (c + 1))
                    pe.wait_ge(share_done, LEAD + c)
                    nc.tensor.matmul(total_ps[:], ones[:], total[:, k, :], start=True, stop=True).then_inc(summed, 1)

                def products(b, i, k, first):
                    c = b * TPB + i

                    def scores(m):
                        pe.wait_ge(exp_done, LEAD + c * KEYS + m - 2)
                        keys = chunk(m, CH)
                        for n, (left, right) in enumerate(((q_high, q_low), (q_low, q_high), (q_high, q_high))):
                            last = nc.tensor.matmul(score_ps[m % 3][:], left[:, keys], right[:, chunk(i)],
                                                    start=(n == 0), stop=(n == 2))
                        last.then_inc(scores_done, 1)

                    pe.wait_ge(exp_done, LEAD + c * KEYS)
                    scores(0)
                    scores(1)
                    if first:
                        pe.wait_ge(q_copied, LEAD + TPB * (b + 1))
                    for m in range(KEYS):
                        if m + 2 < KEYS:
                            scores(m + 2)
                        pe.wait_ge(masked_done, LEAD + c * KEYS + m + 1)
                        if m == 0:
                            pe.wait_ge(scaled, LEAD + c - 1)
                        nc.tensor.matmul(out_ps[k][:], q[:, m, :], weight[:, m % SLOTS, :],
                                         start=(m == 0), stop=(m == KEYS - 1)).then_inc(values_done, 1)
                        if m == FINISH - 2 and not first:
                            finish(c - 1, 1 - k)

                over_chunks(pe, batch, products, finish)

            @block.scalar
            def _(act):
                def batch(b):
                    act.wait_ge(scores_done, LEAD + TPB * KEYS * b)
                    act.wait_ge(q_loaded, 16 * (b + 1))
                    nc.scalar.activation(q_high[:], q_in[:], ACT.Copy).then_inc(high_done, 1)

                with act.Fori(0, BATCH) as b:
                    batch(b)
                    with act.Fori(0, TPB) as i:
                        c = b * TPB + i
                        for m in range(KEYS):
                            act.wait_ge(scores_done, LEAD + c * KEYS + m + 1)
                            act.wait_ge(values_done, LEAD + c * KEYS + m - (SLOTS - 1))
                            act.wait_ge(total_done, LEAD + (KEYS - 1) * c + (max(m - SLOTS, 1) if m >= SLOTS else 0))
                            nc.scalar.activation(weight[:, m % SLOTS, :], score_ps[m % 3][:], ACT.Exp,
                                                 scale=1.0 / math.sqrt(CH)).then_inc(exp_done, 1)

            @block.vector
            def _(dve):
                dve.wait_ge(made, 3)

                def batch(b):
                    dve.wait_ge(values_done, LEAD + TPB * KEYS * b)
                    for n in range(TPB):
                        dve.wait_ge(turned, LEAD + TPB * b + n + 1)
                        nc.vector.tensor_copy(q[:, 4 * n:4 * n + 4, :].rearrange("p a b -> p (a b)"), turn_ps[n % 2][:]
                                              ).then_inc(q_copied, 1)

                def finish(c, k):
                    dve.wait_ge(summed, LEAD + c + 1)
                    dve.wait_ge(added, LEAD + c)
                    nc.vector.reciprocal(share[:], total_ps[:]).then_inc(share_done, 1)
                    dve.wait_ge(share_done, LEAD + c + 1)
                    dve.wait_ge(values_done, LEAD + KEYS * (c + 1))
                    nc.vector.tensor_tensor(share[:], out_ps[k][:], share[:], ALU.mult).then_inc(scaled, 1)
                    dve.wait_ge(scaled, LEAD + c + 1)
                    nc.vector.tensor_tensor(const.x[:, chunk(c)], const.x[:, chunk(c)], share[:], ALU.add
                                            ).then_inc(added, 1)

                def masks(b, i, k, first):
                    c = b * TPB + i
                    for m in range(KEYS):
                        dve.wait_ge(exp_done, LEAD + c * KEYS + m + 1)
                        nc.vector.tensor_tensor(weight[:, m % SLOTS, :], weight[:, m % SLOTS, :],
                                                strip[:, bass.ds(i * TILE + DIAG - m * CH, TILE)], ALU.mult
                                                ).then_inc(masked_done, 1)
                        if m == FINISH and not first:
                            finish(c - 1, 1 - k)

                over_chunks(dve, batch, masks, finish)
                dve.wait_ge(added, LEAD + NT)


def attention(nc, const, normed_dram):
    build_layer_norm(nc, const, "ln2", normed_dram)
    build_attention(nc, const, normed_dram)


def experts(nc, const, name, w, out=None):
    E, K, H, O = 64, 8, 512, CH
    JT = H // CH
    PAIRS = BATCH // 2
    HALF, QUAD = CH // BATCH, 4
    QUADS = HALF // QUAD
    with Part(nc, name) as part:
        gate_t = part.sb("gate_t", [CH, E])
        gate_b = part.sb("gate_b", [CH, 1])
        b1 = part.sb("b1", [CH, E // HALF, H])
        b2_t = part.sb("b2_t", [CH, E])
        token_weight = part.sb("token_weight", [CH, PAIRS, TOK])
        pooled_t = part.sb("pooled_t", [CH, E, BATCH])
        out_t = part.sb("out_t", [CH, PAIRS, 2, E])
        with Part(nc, name + "g") as pre:
            gate = pre.sb("gate", [E, CH])
            b2 = pre.sb("b2", [E, O])
            loaded, = pre.sems("loaded")
            with nc.Block() as block:
                @block.sync
                def _(sp):
                    with nc.allow_non_contiguous_dma("small weights"):
                        for dst, src in ((gate[:], w["gate_w"]), (gate_b[0:E, :], column(w["gate_b"])),
                                         (gate_b[E:2 * E, :], column(w["gate_b"])),
                                         (b2[:], w["weight2"][:, H, :])):
                            sp.dma_start(dst, src).then_inc(loaded, 16)
                        for h in range(E // HALF):
                            sp.dma_start(b1[:, h, :], w["weight1"][h * HALF:(h + 1) * HALF, CH, :].unsqueeze(1)
                                         .to_broadcast([HALF, BATCH, H])).then_inc(loaded, 16)
                        sp.wait_ge(loaded, 16 * (4 + E // HALF))
            build_transposes(nc, name + "t", const, [(gate_t[:], gate[:], None), (b2_t[:], b2[:], None)])
        with Part(nc, name + "p") as pre:
            xh = pre.sb("xh", [CH, BATCH * TOK])
            build_layer_norm(nc, const, name + "n", None, keep=xh)
            logit = pre.sb("logit", [CH, PAIRS, TOK])
            top = pre.sb("top", [CH, PAIRS, K])
            top_exp = pre.sb("top_exp", [CH, PAIRS, K])
            minus_max = pre.sb("minus_max", [CH, PAIRS])
            total = pre.sb("total", [CH, PAIRS])
            share = pre.sb("share", [CH, PAIRS])
            x_tok = pre.sb("x_tok", [CH, 2, 2, CH])
            w_tok = pre.sb("w_tok", [CH, 2, CH])
            logit_ps = [pre.ps(f"logit_ps{k}", [CH, TILE]) for k in range(2)]
            turn_ps = [pre.ps(f"turn_ps{k}", [CH, 3, CH]) for k in range(2)]
            pooled_ps = [pre.ps(f"pooled_ps{k}", [CH, E]) for k in range(2)]
            (logits_done, logit_copied, top_done, max_done, exp_done, top_exp_done, share_done, left_done,
             picked_done, weight_done, turned, turn_copied, x_copied, pooled, pooled_copied) = sems = pre.sems(
                "logits_done logit_copied top_done max_done exp_done top_exp_done share_done left_done "
                "picked_done weight_done turned turn_copied x_copied pooled pooled_copied")
            prime(nc, sems)
            SUBS = TOK // CH
            with nc.Block() as block:
                @block.tensor
                def _(pe):
                    for b in range(BATCH):
                        at = slice(E * (b % 2), E * (b % 2 + 1))
                        for i in range(TPB):
                            n = b * TPB + i
                            pe.wait_ge(logit_copied, LEAD + n - 1)
                            nc.tensor.matmul(logit_ps[i % 2][at, :], gate_t[:], xh[:, chunk(n)],
                                             start=True, stop=True).then_inc(logits_done, 1)
                    for pair in range(PAIRS):
                        pe.wait_ge(weight_done, LEAD + pair + 1)
                        pe.wait_ge(pooled_copied, LEAD + 2 * pair)

                        def turn(i):
                            pe.wait_ge(turn_copied, LEAD + pair * SUBS + i - 1)
                            pe.wait_ge(x_copied, LEAD + pair * SUBS + i - 1)
                            for k in range(2):
                                nc.tensor.transpose(turn_ps[i % 2][:, k, :], xh[:, chunk((2 * pair + k) * SUBS + i, CH)],
                                                    const.ident[:])
                            nc.tensor.transpose(turn_ps[i % 2][:, 2, :], token_weight[:, pair, chunk(i, CH)],
                                                const.ident[:]).then_inc(turned, 1)

                        turn(0)
                        for i in range(SUBS):
                            if i + 1 < SUBS:
                                turn(i + 1)
                            pe.wait_ge(turn_copied, LEAD + pair * SUBS + i + 1)
                            pe.wait_ge(x_copied, LEAD + pair * SUBS + i + 1)
                            for k in range(2):
                                last = nc.tensor.matmul(pooled_ps[k][:], x_tok[:, i % 2, k, :],
                                                        w_tok[:, i % 2, E * k:E * (k + 1)],
                                                        start=(i == 0), stop=(i == SUBS - 1))
                            last.then_inc(pooled, 1)

                @block.scalar
                def _(act):
                    for b in range(BATCH):
                        at = slice(E * (b % 2), E * (b % 2 + 1))
                        for i in range(TPB):
                            n = b * TPB + i
                            act.wait_ge(logits_done, LEAD + n + 1)
                            nc.scalar.activation(logit[at, b // 2, chunk(i)], logit_ps[i % 2][at, :], ACT.Identity,
                                                 bias=gate_b[at, 0:1]).then_inc(logit_copied, 1)
                    for pair in range(PAIRS):
                        one = slice(pair, pair + 1)
                        act.wait_ge(max_done, LEAD + pair + 1)
                        nc.scalar.activation(token_weight[:, pair, :], logit[:, pair, :], ACT.Exp, bias=minus_max[:, one],
                                             accum_out=total[:, one]).then_inc(exp_done, 1)
                        nc.scalar.activation(top_exp[:, pair, :], top[:, pair, :], ACT.Exp, bias=minus_max[:, one]
                                             ).then_inc(top_exp_done, 1)
                    for n in range(PAIRS * SUBS):
                        act.wait_ge(turned, LEAD + n + 1)
                        act.wait_ge(pooled, LEAD + n - 1)
                        nc.scalar.activation(x_tok[:, n % 2, :, :], turn_ps[n % 2][:, 0:2, :], ACT.Copy
                                             ).then_inc(x_copied, 1)
                        act.wait_ge(x_copied, LEAD + n + 1)
                        nc.scalar.activation(w_tok[:, n % 2, :], turn_ps[n % 2][:, 2, :], ACT.Copy
                                             ).then_inc(turn_copied, 1)

                @block.vector
                def _(dve):
                    for pair in range(PAIRS):
                        one = slice(pair, pair + 1)
                        dve.wait_ge(logit_copied, LEAD + (pair + 1) * 2 * TPB)
                        nc.vector.max(top[:, pair, :], logit[:, pair, :]).then_inc(top_done, 1)
                        dve.wait_ge(top_done, LEAD + pair + 1)
                        nc.vector.tensor_scalar(minus_max[:, one], top[:, pair, 0:1], -1.0, None, ALU.mult
                                                ).then_inc(max_done, 1)
                    for pair in range(PAIRS):
                        one = slice(pair, pair + 1)
                        dve.wait_ge(exp_done, LEAD + pair + 1)
                        dve.wait_ge(top_exp_done, LEAD + pair + 1)
                        nc.vector.reciprocal(share[:, one], total[:, one]).then_inc(share_done, 1)
                        nc.vector.match_replace(logit[:, pair, :], top_exp[:, pair, :], token_weight[:, pair, :], 0.0
                                                ).then_inc(left_done, 1)
                        dve.wait_ge(left_done, LEAD + pair + 1)
                        nc.vector.tensor_tensor(token_weight[:, pair, :], token_weight[:, pair, :], logit[:, pair, :],
                                                ALU.subtract).then_inc(picked_done, 1)
                        dve.wait_ge(picked_done, LEAD + pair + 1)
                        dve.wait_ge(share_done, LEAD + pair + 1)
                        nc.vector.tensor_scalar(token_weight[:, pair, :], token_weight[:, pair, :], share[:, one], None,
                                                ALU.mult).then_inc(weight_done, 1)
                    for pair in range(PAIRS):
                        for k in range(2):
                            dve.wait_ge(pooled, LEAD + SUBS * (pair + 1))
                            nc.vector.tensor_copy(pooled_t[:, :, 2 * pair + k], pooled_ps[k][:]).then_inc(pooled_copied, 1)

        with Part(nc, name + "x") as pre:
            wide = pre.sb("wide", [CH, HALF * (CH + BATCH)])
            own_columns = wide[:].rearrange("d (e k) -> d e k", k=CH + BATCH)[:, :, 0:BATCH]
            raw = pre.sb("raw", [CH, H])
            hidden = pre.sb("hidden", [CH, H])
            LANES = 32
            QUARTERS, EIGHT = CH // LANES, LANES // BATCH
            hidden_wide = pre.sb("hidden_wide", [CH, JT * QUARTERS, EIGHT * (LANES + BATCH)])
            own_hidden = hidden_wide[:].rearrange("j t (e k) -> j t e k", k=LANES + BATCH)[:, :, :, 0:BATCH]
            out_rows = pre.sb("out_rows", [CH, O])
            hidden_ps = pre.ps("hidden_ps", [CH, H])
            turn_ps = pre.ps("turn_ps", [CH, JT, CH])
            out_ps = pre.ps("out_ps", [CH, O])
            out_turn_ps = pre.ps("out_turn_ps", [CH, HALF, BATCH])
            ring = [pre.sb(f"ring{n}", [CH, QUAD, H]) for n in range(QUADS)]
            ring_loaded = [pre.sem(f"ring_loaded{n}") for n in range(QUADS)]
            ring_used = [pre.sem(f"ring_used{n}") for n in range(QUADS)]
            (wide_done, biased_done, gelu_done, turned, turn_copied, rows_done, rows_turned, out_done) = sems = pre.sems(
                "wide_done biased_done gelu_done turned turn_copied rows_done rows_turned out_done")
            zeroed = pre.sem("zeroed")
            prime(nc, (*sems, *ring_used))
            layer_done = ring_used[QUADS - 1]
            with nc.Block() as block:
                @block.gpsimd
                def _(pool):
                    nc.gpsimd.memset(wide[:], 0.0).then_inc(zeroed, 1)
                    nc.gpsimd.memset(hidden_wide[:], 0.0).then_inc(zeroed, 1)

                @block.sync
                def _(sp):
                    with sp.Fori(0, E // HALF) as h:
                        for layer in range(2):
                            for n in range(QUADS):
                                experts_of = bass.ds(h * HALF + n * QUAD, QUAD)
                                if layer == 0:
                                    src = w["weight1"][experts_of, 0:CH, :].rearrange("e d j -> d e j")
                                else:
                                    src = w["weight2"][experts_of, 0:H, :].rearrange("e (p t) o -> p e (t o)", t=JT)
                                sp.wait_ge(ring_used[n], LEAD + 2 * h + layer)
                                sp.dma_start(ring[n][:], src).then_inc(ring_loaded[n], 16)

                @block.tensor
                def _(pe):
                    with pe.Fori(0, E // HALF) as h:
                        pe.wait_ge(wide_done, LEAD + h + 1)
                        pe.wait_ge(biased_done, LEAD + h)
                        for n in range(QUADS):
                            pe.wait_ge(ring_loaded[n], 16 * (2 * h + 1))
                            for e in range(n * QUAD, (n + 1) * QUAD):
                                last = nc.tensor.matmul(hidden_ps[:], wide[:, chunk(e, CH)], ring[n][:, e % QUAD, :],
                                                        start=(e == 0), stop=(e == HALF - 1))
                            last.then_inc(ring_used[n], 1)
                        pe.wait_ge(gelu_done, LEAD + h + 1)
                        pe.wait_ge(turn_copied, LEAD + h)
                        for t in range(JT):
                            last = nc.tensor.transpose(turn_ps[:, t, :], hidden[:, t::JT], const.ident[:])
                        last.then_inc(turned, 1)
                        pe.wait_ge(turn_copied, LEAD + h + 1)
                        pe.wait_ge(rows_done, LEAD + h)
                        for n in range(QUADS):
                            pe.wait_ge(ring_loaded[n], 16 * (2 * h + 2))
                            for e in range(n * QUAD, (n + 1) * QUAD):
                                quarter, lane = divmod(e, EIGHT)
                                for t in range(JT):
                                    last = nc.tensor.matmul(
                                        out_ps[quarter * LANES:(quarter + 1) * LANES, :],
                                        hidden_wide[:, t * QUARTERS + quarter, chunk(lane, LANES)],
                                        ring[n][:, e % QUAD, chunk(t, O)], start=(lane == 0 and t == 0),
                                        stop=(lane == EIGHT - 1 and t == JT - 1))
                            last.then_inc(ring_used[n], 1)
                        pe.wait_ge(rows_done, LEAD + h + 1)
                        pe.wait_ge(out_done, LEAD + BATCH * h)
                        nc.tensor.transpose(out_turn_ps[:].rearrange("o e b -> o (e b)"), out_rows[:], const.ident[:]
                                            ).then_inc(rows_turned, 1)

                @block.scalar
                def _(act):
                    with act.Fori(0, E // HALF) as h:
                        act.wait_ge(biased_done, LEAD + h + 1)
                        act.wait_ge(turned, LEAD + h)
                        nc.scalar.activation(hidden[:], raw[:], ACT.Gelu).then_inc(gelu_done, 1)

                @block.vector
                def _(dve):
                    dve.wait_ge(zeroed, 2)
                    with dve.Fori(0, E // HALF) as h:
                        dve.wait_ge(layer_done, LEAD + 2 * h)
                        nc.vector.tensor_scalar(own_columns, pooled_t[:, bass.ds(h * HALF, HALF), :], 1.0, None, ALU.mult
                                                ).then_inc(wide_done, 1)
                        dve.wait_ge(layer_done, LEAD + 2 * h + 1)
                        dve.wait_ge(gelu_done, LEAD + h)
                        nc.vector.tensor_tensor(raw[:], hidden_ps[:], b1[:, bass.ds(h, 1), :].rearrange("p a j -> p (a j)"),
                                                ALU.add).then_inc(biased_done, 1)
                        dve.wait_ge(turned, LEAD + h + 1)
                        nc.vector.tensor_copy(own_hidden, turn_ps[:].rearrange("j t (q e b) -> j (t q) e b", q=QUARTERS,
                                                                               b=BATCH)).then_inc(turn_copied, 1)
                        dve.wait_ge(layer_done, LEAD + 2 * h + 2)
                        dve.wait_ge(rows_turned, LEAD + h)
                        nc.vector.tensor_copy(out_rows[:], out_ps[:]).then_inc(rows_done, 1)
                        dve.wait_ge(rows_turned, LEAD + h + 1)
                        for b in range(BATCH):
                            nc.vector.tensor_tensor(
                                out_t[:, b // 2, b % 2, bass.ds(h * HALF, HALF)], out_turn_ps[:, :, b],
                                b2_t[:, bass.ds(h * HALF, HALF)], ALU.add).then_inc(out_done, 1)
                    dve.wait_ge(out_done, LEAD + BATCH * (E // HALF))

        with Part(nc, name + "o") as pre:
            out_e = pre.sb("out_e", [CH, PAIRS, 2, O])
            back_ps = [pre.ps(f"back_ps{k}", [CH, TILE]) for k in range(2)]
            back_done, added = sems = pre.sems("back_done added")
            zeroed, leaving = pre.sems("zeroed leaving")
            prime(nc, sems)
            with nc.Block() as block:
                @block.gpsimd
                def _(pool):
                    nc.gpsimd.memset(out_e[:], 0.0).then_inc(zeroed, 1)
                    pool.wait_ge(zeroed, 1)
            build_transposes(nc, name + "u", const,
                             [(out_e[E * k:E * (k + 1), p, k, :], out_t[:, p, k, :], None)
                              for p in range(PAIRS) for k in range(2)])
            with nc.Block() as block:
                @block.sync
                def _(sp):
                    if out is not None:
                        for n in range(2 * BATCH):
                            b, k = divmod(n, 2)
                            sp.wait_ge(added, LEAD + (n + 1) * TPB // 2)
                            sp.dma_start(out[b, :, k * IMG // 2:(k + 1) * IMG // 2, :].rearrange("c h w -> c (h w)"),
                                         const.x[:, chunk(n, TOK // 2)]).then_inc(leaving, 16)
                        sp.wait_ge(leaving, 16 * 2 * BATCH)

                @block.tensor
                def _(pe):
                    for b in range(BATCH):
                        for i in range(TPB):
                            t = b * TPB + i
                            pe.wait_ge(added, LEAD + t - 1)
                            nc.tensor.matmul(back_ps[i % 2][:], out_e[:, b // 2, b % 2, :], token_weight[:, b // 2, chunk(i)],
                                             start=True, stop=True).then_inc(back_done, 1)

                @block.vector
                def _(dve):
                    with dve.Fori(0, NT // 2) as j:
                        for k in range(2):
                            t = 2 * j + k
                            dve.wait_ge(back_done, LEAD + t + 1)
                            nc.vector.tensor_tensor(const.x[:, chunk(t)], back_ps[k][:], const.x[:, chunk(t)], ALU.add
                                                    ).then_inc(added, 1)
                    dve.wait_ge(added, LEAD + NT)


def build_ssd(nc, const, name, w, normed_dram, back):
    DI, NS, HEADS, HD, TAPS = 256, 64, 4, 64, 4
    HALVES = DI // CH
    SUBS = TILE // CH
    CONV = 3
    IN = 2 * DI + 2 * NS + HEADS
    CAP = 40.0
    ALMOST_ONE = 1.0 - 2.0 ** -23
    DT, DA, DTD, DCH = range(4)
    edge = TILE if back else 0
    here = 0 if back else TAPS - 1

    def tap(k):
        return TAPS - 1 - k if back else k

    def place(t):
        return t * -1 + (NT - 1) if back else t

    def placed(eng, t):
        if isinstance(t, int):
            return place(t)
        at = eng.snap(place(t))
        eng.compute_val(at)
        return at

    def sub(u):
        return SUBS - 1 - u if back else u

    with Part(nc, name) as part:
        in_w = part.sb("in_w", [CH, IN])
        conv_w = part.sb("conv_w", [CH, CONV, TAPS])
        conv_b = part.sb("conv_b", [CH, CONV])
        d_skip = part.sb("d_skip", [CH, HALVES])
        out_w = part.sb("out_w", [CH, HALVES, CH])
        after = part.sb("after", [CH, CH])
        upto = part.sb("upto", [CH, CH])
        scalars = part.sb("scalars", [CH, NT * SUBS, 4, HEADS])
        keep = part.sb("keep", [CH, NT])

        with Part(nc, name + "w") as pre:
            norm_w = pre.sb("norm_w", [CH, HALVES])
            rows = pre.sb("rows", [1, 2 * HEADS])
            ones_row = pre.sb("ones_row", [1, CH])
            head_row = pre.sb("head_row", [1, HEADS])
            heads = pre.sb("heads", [CH, 2 * HEADS])
            minus_a = pre.sb("minus_a", [CH, HEADS])
            heads_ps = pre.ps("heads_ps", [CH, 2 * HEADS])
            ones = pre.sb("ones", [CH, CH])
            dt_ps = pre.ps("dt_ps", [CH, NT * SUBS, HEADS])
            sum_ps = [pre.ps(f"sum_ps{k}", [CH, TILE]) for k in range(2)]
            BLOCK = TOK // 2
            xh = pre.sb("xh", [CH, 2, BLOCK])
            a = pre.sb("a", [CH, NT * SUBS, HEADS])
            e = pre.sb("e", [CH, NT * SUBS, HEADS])
            small = pre.sb("small", [CH, NT * SUBS, HEADS])
            log = pre.sb("log", [CH, NT * SUBS, HEADS])
            dt = pre.sb("dt", [CH, NT * SUBS, HEADS])
            da = pre.sb("da", [CH, NT * SUBS, HEADS])
            almost_one = pre.sb("almost_one", [CH, 1])
            (loaded, made, heads_done, step, exp_done, projected, dt_step, e_done, small_done, log_done, da_done,
             sums_done, sums_exp, scalars_done) = pre.sems(
                "loaded made heads_done step exp_done projected dt_step e_done small_done log_done da_done "
                "sums_done sums_exp scalars_done")
            xh_loaded = pre.sems("xh_loaded0 xh_loaded1")
            xh_used = pre.sem("xh_used")
            prime(nc, (xh_used,))
            with nc.Block() as block:
                @block.sync
                def _(sp):
                    with nc.allow_non_contiguous_dma("small weights"):
                        n = 0
                        loads = [(in_w[:], w["in_proj"]),
                                 (conv_w[:], w["conv_w"].rearrange("(t p) k -> p t k", p=CH)),
                                 (conv_b[:], w["conv_b"].rearrange("(t p) -> p t", p=CH)),
                                 (norm_w[:], half_columns(w["norm_w"])),
                                 (out_w[:], w["out_proj"].rearrange("(h p) c -> p h c", p=CH)),
                                 (rows[0:1, 0:HEADS], w["dt_bias"].rearrange("(a n) -> a n", a=1)),
                                 (rows[0:1, HEADS:], w["A_log"].rearrange("(a n) -> a n", a=1))]
                        for h in range(HEADS):
                            loads.append((d_skip[HD * (h % 2):HD * (h % 2 + 1), h // 2:h // 2 + 1],
                                          w["D"][h:h + 1].rearrange("(a n) -> a n", a=1).to_broadcast([HD, 1])))
                        for dst, src in loads:
                            sp.dma_start(dst, src).then_inc(loaded, 16)
                            n += 1
                        sp.wait_ge(loaded, 16 * n)
                    with sp.Fori(0, BATCH) as i:
                        for k in range(2):
                            sp.wait_ge(xh_used, LEAD + 2 * i + k - 1)
                            sp.dma_start(xh[:, k, :], normed_dram[:, chunk(2 * i + k, BLOCK)]).then_inc(xh_loaded[k], 16)

                @block.gpsimd
                def _(pool):
                    nc.gpsimd.memset(ones_row[:], 1.0).then_inc(made, 1)
                    nc.gpsimd.memset(ones[:], 1.0).then_inc(made, 1)
                    nc.gpsimd.memset(after[:], 1.0).then_inc(made, 1)
                    nc.gpsimd.memset(upto[:], 1.0).then_inc(made, 1)
                    nc.gpsimd.memset(keep[:], 1.0).then_inc(made, 1)
                    nc.gpsimd.memset(almost_one[:], ALMOST_ONE).then_inc(made, 1)
                    pool.wait_ge(made, 6)
                    sign = -1 if back else 1
                    nc.gpsimd.affine_select(out=after[:], in_=after[:], compare_op=ALU.is_gt, fill=0.0, base=0,
                                            pattern=[[-sign, CH]], channel_multiplier=sign).then_inc(made, 1)
                    nc.gpsimd.affine_select(out=upto[:], in_=upto[:], compare_op=ALU.is_ge, fill=0.0, base=0,
                                            pattern=[[sign, CH]], channel_multiplier=-sign).then_inc(made, 1)
                    nc.gpsimd.memset(keep[:, 0:NT:TPB], 0.0).then_inc(made, 1)
                    pool.wait_ge(made, 9)

                @block.tensor
                def _(pe):
                    pe.wait_ge(made, 9)
                    pe.wait_ge(loaded, 16 * 11)
                    nc.tensor.matmul(heads_ps[:], ones_row[0:1, :], rows[0:1, :], start=True, stop=True
                                     ).then_inc(heads_done, 1)
                    with pe.Fori(0, BATCH) as i:
                        for k in range(2):
                            pe.wait_ge(xh_loaded[k], 16 * (i + 1))
                            for c in range(BLOCK // CH):
                                last = nc.tensor.matmul(
                                    dt_ps[:, bass.ds((2 * i + k) * (BLOCK // CH) + c, 1), :].rearrange("p a h -> p (a h)"),
                                    xh[:, k, chunk(c, CH)], in_w[:, IN - HEADS:], start=True, stop=True)
                            last.then_inc(xh_used, 1)
                    pe.wait_ge(da_done, 1)
                    flat = da[:].rearrange("p s h -> p (s h)")
                    nc.tensor.matmul(sum_ps[0][:], after[:], flat, start=True, stop=True).then_inc(sums_done, 1)
                    nc.tensor.matmul(sum_ps[1][:], ones[:], flat, start=True, stop=True).then_inc(sums_done, 1)

                @block.scalar
                def _(act):
                    nc.scalar.preload_act_table_set("natural_log_exp_and_others")
                    act.wait_ge(step, 1)
                    nc.scalar.activation(minus_a[:], heads[:, HEADS:], ACT.Exp).then_inc(exp_done, 1)
                    act.wait_ge(dt_step, 2)
                    nc.scalar.activation(e[:], a[:], ACT.Exp).then_inc(e_done, 1)
                    act.wait_ge(e_done, 1)
                    nc.scalar.activation(small[:], e[:], ACT.Exp, scale=-0.5).then_inc(small_done, 1)
                    nc.scalar.activation(log[:], e[:], ACT.Ln, bias=almost_one[:, 0:1]).then_inc(log_done, 1)
                    act.wait_ge(sums_done, 1)
                    act.wait_ge(dt_step, 7)
                    nc.scalar.activation(a[:].rearrange("p s h -> p (s h)"), sum_ps[0][:], ACT.Exp).then_inc(sums_exp, 1)
                    act.wait_ge(sums_done, 2)
                    nc.scalar.activation(scalars[:, :, DCH, :], sum_ps[1][:].rearrange("p (s h) -> p s h", h=HEADS),
                                         ACT.Exp).then_inc(sums_exp, 1)

                @block.vector
                def _(dve):
                    dve.wait_ge(heads_done, 1)
                    nc.vector.tensor_copy(heads[:], heads_ps[:]).then_inc(step, 1)
                    dve.wait_ge(loaded, 16 * 11)
                    for h in range(HALVES):
                        nc.vector.tensor_scalar(out_w[:, h, :], out_w[:, h, :], norm_w[:, h:h + 1], None, ALU.mult
                                                ).then_inc(step, 1)
                    dve.wait_ge(exp_done, 1)
                    nc.vector.tensor_scalar(minus_a[:], minus_a[:], -1.0, None, ALU.mult).then_inc(step, 1)
                    dve.wait_ge(step, 4)
                    dve.wait_ge(xh_used, LEAD + 2 * BATCH)
                    every = [CH, NT * SUBS, HEADS]
                    nc.vector.tensor_tensor(dt[:], dt_ps[:], heads[:, 0:HEADS].unsqueeze(1).to_broadcast(every), ALU.add
                                            ).then_inc(dt_step, 1)
                    dve.wait_ge(dt_step, 1)
                    nc.vector.tensor_scalar(a[:], dt[:], CAP, None, ALU.min).then_inc(dt_step, 1)
                    dve.wait_ge(log_done, 1)
                    nc.vector.tensor_tensor(dt[:], dt[:], log[:], ALU.max).then_inc(dt_step, 1)
                    dve.wait_ge(small_done, 1)
                    nc.vector.tensor_tensor(small[:], small[:], e[:], ALU.mult).then_inc(dt_step, 1)
                    dve.wait_ge(dt_step, 4)
                    nc.vector.tensor_tensor(dt[:], dt[:], small[:], ALU.max).then_inc(dt_step, 1)
                    dve.wait_ge(dt_step, 5)
                    nc.vector.tensor_tensor(da[:], dt[:], minus_a[:].unsqueeze(1).to_broadcast(every), ALU.mult
                                            ).then_inc(da_done, 1)
                    nc.vector.tensor_copy(scalars[:, :, DT, :], dt[:]).then_inc(dt_step, 1)
                    dve.wait_ge(da_done, 1)
                    nc.vector.tensor_copy(scalars[:, :, DA, :], da[:]).then_inc(dt_step, 1)
                    dve.wait_ge(sums_exp, 2)
                    nc.vector.tensor_tensor(scalars[:, :, DTD, :], dt[:], a[:], ALU.mult).then_inc(scalars_done, 1)
                    dve.wait_ge(scalars_done, 1)
                    dve.wait_ge(dt_step, 7)

        xh = [part.sb(f"xh{k}", [CH, TILE]) for k in range(2)]
        xbc = part.sb("xbc", [CH, CONV, TILE + TAPS - 1])
        conv = part.sb("conv", [CH, CONV, TILE])
        xs = [part.sb(f"xs{k}", [CH, HALVES, TILE]) for k in range(2)]
        b_t = [part.sb(f"b_t{k}", [NS, TILE]) for k in range(2)]
        c_t = [part.sb(f"c_t{k}", [NS, TILE]) for k in range(2)]
        gate = [part.sb(f"gate{k}", [CH, HALVES, TILE]) for k in range(2)]
        now = [part.sb(f"now{k}", [CH, SUBS, 4, HEADS]) for k in range(2)]
        seg_w = [part.sb(f"seg_w{u}", [CH, HEADS, CH]) for u in range(SUBS)]
        mix = [part.sb(f"mix{u}", [CH, HEADS, CH]) for u in range(SUBS)]
        cb = [part.sb(f"cb{k}", [CH, CH]) for k in range(2)]
        xdt = [part.sb(f"xdt{k}", [CH, HEADS, HD]) for k in range(2)]
        xdd = [part.sb(f"xdd{k}", [CH, HEADS, HD]) for k in range(2)]
        b_tok = [part.sb(f"b_tok{k}", [CH, NS]) for k in range(2)]
        c_fade = [part.sb(f"c_fade{u}", [NS, HEADS, CH]) for u in range(SUBS)]
        state = part.sb("state", [NS, HEADS, HD])
        y = part.sb("y", [CH, HALVES, TILE])
        square = part.sb("square", [CH, HALVES, TILE])
        logv = part.sb("logv", [CH, TILE])
        rstd = part.sb("rstd", [CH, TILE])
        pre_ps = part.ps("pre_ps", [CH, TILE])
        seg_ps = part.ps("seg_ps", [CH, HEADS, CH])
        fade_ps = part.ps("fade_ps", [NS, HEADS, CH])
        turn_ps = part.ps("turn_ps", [CH, 3, CH])
        cb_ps = part.ps("cb_ps", [CH, CH])
        state_ps = part.ps("state_ps", [NS, HEADS, HD])
        y_ps = [part.ps(f"y_ps{h}", [CH, TILE]) for h in range(HALVES)]
        (pre_filled, pre_drained, tail_done, xbc_done, tap0_done, conv_step, conv_done, silu_done, now_done,
         seg_w_done, seg_done, mix_exp, mix_done, cb_raw, cb_done, turned, xdt_done, xdd_done, b_tok_done,
         fade_done, c_exp, c_fade_done, y_done, state_new, state_done, skipped, gated, squared, log_done, rstd_done,
         normed, state_kept) = sems = part.sems(
            "pre_filled pre_drained tail_done xbc_done tap0_done conv_step conv_done silu_done now_done "
            "seg_w_done seg_done mix_exp mix_done cb_raw cb_done turned xdt_done xdd_done b_tok_done "
            "fade_done c_exp c_fade_done y_done state_new state_done skipped gated squared log_done rstd_done "
            "normed state_kept")
        xh_loaded = part.sems("xh_loaded0 xh_loaded1")
        cleared = part.sem("cleared")
        prime(nc, sems)

        ORDER = ("X0", "X1", "BC", "Z0", "Z1", "MS", "OUT")
        FIRST = ("X0", "X1", "BC", "Z0", "Z1")
        N = len(ORDER)

        def fill(t, what):
            if isinstance(t, int) and t == -1:
                return FIRST.index(what)
            if isinstance(t, int) and t == 0:
                return len(FIRST) + FIRST.index(what)
            base = 2 * len(FIRST) + (t - 1) * N
            if isinstance(t, int) and t == NT - 1:
                return base + {"MS": 0, "OUT": 1, "MS_LAST": 2, "OUT_LAST": 3}[what]
            return base + ORDER.index(what)

        def over_tiles(eng, tile):
            tile(0, 0, True, False)
            with eng.Fori(0, (NT - 2) // 2) as i:
                tile(2 * i + 1, 1, False, False)
                tile(2 * i + 2, 0, False, False)
            tile(NT - 1, 1, False, True)

        with nc.Block() as block:
            @block.sync
            def _(sp):
                def load(t, k):
                    at = placed(sp, t)
                    sp.wait_ge(silu_done, LEAD + 6 * (t - 1))
                    sp.dma_start(xh[k][:], normed_dram[:, chunk(at)]).then_inc(xh_loaded[k], 16)

                load(0, 0)
                load(1, 1)
                with sp.Fori(0, (NT - 2) // 2) as i:
                    load(2 * i + 2, 0)
                    load(2 * i + 3, 1)

            @block.tensor
            def _(pe):
                def into_pre(t, what, pairs):
                    pe.wait_ge(pre_drained, LEAD + fill(t, what))
                    for n, (lhs, rhs) in enumerate(pairs):
                        last = nc.tensor.matmul(pre_ps[:], lhs, rhs, start=(n == 0), stop=(n == len(pairs) - 1))
                    last.then_inc(pre_filled, 1)

                def prepare(t, what, r, k):
                    col = {"Z0": 0, "Z1": CH, "X0": 2 * CH, "X1": 3 * CH, "BC": 4 * CH}[what]
                    if what == "X0":
                        pe.wait_ge(xh_loaded[k], 16 * ((r - k) // 2 + 1 if isinstance(r, int) else half_of(r, k) + 1))
                    into_pre(t, what, [(in_w[:, col:col + CH], xh[k][:])])

                def half_of(r, k):
                    return turns[0] + (1 if k == 0 else (0 if turn_k[0] == 1 else 1))

                turns, turn_k = [None], [None]

                def decays(t, k, u):
                    c = 4 * t + u
                    if u == 0:
                        pe.wait_ge(now_done, LEAD + t + 1)
                    pe.wait_ge(c_exp, LEAD + c)
                    for h in range(HEADS):
                        last = nc.tensor.matmul(fade_ps[:, h, :], now[k][:, sub(u), DA, h:h + 1].to_broadcast([CH, NS]),
                                                upto[:], start=True, stop=True)
                    last.then_inc(fade_done, 1)
                    pe.wait_ge(mix_exp, LEAD + c)
                    pe.wait_ge(seg_w_done, LEAD + c + 1)
                    for h in range(HEADS):
                        last = nc.tensor.matmul(seg_ps[:, h, :], seg_w[u][:, h, :], upto[:], start=True, stop=True)
                    last.then_inc(seg_done, 1)

                def chunk_in(t, k, u, last_tile):
                    c = 4 * t + u
                    cols = chunk(sub(u), CH)
                    if u == 0:
                        pe.wait_ge(silu_done, LEAD + 6 * t + 4)
                    pe.wait_ge(cb_done, LEAD + c)
                    nc.tensor.matmul(cb_ps[:], b_t[k][:, cols], c_t[k][:, cols], start=True, stop=True).then_inc(cb_raw, 1)
                    pe.wait_ge(xdt_done, LEAD + c)
                    pe.wait_ge(xdd_done, LEAD + c)
                    pe.wait_ge(b_tok_done, LEAD + c)
                    for h in range(HALVES):
                        nc.tensor.transpose(turn_ps[:, h, :], xs[k][:, h, cols], const.ident[:])
                    nc.tensor.transpose(turn_ps[:, 2, 0:NS], b_t[k][:, cols], const.ident[0:NS, 0:NS]).then_inc(turned, 1)
                    if u < SUBS - 1:
                        decays(t, k, u + 1)
                    elif not last_tile:
                        decays(t + 1, 1 - k, 0)

                def chunk_out(t, k, u):
                    c = 4 * t + u
                    cols = chunk(sub(u), CH)
                    pe.wait_ge(xdd_done, LEAD + c + 1)
                    pe.wait_ge(b_tok_done, LEAD + c + 1)
                    pe.wait_ge(state_done, LEAD + HEADS * c)
                    nc.tensor.matmul(state_ps[:].rearrange("n h p -> n (h p)"), b_tok[u % 2][:],
                                     xdd[u % 2][:].rearrange("s h p -> s (h p)"), start=True, stop=True
                                     ).then_inc(state_new, 1)
                    if u == 0:
                        pe.wait_ge(skipped, LEAD + HALVES * t)
                        pe.wait_ge(state_kept, LEAD + t + 1)
                    pe.wait_ge(xdt_done, LEAD + c + 1)
                    pe.wait_ge(mix_done, LEAD + c + 1)
                    pe.wait_ge(c_fade_done, LEAD + c + 1)
                    for h in range(HEADS):
                        at = slice(HD * (h % 2), HD * (h % 2 + 1))
                        nc.tensor.matmul(y_ps[h // 2][at, cols], xdt[u % 2][:, h, :], mix[u][:, h, :],
                                         start=True, stop=False)
                        last = nc.tensor.matmul(y_ps[h // 2][at, cols], state[:, h, :], c_fade[u][:, h, :],
                                                start=False, stop=True)
                    last.then_inc(y_done, 1)

                def mean_square(t, what, r):
                    pe.wait_ge(squared, LEAD + HALVES * (r + 1))
                    into_pre(t, what, [(const.mean[:], square[:, h, :]) for h in range(HALVES)])

                def project(t, what, r):
                    pe.wait_ge(normed, LEAD + HALVES * (r + 1))
                    into_pre(t, what, [(out_w[:, h, :], y[:, h, :]) for h in range(HALVES)])

                def tile(t, k, first, last):
                    r, rk = t + 1, 1 - k
                    chunk_in(t, k, 0, last)
                    if not last:
                        prepare(t, "X0", r, rk)
                    if not first:
                        chunk_out(t - 1, 1 - k, SUBS - 1)
                    if not last:
                        prepare(t, "X1", r, rk)
                    chunk_in(t, k, 1, last)
                    if not last:
                        prepare(t, "BC", r, rk)
                    chunk_out(t, k, 0)
                    if not last:
                        prepare(t, "Z0", r, rk)
                    chunk_in(t, k, 2, last)
                    if not last:
                        prepare(t, "Z1", r, rk)
                    chunk_out(t, k, 1)
                    if not first:
                        mean_square(t, "MS", t - 1)
                    chunk_in(t, k, 3, last)
                    chunk_out(t, k, 2)
                    if not first:
                        project(t, "OUT", t - 1)

                for what in FIRST:
                    prepare(-1, what, 0, 0)
                decays(0, 0, 0)
                tile(0, 0, True, False)
                with pe.Fori(0, (NT - 2) // 2) as i:
                    turns[0], turn_k[0] = i, 1
                    tile(2 * i + 1, 1, False, False)
                    turn_k[0] = 0
                    tile(2 * i + 2, 0, False, False)
                tile(NT - 1, 1, False, True)
                chunk_out(NT - 1, 1, SUBS - 1)
                mean_square(NT - 1, "MS_LAST", NT - 1)
                project(NT - 1, "OUT_LAST", NT - 1)

            @block.scalar
            def _(act):
                def taken(t, what, n):
                    r = t + 1
                    if n == 0:
                        act.wait_ge(tail_done, LEAD + r + 1)
                    act.wait_ge(pre_filled, LEAD + fill(t, what) + 1)
                    nc.scalar.activation(xbc[:, n, here:here + TILE], pre_ps[:], ACT.Copy).then_inc(pre_drained, 1)
                    act.wait_ge(pre_drained, LEAD + fill(t, what) + 1)
                    act.wait_ge(silu_done, LEAD + 6 * r)
                    nc.scalar.activation(conv[:, n, :], xbc[:, n, tap(0):tap(0) + TILE], ACT.Identity,
                                         bias=conv_b[:, n:n + 1], scale=conv_w[:, n, 0:1]).then_inc(tap0_done, 1)

                def z(t, n, k):
                    r = t + 1
                    act.wait_ge(pre_filled, LEAD + fill(t, f"Z{n}") + 1)
                    act.wait_ge(gated, LEAD + HALVES * (r - 1))
                    nc.scalar.activation(gate[k][:, n, :], pre_ps[:], ACT.Copy).then_inc(pre_drained, 1)
                    act.wait_ge(pre_drained, LEAD + fill(t, f"Z{n}") + 1)

                def silus(t, k):
                    r = t + 1
                    act.wait_ge(skipped, LEAD + HALVES * (r - 1))
                    act.wait_ge(turned, LEAD + SUBS * (r - 1))
                    act.wait_ge(c_fade_done, LEAD + SUBS * (r - 1))
                    act.wait_ge(conv_done, LEAD + CONV * (r + 1))
                    for n in range(HALVES):
                        nc.scalar.activation(xs[k][:, n, :], conv[:, n, :], ACT.Silu).then_inc(silu_done, 1)
                    nc.scalar.activation(b_t[k][:], conv[0:NS, 2, :], ACT.Silu).then_inc(silu_done, 1)
                    nc.scalar.activation(c_t[k][:], conv[NS:2 * NS, 2, :], ACT.Silu).then_inc(silu_done, 1)
                    for n in range(HALVES):
                        nc.scalar.activation(gate[k][:, n, :], gate[k][:, n, :], ACT.Silu).then_inc(silu_done, 1)

                def decays(t, u):
                    c = 4 * t + u
                    act.wait_ge(fade_done, LEAD + c + 1)
                    act.wait_ge(y_done, LEAD + c - SUBS + 1)
                    nc.scalar.activation(c_fade[u][:], fade_ps[:], ACT.Exp).then_inc(c_exp, 1)
                    act.wait_ge(seg_done, LEAD + c + 1)
                    nc.scalar.activation(mix[u][:], seg_ps[:], ACT.Exp).then_inc(mix_exp, 1)

                def squares(r):
                    for n in range(HALVES):
                        act.wait_ge(gated, LEAD + HALVES * r + n + 1)
                        nc.scalar.activation(square[:, n, :], y[:, n, :], ACT.Square).then_inc(squared, 1)

                def rstds(t, what, r):
                    act.wait_ge(pre_filled, LEAD + fill(t, what) + 1)
                    nc.scalar.activation(logv[:], pre_ps[:], ACT.Ln, bias=const.eps[:, 0:1], scale=1.0 / HALVES
                                         ).then_inc(pre_drained, 1)
                    act.wait_ge(pre_drained, LEAD + fill(t, what) + 1)
                    act.wait_ge(normed, LEAD + HALVES * r)
                    nc.scalar.activation(rstd[:], logv[:], ACT.Exp, scale=-0.5).then_inc(rstd_done, 1)

                def tile(t, k, first, last):
                    decays(t, 1)
                    if not last:
                        taken(t, "X0", 0)
                        taken(t, "X1", 1)
                    decays(t, 2)
                    if not last:
                        taken(t, "BC", 2)
                    if not first:
                        squares(t - 1)
                    if not last:
                        z(t, 0, 1 - k)
                    decays(t, 3)
                    if not last:
                        z(t, 1, 1 - k)
                    if not first:
                        rstds(t, "MS", t - 1)
                    if not last:
                        silus(t, 1 - k)
                        nc.scalar.preload_act_table_set("natural_log_exp_and_others")
                        decays(t + 1, 0)

                taken(-1, "X0", 0)
                taken(-1, "X1", 1)
                taken(-1, "BC", 2)
                z(-1, 0, 0)
                z(-1, 1, 0)
                silus(-1, 0)
                nc.scalar.preload_act_table_set("natural_log_exp_and_others")
                decays(0, 0)
                over_tiles(act, tile)
                squares(NT - 1)
                rstds(NT - 1, "MS_LAST", NT - 1)

            @block.vector
            def _(dve):
                def tail(t):
                    r = t + 1
                    dve.wait_ge(conv_done, LEAD + CONV * r)
                    dst, src = (slice(TILE, TILE + TAPS - 1), slice(0, TAPS - 1)) if back else (
                        slice(0, TAPS - 1), slice(TILE, TILE + TAPS - 1))
                    nc.vector.tensor_scalar(xbc[:, :, dst], xbc[:, :, src], keep[:, bass.ds(r, 1)], None, ALU.mult
                                            ).then_inc(tail_done, 1)

                def convolve(t, n):
                    r = t + 1
                    dve.wait_ge(tap0_done, LEAD + CONV * r + n + 1)
                    for j in range(1, TAPS):
                        if j > 1:
                            dve.wait_ge(conv_step, LEAD + (CONV * r + n) * (TAPS - 2) + j - 1)
                        done = conv_step if j < TAPS - 1 else conv_done
                        nc.vector.scalar_tensor_tensor(
                            out=conv[:, n, :], in0=xbc[:, n, tap(j):tap(j) + TILE], scalar=conv_w[:, n, j:j + 1],
                            in1=conv[:, n, :], op0=ALU.mult, op1=ALU.add).then_inc(done, 1)

                def take_scalars(t, k):
                    r = t + 1
                    at = placed(dve, r)
                    dve.wait_ge(seg_done, LEAD + SUBS * (r - 1))
                    dve.wait_ge(state_done, LEAD + SUBS * HEADS * (r - 1))
                    nc.vector.tensor_scalar(now[k][:].rearrange("p s f h -> p (s f h)"),
                                            scalars[:, bass.ds(at * SUBS, SUBS), :, :].rearrange(
                                                "p s f h -> p (s f h)"), 1.0, None, ALU.mult).then_inc(now_done, 1)

                def chunk_in(t, k, u):
                    c = 4 * t + u
                    wide = [CH, HEADS, HD]
                    dve.wait_ge(cb_raw, LEAD + c + 1)
                    dve.wait_ge(mix_done, LEAD + c - 1)
                    nc.vector.tensor_tensor(cb[u % 2][:], cb_ps[:], upto[:], ALU.mult).then_inc(cb_done, 1)
                    dve.wait_ge(turned, LEAD + c + 1)
                    dve.wait_ge(y_done, LEAD + c - 1)
                    tok = turn_ps[:, 0:2, :].rearrange("s a (b p) -> s (a b) p", p=HD)
                    nc.vector.tensor_tensor(xdt[u % 2][:], tok,
                                            now[k][:, sub(u), DT, :].unsqueeze(2).to_broadcast(wide), ALU.mult
                                            ).then_inc(xdt_done, 1)
                    dve.wait_ge(state_new, LEAD + c - 1)
                    nc.vector.tensor_copy(b_tok[u % 2][:], turn_ps[:, 2, 0:NS]).then_inc(b_tok_done, 1)
                    nc.vector.tensor_tensor(xdd[u % 2][:], tok,
                                            now[k][:, sub(u), DTD, :].unsqueeze(2).to_broadcast(wide), ALU.mult
                                            ).then_inc(xdd_done, 1)
                    dve.wait_ge(mix_exp, LEAD + c + 1)
                    dve.wait_ge(cb_done, LEAD + c + 1)
                    nc.vector.tensor_tensor(mix[u][:], mix[u][:],
                                            cb[u % 2][:].unsqueeze(1).to_broadcast([CH, HEADS, CH]), ALU.mult
                                            ).then_inc(mix_done, 1)

                def chunk_out(t, k, u):
                    c = 4 * t + u
                    dve.wait_ge(state_new, LEAD + c + 1)
                    dve.wait_ge(y_done, LEAD + c + 1)
                    for h in range(HEADS):
                        nc.vector.scalar_tensor_tensor(out=state[:, h, :], in0=state[:, h, :],
                                                       scalar=now[k][0:NS, sub(u), DCH, h:h + 1], in1=state_ps[:, h, :],
                                                       op0=ALU.mult, op1=ALU.add).then_inc(state_done, 1)
                    dve.wait_ge(state_done, LEAD + HEADS * (c + 1))

                def skip(t, r, k):
                    for n in range(HALVES):
                        if t is None:
                            dve.wait_ge(pre_filled, LEAD + fill(NT - 1, "OUT") + 1)
                        else:
                            dve.wait_ge(pre_filled, LEAD + fill(t, "MS" if isinstance(t, int) else "X0"))
                        nc.vector.scalar_tensor_tensor(out=y[:, n, :], in0=xs[k][:, n, :], scalar=d_skip[:, n:n + 1],
                                                       in1=y_ps[n][:], op0=ALU.mult, op1=ALU.add).then_inc(skipped, 1)

                def add(t, what, r):
                    at = placed(dve, r)
                    dve.wait_ge(pre_filled, LEAD + fill(t, what) + 1)
                    nc.vector.tensor_tensor(const.x[:, chunk(at)], pre_ps[:], const.x[:, chunk(at)], ALU.add
                                            ).then_inc(pre_drained, 1)

                def tile(t, k, first, last):
                    if not last:
                        tail(t)
                    chunk_in(t, k, 0)
                    if not first:
                        chunk_out(t - 1, 1 - k, SUBS - 1)
                        skip(t, t - 1, 1 - k)
                    dve.wait_ge(state_done, LEAD + SUBS * HEADS * t)
                    nc.vector.tensor_scalar(state[:], state[:], keep[0:NS, bass.ds(t, 1)], None, ALU.mult
                                            ).then_inc(state_kept, 1)
                    if not last:
                        take_scalars(t, 1 - k)
                    chunk_in(t, k, 1)
                    dve.wait_ge(state_kept, LEAD + t + 1)
                    chunk_out(t, k, 0)
                    if not last:
                        convolve(t, 0)
                        convolve(t, 1)
                    chunk_in(t, k, 2)
                    if not last:
                        convolve(t, 2)
                    chunk_out(t, k, 1)
                    chunk_in(t, k, 3)
                    chunk_out(t, k, 2)
                    if not first:
                        add(t, "OUT", t - 1)

                nc.vector.memset(state[:], 0.0).then_inc(cleared, 1)
                nc.vector.memset(xbc[:], 0.0).then_inc(cleared, 1)
                dve.wait_ge(cleared, 2)
                tail(-1)
                take_scalars(-1, 0)
                for n in range(CONV):
                    convolve(-1, n)
                over_tiles(dve, tile)
                chunk_out(NT - 1, 1, SUBS - 1)
                skip(None, NT - 1, 1)
                add(NT - 1, "OUT_LAST", NT - 1)

            @block.gpsimd
            def _(pool):
                def segments(t, k, u):
                    c = 4 * t + u
                    if u == 0:
                        pool.wait_ge(now_done, LEAD + t + 1)
                    pool.wait_ge(seg_done, LEAD + c - SUBS + 1)
                    wide = [CH, HEADS, CH]
                    nc.gpsimd.tensor_tensor(seg_w[u][:], after[:].unsqueeze(1).to_broadcast(wide),
                                            now[k][:, sub(u), DA, :].unsqueeze(2).to_broadcast(wide), ALU.mult
                                            ).then_inc(seg_w_done, 1)

                def fade(t, k, u):
                    c = 4 * t + u
                    if u == 0:
                        pool.wait_ge(silu_done, LEAD + 6 * t + 4)
                    pool.wait_ge(c_exp, LEAD + c + 1)
                    nc.gpsimd.tensor_tensor(c_fade[u][:], c_fade[u][:],
                                            c_t[k][:, chunk(sub(u), CH)].unsqueeze(1).to_broadcast([NS, HEADS, CH]),
                                            ALU.mult).then_inc(c_fade_done, 1)

                def gates(t, k):
                    pool.wait_ge(silu_done, LEAD + 6 * (t + 1))
                    for n in range(HALVES):
                        pool.wait_ge(skipped, LEAD + HALVES * t + n + 1)
                        nc.gpsimd.tensor_tensor(y[:, n, :], y[:, n, :], gate[k][:, n, :], ALU.mult).then_inc(gated, 1)

                def norm(r):
                    pool.wait_ge(rstd_done, LEAD + r + 1)
                    pool.wait_ge(squared, LEAD + HALVES * (r + 1))
                    for n in range(HALVES):
                        nc.gpsimd.tensor_tensor(y[:, n, :], y[:, n, :], rstd[:], ALU.mult).then_inc(normed, 1)

                def tile(t, k, first, last):
                    segments(t, k, 2)
                    fade(t, k, 0)
                    segments(t, k, 3)
                    if not first:
                        gates(t - 1, 1 - k)
                    fade(t, k, 1)
                    if not last:
                        segments(t + 1, 1 - k, 0)
                    fade(t, k, 2)
                    if not last:
                        segments(t + 1, 1 - k, 1)
                    fade(t, k, 3)
                    if not first:
                        norm(t - 1)

                segments(0, 0, 0)
                segments(0, 0, 1)
                over_tiles(pool, tile)
                gates(NT - 1, 1)
                norm(NT - 1)


def bimamba(nc, const, fwd, bwd, normed_dram):
    build_layer_norm(nc, const, "ln3", normed_dram)
    build_ssd(nc, const, "sf", fwd, normed_dram, False)
    build_ssd(nc, const, "sb", bwd, normed_dram, True)


def build(nc, a, out):
    def of(prefix):
        return {n[len(prefix):]: v for n, v in a.items() if n.startswith(prefix)}

    normed_dram = nc.dram_tensor("normed_dram", (CH, (NT + 1) * TILE), F32, kind="Internal").ap()
    mixed_dram = nc.dram_tensor("mixed_dram", (CH, NT * TILE), F32, kind="Internal").ap()
    with Part(nc, "k") as part:
        const = Constants(part)
        build_constants(nc, const)
        layer0(nc, const, of("L0_conv_"), a["x"], normed_dram, mixed_dram)
        layer1(nc, const, of("L1_conv_"))
        attention(nc, const, normed_dram)
        experts(nc, const, "f2", of("L2_ffn_"))
        bimamba(nc, const, of("L3_attn_fwd_"), of("L3_attn_bwd_"), normed_dram)
        experts(nc, const, "f3", of("L3_ffn_"), out)


_INS = ["x", "L0_conv_gamma", "L0_conv_beta", "L0_conv_W_in", "L0_conv_conv_w", "L0_conv_conv_b", "L0_conv_W_x",
        "L0_conv_W_dt", "L0_conv_b_dt", "L0_conv_A_log", "L0_conv_D_skip", "L0_conv_W_out", "L0_conv_W_p",
        "L0_conv_b_p", "L0_conv_s1", "L0_conv_s2", "L1_conv_w_kg", "L1_conv_b_kg", "L1_conv_w_pw", "L1_conv_b_pw",
        "L2_ffn_gate_w", "L2_ffn_gate_b", "L2_ffn_weight1", "L2_ffn_weight2",
        "L3_attn_fwd_in_proj", "L3_attn_fwd_conv_w", "L3_attn_fwd_conv_b", "L3_attn_fwd_A_log",
        "L3_attn_fwd_dt_bias", "L3_attn_fwd_D", "L3_attn_fwd_norm_w", "L3_attn_fwd_out_proj",
        "L3_attn_bwd_in_proj", "L3_attn_bwd_conv_w", "L3_attn_bwd_conv_b", "L3_attn_bwd_A_log",
        "L3_attn_bwd_dt_bias", "L3_attn_bwd_D", "L3_attn_bwd_norm_w", "L3_attn_bwd_out_proj",
        "L3_ffn_gate_w", "L3_ffn_gate_b", "L3_ffn_weight1", "L3_ffn_weight2"]
_OUT = (BATCH, CH, IMG, IMG)


def kernel(**inputs):
    import numpy as _np
    import concourse.bacc as _bacc
    from concourse.bass_utils import run_bass_kernel_spmd as _run

    nc = _bacc.Bacc("TRN2", target_bir_lowering=False, num_devices=1)
    arrays, args = {}, {}
    for name in _INS:
        a = _np.ascontiguousarray(inputs[name])
        arrays[f"in_{name}"] = a
        args[name] = nc.dram_tensor(f"in_{name}", a.shape, mybir.dt.from_np(a.dtype), kind="ExternalInput").ap()
    out = nc.dram_tensor("out_x", _OUT, F32, kind="ExternalOutput").ap()
    build(nc, args, out)
    r = _run(nc, [arrays], core_ids=[0])
    return r.results[0]["out_x"]
```
